# Optimizing a Trainium2 kernel written in Bass

```python
import numpy as np
import jax
import jax.numpy as jnp

def _softmax(x, axis=-1):
    return jax.nn.softmax(x, axis=axis)

def _gelu(x):
    return jax.nn.gelu(x, approximate=True)

def _silu(x):
    return jax.nn.silu(x)

def _sigmoid(x):
    return jax.nn.sigmoid(x)

def _layernorm(x, axis=-1, eps=1e-05):
    m = jnp.mean(x, axis=axis, keepdims=True)
    v = jnp.var(x, axis=axis, keepdims=True)
    return (x - m) / jnp.sqrt(v + eps)

def _scatter_add(tgt, idx, src, axis=0):
    return tgt.at[idx].add(src)

def _segment_sum(src, seg, n):
    return jax.ops.segment_sum(src, seg, n)
kernel_name = 'mk_recurrent_d4_jaxref_r8_be4988'

def setup_inputs(seed: int=0):
    np.random.seed(seed)
    _w = jnp.asarray

    def _L0_attn_setup():
        import jax, jax.numpy as jnp
        import numpy as np
        B, S, HID = (2, 128, 512)
        N_HEADS, N_KV_HEADS = (32, 8)
        HEAD_DIM = HID // N_HEADS
        N_REP = N_HEADS // N_KV_HEADS
        ROPE_THETA = 10000.0

        def _rope(x, cos, sin):
            xe = x[..., 0::2]
            xo = x[..., 1::2]
            oe = xe * cos - xo * sin
            oo = xe * sin + xo * cos
            return jnp.stack([oe, oo], axis=-1).reshape(x.shape)
        key = jax.random.key(seed)
        ks = jax.random.split(key, 5)
        scale = 0.02
        return {'hidden_states': jax.random.normal(ks[0], (B, S, HID), dtype=jnp.float32), 'Wq': jax.random.normal(ks[1], (HID, HID), dtype=jnp.float32) * scale, 'Wk': jax.random.normal(ks[2], (N_KV_HEADS * HEAD_DIM, HID), dtype=jnp.float32) * scale, 'Wv': jax.random.normal(ks[3], (N_KV_HEADS * HEAD_DIM, HID), dtype=jnp.float32) * scale, 'Wo': jax.random.normal(ks[4], (HID, HID), dtype=jnp.float32) * scale}
    _L0_attn_in = _L0_attn_setup()

    def _L0_ffn_setup():
        import jax, jax.numpy as jnp
        import numpy as np
        _TRIPLES = [(1, 2, 3), (1, 4, 5), (1, 7, 6), (2, 4, 6), (2, 5, 7), (3, 4, 7), (3, 6, 5)]

        def _oct_struct():
            S = np.zeros((8, 8, 8), np.float32)
            S[0, 0, 0] = 1.0
            for i in range(1, 8):
                S[0, i, i] = 1.0
                S[i, 0, i] = 1.0
                S[i, i, 0] = -1.0
            for a, b, c in _TRIPLES:
                for x, y, z in ((a, b, c), (b, c, a), (c, a, b)):
                    S[x, y, z] = 1.0
                    S[y, x, z] = -1.0
            return jnp.asarray(S)
        S_OCT = _oct_struct()
        N_EMBD = 512
        HIDDEN = 1366

        def ternary_dequant(W):
            scale = jnp.mean(jnp.abs(W))
            Wq = scale * jnp.clip(jnp.round(W / scale), -1.0, 1.0)
            return W + jax.lax.stop_gradient(Wq - W)

        def oct_ternary_linear(xp, W):
            Wq = ternary_dequant(W)
            M = jnp.einsum('jik,jod->koid', S_OCT, Wq)
            return jnp.einsum('...id,koid->...ko', xp, M)
        key = jax.random.key(seed)
        k1, k2, k3, k4 = jax.random.split(key, 4)
        B, T = (2, 256)
        d8, h8 = (N_EMBD // 8, HIDDEN // 8)
        std_in = 1.0 / np.sqrt(N_EMBD)
        std_h = 1.0 / np.sqrt(HIDDEN)
        return {'x': jax.random.normal(k1, (B, T, N_EMBD), jnp.float32), 'w_gate': jax.random.normal(k2, (8, h8, d8), jnp.float32) * std_in, 'w_up': jax.random.normal(k3, (8, h8, d8), jnp.float32) * std_in, 'w_down': jax.random.normal(k4, (8, d8, h8), jnp.float32) * std_h}
    _L0_ffn_in = _L0_ffn_setup()

    def _L1_attn_setup():
        import jax, jax.numpy as jnp
        import numpy as np
        HIDDEN = 512
        N_HEADS = 32
        HEAD_DIM = HIDDEN // N_HEADS
        B, S = (2, 256)
        key = jax.random.key(seed)
        ks = jax.random.split(key, 5)
        scale = 1.0 / np.sqrt(HIDDEN)
        x = jax.random.normal(ks[0], (B, S, HIDDEN), dtype=jnp.float32)
        Wq = jax.random.uniform(ks[1], (HIDDEN, HIDDEN), jnp.float32, -scale, scale)
        Wk = jax.random.uniform(ks[2], (HIDDEN, HIDDEN), jnp.float32, -scale, scale)
        Wv = jax.random.uniform(ks[3], (HIDDEN, HIDDEN), jnp.float32, -scale, scale)
        Wo = jax.random.uniform(ks[4], (HIDDEN, HIDDEN), jnp.float32, -scale, scale)
        return {'x': x, 'Wq': Wq, 'Wk': Wk, 'Wv': Wv, 'Wo': Wo}
    _L1_attn_in = _L1_attn_setup()

    def _L1_ffn_setup():
        import jax, jax.numpy as jnp
        import numpy as np
        B, S, K, N = (4, 256, 512, 512)
        GS = 128
        G = K // GS

        def _dequantize(qweight, qzeros, scales, g_idx):
            shifts = jnp.arange(8, dtype=jnp.int32) * 4
            q = (qweight[:, None, :] >> shifts[None, :, None] & 15).reshape(-1, qweight.shape[1])
            z = (qzeros[:, :, None] >> shifts[None, None, :] & 15).reshape(qzeros.shape[0], -1) + 1
            zr = z[g_idx]
            sr = scales[g_idx]
            return (q.astype(sr.dtype) - zr.astype(sr.dtype)) * sr
        key = jax.random.key(seed)
        k1, k2, k3, k4, k5 = jax.random.split(key, 5)
        x = jax.random.normal(k1, (B, S, K), dtype=jnp.float16)
        qweight = jax.random.randint(k2, (K // 8, N), 0, 2 ** 31 - 1, dtype=jnp.int32)
        qzeros = jax.random.randint(k3, (G, N // 8), 0, 2 ** 31 - 1, dtype=jnp.int32)
        scales = (jax.random.uniform(k4, (G, N), dtype=jnp.float32) * 0.009 + 0.001).astype(jnp.float16)
        g_idx = (jnp.arange(K, dtype=jnp.int32) // GS).astype(jnp.int32)
        bias = (jax.random.normal(k5, (N,), dtype=jnp.float32) * 0.01).astype(jnp.float16)
        return {'x': x, 'qweight': qweight, 'qzeros': qzeros, 'scales': scales, 'g_idx': g_idx, 'bias': bias}
    _L1_ffn_in = _L1_ffn_setup()

    def _L2_attn_setup():
        import jax, jax.numpy as jnp
        import numpy as np
        import math
        B, T, D_IN, D_OUT = (2, 256, 512, 512)
        N_HEADS, N_KV = (32, 8)
        HEAD_DIM = D_OUT // N_HEADS
        GROUP_SIZE = N_HEADS // N_KV
        ROPE_BASE = 500000.0
        CTX = 256

        def _rope_tables(head_dim, base, seq_len):
            inv_freq = 1.0 / base ** (jnp.arange(0, head_dim, 2, dtype=jnp.float32) / head_dim)
            t = jnp.arange(seq_len, dtype=jnp.float32)
            freqs = jnp.einsum('i,j->ij', t, inv_freq)
            return (jnp.cos(freqs), jnp.sin(freqs))

        def _apply_rope(x, cos, sin):
            x1, x2 = jnp.split(x, 2, axis=-1)
            c = cos[None, None]
            s = sin[None, None]
            return jnp.concatenate([x1 * c - x2 * s, x1 * s + x2 * c], axis=-1)
        key = jax.random.key(seed)
        ks = jax.random.split(key, 5)
        scale = 0.02
        return {'x': jax.random.normal(ks[0], (B, T, D_IN), dtype=jnp.float32), 'Wq': jax.random.normal(ks[1], (D_IN, D_OUT), dtype=jnp.float32) * scale, 'Wk': jax.random.normal(ks[2], (D_IN, N_KV * HEAD_DIM), dtype=jnp.float32) * scale, 'Wv': jax.random.normal(ks[3], (D_IN, N_KV * HEAD_DIM), dtype=jnp.float32) * scale, 'Wo': jax.random.normal(ks[4], (D_OUT, D_OUT), dtype=jnp.float32) * scale}
    _L2_attn_in = _L2_attn_setup()

    def _L2_ffn_setup():
        import jax, jax.numpy as jnp
        import numpy as np
        BS = 128
        FP8_MAX = 448.0

        def act_quant(x):
            T, K = x.shape
            xb = x.reshape(T, K // BS, BS)
            amax = jnp.max(jnp.abs(xb), axis=-1)
            scale = amax / FP8_MAX + 1e-12
            xq = (xb / scale[:, :, None]).reshape(T, K)
            return (xq, scale)

        def linear_dsv3(x, wq, w_scale):
            T, K = x.shape
            N = wq.shape[0]
            xq, xs = act_quant(x)
            xdq = (xq.reshape(T, K // BS, BS) * xs[:, :, None]).reshape(T, K)
            wdq = (wq.reshape(N // BS, BS, K // BS, BS) * w_scale[:, None, :, None]).reshape(N, K)
            return xdq @ wdq.T
        key = jax.random.key(seed)
        ks = jax.random.split(key, 4)
        DIM, INTER = (512, 1792)

        def make_qweight(k, n, m):
            w = jax.random.normal(k, (n, m), dtype=jnp.float32) * 0.02
            wb = w.reshape(n // BS, BS, m // BS, BS)
            amax = jnp.max(jnp.abs(wb), axis=(1, 3))
            scale = amax / FP8_MAX + 1e-12
            wq = (wb / scale[:, None, :, None]).reshape(n, m)
            return (wq, scale)
        x = jax.random.normal(ks[0], (2, 128, DIM), dtype=jnp.float32)
        w1, w1_scale = make_qweight(ks[1], INTER, DIM)
        w3, w3_scale = make_qweight(ks[2], INTER, DIM)
        w2, w2_scale = make_qweight(ks[3], DIM, INTER)
        return {'x': x, 'w1': w1, 'w1_scale': w1_scale, 'w3': w3, 'w3_scale': w3_scale, 'w2': w2, 'w2_scale': w2_scale}
    _L2_ffn_in = _L2_ffn_setup()

    def _L3_attn_setup():
        import jax, jax.numpy as jnp
        import numpy as np
        NUM_HEADS = 32
        NUM_KV_GROUPS = 8
        ROPE_BASE = 10000.0

        def _rope_tables(seq_len, head_dim):
            inv_freq = 1.0 / ROPE_BASE ** (jnp.arange(0, head_dim, 2, dtype=jnp.float32) / head_dim)
            ang = jnp.arange(seq_len, dtype=jnp.float32)[:, None] * inv_freq[None, :]
            ang = jnp.concatenate([ang, ang], axis=-1)
            return (jnp.cos(ang), jnp.sin(ang))

        def _apply_rope(t, cos, sin):
            hd = t.shape[-1]
            x1, x2 = (t[..., :hd // 2], t[..., hd // 2:])
            rotated = jnp.concatenate([-x2, x1], axis=-1)
            return t * cos[None, None] + rotated * sin[None, None]
        key = jax.random.key(seed)
        k0, k1, k2, k3, k4 = jax.random.split(key, 5)
        B, S, D = (1, 256, 512)
        KV_DIM = NUM_KV_GROUPS * (D // NUM_HEADS)
        s = 0.02
        return {'x': jax.random.normal(k0, (B, S, D), jnp.float32), 'Wq': jax.random.normal(k1, (D, D), jnp.float32) * s, 'Wk': jax.random.normal(k2, (D, KV_DIM), jnp.float32) * s, 'Wv': jax.random.normal(k3, (D, KV_DIM), jnp.float32) * s, 'Wo': jax.random.normal(k4, (D, D), jnp.float32) * s}
    _L3_attn_in = _L3_attn_setup()

    def _L3_ffn_setup():
        import jax, jax.numpy as jnp
        import numpy as np
        HIDDEN = 512
        INTER = 1376
        RANK = 128
        B, S = (2, 256)
        key = jax.random.key(seed)
        ks = jax.random.split(key, 7)
        sc = 0.02
        return {'x': jax.random.normal(ks[0], (B, S, HIDDEN), dtype=jnp.float32), 'U1': jax.random.normal(ks[1], (HIDDEN, RANK), dtype=jnp.float32) * sc, 'V1': jax.random.normal(ks[2], (RANK, 2 * INTER), dtype=jnp.float32) * sc, 'U2': jax.random.normal(ks[3], (INTER, RANK), dtype=jnp.float32) * sc, 'V2': jax.random.normal(ks[4], (RANK, HIDDEN), dtype=jnp.float32) * sc, 'b1': jax.random.normal(ks[5], (2 * INTER,), dtype=jnp.float32) * sc, 'b2': jax.random.normal(ks[6], (HIDDEN,), dtype=jnp.float32) * sc}
    _L3_ffn_in = _L3_ffn_setup()
    _d = {'L0_attn_hidden_states': _L0_attn_in['hidden_states'], 'L0_attn_Wq': _L0_attn_in['Wq'], 'L0_attn_Wk': _L0_attn_in['Wk'], 'L0_attn_Wv': _L0_attn_in['Wv'], 'L0_attn_Wo': _L0_attn_in['Wo'], 'L0_ffn_w_gate': _L0_ffn_in['w_gate'], 'L0_ffn_w_up': _L0_ffn_in['w_up'], 'L0_ffn_w_down': _L0_ffn_in['w_down'], 'L1_attn_Wq': _L1_attn_in['Wq'], 'L1_attn_Wk': _L1_attn_in['Wk'], 'L1_attn_Wv': _L1_attn_in['Wv'], 'L1_attn_Wo': _L1_attn_in['Wo'], 'L1_ffn_qweight': _L1_ffn_in['qweight'], 'L1_ffn_qzeros': _L1_ffn_in['qzeros'], 'L1_ffn_scales': _L1_ffn_in['scales'], 'L1_ffn_g_idx': _L1_ffn_in['g_idx'], 'L1_ffn_bias': _L1_ffn_in['bias'], 'L2_attn_Wq': _L2_attn_in['Wq'], 'L2_attn_Wk': _L2_attn_in['Wk'], 'L2_attn_Wv': _L2_attn_in['Wv'], 'L2_attn_Wo': _L2_attn_in['Wo'], 'L2_ffn_w1': _L2_ffn_in['w1'], 'L2_ffn_w1_scale': _L2_ffn_in['w1_scale'], 'L2_ffn_w3': _L2_ffn_in['w3'], 'L2_ffn_w3_scale': _L2_ffn_in['w3_scale'], 'L2_ffn_w2': _L2_ffn_in['w2'], 'L2_ffn_w2_scale': _L2_ffn_in['w2_scale'], 'L3_attn_Wq': _L3_attn_in['Wq'], 'L3_attn_Wk': _L3_attn_in['Wk'], 'L3_attn_Wv': _L3_attn_in['Wv'], 'L3_attn_Wo': _L3_attn_in['Wo'], 'L3_ffn_U1': _L3_ffn_in['U1'], 'L3_ffn_V1': _L3_ffn_in['V1'], 'L3_ffn_U2': _L3_ffn_in['U2'], 'L3_ffn_V2': _L3_ffn_in['V2'], 'L3_ffn_b1': _L3_ffn_in['b1'], 'L3_ffn_b2': _L3_ffn_in['b2']}
    _x0 = _d['L0_attn_hidden_states']
    _d['L0_attn_hidden_states'] = jax.random.normal(jax.random.fold_in(jax.random.key(seed), 1), (4, 256, 512), dtype=_x0.dtype)
    del _x0
    return _d

def reference(L0_attn_hidden_states, L0_attn_Wq, L0_attn_Wk, L0_attn_Wv, L0_attn_Wo, L0_ffn_w_gate, L0_ffn_w_up, L0_ffn_w_down, L1_attn_Wq, L1_attn_Wk, L1_attn_Wv, L1_attn_Wo, L1_ffn_qweight, L1_ffn_qzeros, L1_ffn_scales, L1_ffn_g_idx, L1_ffn_bias, L2_attn_Wq, L2_attn_Wk, L2_attn_Wv, L2_attn_Wo, L2_ffn_w1, L2_ffn_w1_scale, L2_ffn_w3, L2_ffn_w3_scale, L2_ffn_w2, L2_ffn_w2_scale, L3_attn_Wq, L3_attn_Wk, L3_attn_Wv, L3_attn_Wo, L3_ffn_U1, L3_ffn_V1, L3_ffn_U2, L3_ffn_V2, L3_ffn_b1, L3_ffn_b2):

    def _L0_attn_ref(hidden_states, Wq, Wk, Wv, Wo):
        import jax, jax.numpy as jnp
        import numpy as np
        B, S, HID = (2, 128, 512)
        N_HEADS, N_KV_HEADS = (32, 8)
        HEAD_DIM = HID // N_HEADS
        N_REP = N_HEADS // N_KV_HEADS
        ROPE_THETA = 10000.0

        def _rope(x, cos, sin):
            xe = x[..., 0::2]
            xo = x[..., 1::2]
            oe = xe * cos - xo * sin
            oo = xe * sin + xo * cos
            return jnp.stack([oe, oo], axis=-1).reshape(x.shape)
        b, s, _ = hidden_states.shape
        q = (hidden_states @ Wq.T).reshape(b, s, N_HEADS, HEAD_DIM).transpose(0, 2, 1, 3)
        k = (hidden_states @ Wk.T).reshape(b, s, N_KV_HEADS, HEAD_DIM).transpose(0, 2, 1, 3)
        v = (hidden_states @ Wv.T).reshape(b, s, N_KV_HEADS, HEAD_DIM).transpose(0, 2, 1, 3)
        pos = jnp.arange(s, dtype=jnp.float32)
        inv_freq = 1.0 / ROPE_THETA ** (jnp.arange(0, HEAD_DIM, 2, dtype=jnp.float32) / HEAD_DIM)
        freqs = pos[:, None] * inv_freq[None, :]
        cos, sin = (jnp.cos(freqs), jnp.sin(freqs))
        q = _rope(q, cos, sin)
        k = _rope(k, cos, sin)
        k = jnp.repeat(k, N_REP, axis=1)
        v = jnp.repeat(v, N_REP, axis=1)
        scores = jnp.einsum('bhsd,bhtd->bhst', q, k) / jnp.sqrt(jnp.float32(HEAD_DIM))
        causal = jnp.tril(jnp.ones((s, s), dtype=bool))
        scores = jnp.where(causal[None, None], scores, jnp.finfo(scores.dtype).min)
        attn = jax.nn.softmax(scores, axis=-1)
        out = jnp.einsum('bhst,bhtd->bhsd', attn, v)
        out = out.transpose(0, 2, 1, 3).reshape(b, s, HID)
        return out @ Wo.T

    def _L0_ffn_ref(x, w_gate, w_up, w_down):
        import jax, jax.numpy as jnp
        import numpy as np
        _TRIPLES = [(1, 2, 3), (1, 4, 5), (1, 7, 6), (2, 4, 6), (2, 5, 7), (3, 4, 7), (3, 6, 5)]

        def _oct_struct():
            S = np.zeros((8, 8, 8), np.float32)
            S[0, 0, 0] = 1.0
            for i in range(1, 8):
                S[0, i, i] = 1.0
                S[i, 0, i] = 1.0
                S[i, i, 0] = -1.0
            for a, b, c in _TRIPLES:
                for x, y, z in ((a, b, c), (b, c, a), (c, a, b)):
                    S[x, y, z] = 1.0
                    S[y, x, z] = -1.0
            return jnp.asarray(S)
        S_OCT = _oct_struct()
        N_EMBD = 512
        HIDDEN = 1366

        def ternary_dequant(W):
            scale = jnp.mean(jnp.abs(W))
            Wq = scale * jnp.clip(jnp.round(W / scale), -1.0, 1.0)
            return W + jax.lax.stop_gradient(Wq - W)

        def oct_ternary_linear(xp, W):
            Wq = ternary_dequant(W)
            M = jnp.einsum('jik,jod->koid', S_OCT, Wq)
            return jnp.einsum('...id,koid->...ko', xp, M)
        B, T, D = x.shape
        xp = x.reshape(B, T, 8, D // 8)
        gate = oct_ternary_linear(xp, w_gate).reshape(B, T, -1)
        up = oct_ternary_linear(xp, w_up).reshape(B, T, -1)
        h = jax.nn.silu(gate) * up
        hp = h.reshape(B, T, 8, h.shape[-1] // 8)
        out = oct_ternary_linear(hp, w_down).reshape(B, T, D)
        return out

    def _L1_attn_ref(x, Wq, Wk, Wv, Wo):
        import jax, jax.numpy as jnp
        import numpy as np
        HIDDEN = 512
        N_HEADS = 32
        HEAD_DIM = HIDDEN // N_HEADS
        B, S = (2, 256)
        b, s, _ = x.shape
        q = (x @ Wq.T).reshape(b, s, N_HEADS, HEAD_DIM).transpose(0, 2, 1, 3)
        k = (x @ Wk.T).reshape(b, s, N_HEADS, HEAD_DIM).transpose(0, 2, 1, 3)
        v = (x @ Wv.T).reshape(b, s, N_HEADS, HEAD_DIM).transpose(0, 2, 1, 3)
        scores = jnp.einsum('bhqd,bhkd->bhqk', q, k) / jnp.sqrt(jnp.float32(HEAD_DIM))
        attn = jax.nn.softmax(scores, axis=-1)
        out = jnp.einsum('bhqk,bhkd->bhqd', attn, v)
        out = out.transpose(0, 2, 1, 3).reshape(b, s, HIDDEN)
        return out @ Wo.T

    def _L1_ffn_ref(x, qweight, qzeros, scales, g_idx, bias):
        import jax, jax.numpy as jnp
        import numpy as np
        B, S, K, N = (4, 256, 512, 512)
        GS = 128
        G = K // GS

        def _dequantize(qweight, qzeros, scales, g_idx):
            shifts = jnp.arange(8, dtype=jnp.int32) * 4
            q = (qweight[:, None, :] >> shifts[None, :, None] & 15).reshape(-1, qweight.shape[1])
            z = (qzeros[:, :, None] >> shifts[None, None, :] & 15).reshape(qzeros.shape[0], -1) + 1
            zr = z[g_idx]
            sr = scales[g_idx]
            return (q.astype(sr.dtype) - zr.astype(sr.dtype)) * sr
        W = _dequantize(qweight, qzeros, scales, g_idx)
        xf = x.reshape(-1, x.shape[-1])
        out = jnp.matmul(xf, W, preferred_element_type=jnp.float32).astype(x.dtype)
        out = out.reshape(x.shape[:-1] + (W.shape[1],)) + bias
        return out

    def _L2_attn_ref(x, Wq, Wk, Wv, Wo):
        import jax, jax.numpy as jnp
        import numpy as np
        import math
        B, T, D_IN, D_OUT = (2, 256, 512, 512)
        N_HEADS, N_KV = (32, 8)
        HEAD_DIM = D_OUT // N_HEADS
        GROUP_SIZE = N_HEADS // N_KV
        ROPE_BASE = 500000.0
        CTX = 256

        def _rope_tables(head_dim, base, seq_len):
            inv_freq = 1.0 / base ** (jnp.arange(0, head_dim, 2, dtype=jnp.float32) / head_dim)
            t = jnp.arange(seq_len, dtype=jnp.float32)
            freqs = jnp.einsum('i,j->ij', t, inv_freq)
            return (jnp.cos(freqs), jnp.sin(freqs))

        def _apply_rope(x, cos, sin):
            x1, x2 = jnp.split(x, 2, axis=-1)
            c = cos[None, None]
            s = sin[None, None]
            return jnp.concatenate([x1 * c - x2 * s, x1 * s + x2 * c], axis=-1)
        b, t, _ = x.shape
        cos, sin = _rope_tables(HEAD_DIM, ROPE_BASE, t)
        q = (x @ Wq).reshape(b, t, N_HEADS, HEAD_DIM).transpose(0, 2, 1, 3)
        k = (x @ Wk).reshape(b, t, N_KV, HEAD_DIM).transpose(0, 2, 1, 3)
        v = (x @ Wv).reshape(b, t, N_KV, HEAD_DIM).transpose(0, 2, 1, 3)
        q = _apply_rope(q, cos, sin)
        k = _apply_rope(k, cos, sin)
        k_h = jnp.repeat(k, GROUP_SIZE, axis=1)
        v_h = jnp.repeat(v, GROUP_SIZE, axis=1)
        scores = jnp.einsum('bhqd,bhkd->bhqk', q, k_h) / math.sqrt(HEAD_DIM)
        causal = jnp.triu(jnp.ones((t, t), dtype=bool), k=1)
        scores = jnp.where(causal[None, None], jnp.finfo(scores.dtype).min, scores)
        attn = jax.nn.softmax(scores, axis=-1)
        ctx = jnp.einsum('bhqk,bhkd->bhqd', attn, v_h)
        ctx = ctx.transpose(0, 2, 1, 3).reshape(b, t, D_OUT)
        return ctx @ Wo

    def _L2_ffn_ref(x, w1, w1_scale, w3, w3_scale, w2, w2_scale):
        import jax, jax.numpy as jnp
        import numpy as np
        BS = 128
        FP8_MAX = 448.0

        def act_quant(x):
            T, K = x.shape
            xb = x.reshape(T, K // BS, BS)
            amax = jnp.max(jnp.abs(xb), axis=-1)
            scale = amax / FP8_MAX + 1e-12
            xq = (xb / scale[:, :, None]).reshape(T, K)
            return (xq, scale)

        def linear_dsv3(x, wq, w_scale):
            T, K = x.shape
            N = wq.shape[0]
            xq, xs = act_quant(x)
            xdq = (xq.reshape(T, K // BS, BS) * xs[:, :, None]).reshape(T, K)
            wdq = (wq.reshape(N // BS, BS, K // BS, BS) * w_scale[:, None, :, None]).reshape(N, K)
            return xdq @ wdq.T
        B, S, D = x.shape
        xf = x.reshape(-1, D)
        g = linear_dsv3(xf, w1, w1_scale)
        u = linear_dsv3(xf, w3, w3_scale)
        h = jax.nn.silu(g) * u
        y = linear_dsv3(h, w2, w2_scale)
        return y.reshape(B, S, D)

    def _L3_attn_ref(x, Wq, Wk, Wv, Wo):
        import jax, jax.numpy as jnp
        import numpy as np
        NUM_HEADS = 32
        NUM_KV_GROUPS = 8
        ROPE_BASE = 10000.0

        def _rope_tables(seq_len, head_dim):
            inv_freq = 1.0 / ROPE_BASE ** (jnp.arange(0, head_dim, 2, dtype=jnp.float32) / head_dim)
            ang = jnp.arange(seq_len, dtype=jnp.float32)[:, None] * inv_freq[None, :]
            ang = jnp.concatenate([ang, ang], axis=-1)
            return (jnp.cos(ang), jnp.sin(ang))

        def _apply_rope(t, cos, sin):
            hd = t.shape[-1]
            x1, x2 = (t[..., :hd // 2], t[..., hd // 2:])
            rotated = jnp.concatenate([-x2, x1], axis=-1)
            return t * cos[None, None] + rotated * sin[None, None]
        B, S, D = x.shape
        H, G = (NUM_HEADS, NUM_KV_GROUPS)
        hd = D // H
        gs = H // G
        q = (x @ Wq).reshape(B, S, H, hd).transpose(0, 2, 1, 3)
        k = (x @ Wk).reshape(B, S, G, hd).transpose(0, 2, 1, 3)
        v = (x @ Wv).reshape(B, S, G, hd).transpose(0, 2, 1, 3)
        cos, sin = _rope_tables(S, hd)
        q = _apply_rope(q, cos, sin)
        k = _apply_rope(k, cos, sin)
        k = jnp.repeat(k, gs, axis=1)
        v = jnp.repeat(v, gs, axis=1)
        scores = jnp.einsum('bhqd,bhkd->bhqk', q, k)
        causal = jnp.triu(jnp.ones((S, S), dtype=bool), k=1)
        scores = jnp.where(causal[None, None], -jnp.inf, scores)
        attn = jax.nn.softmax(scores / jnp.sqrt(jnp.float32(hd)), axis=-1)
        ctx = jnp.einsum('bhqk,bhkd->bqhd', attn, v).reshape(B, S, D)
        return ctx @ Wo

    def _L3_ffn_ref(x, U1, V1, U2, V2, b1, b2):
        import jax, jax.numpy as jnp
        import numpy as np
        HIDDEN = 512
        INTER = 1376
        RANK = 128
        B, S = (2, 256)
        P = jnp.einsum('bsh,hr->bsr', x, U1)
        H = jnp.einsum('bsr,rf->bsf', P, V1) + b1
        gate, up = (H[..., :INTER], H[..., INTER:])
        act = jax.nn.silu(gate) * up
        Z = jnp.einsum('bsi,ir->bsr', act, U2)
        out = jnp.einsum('bsr,rh->bsh', Z, V2) + b2
        return out
    x = L0_attn_hidden_states
    xn = _layernorm(x, axis=-1)
    s = _L0_attn_ref(xn, L0_attn_Wq, L0_attn_Wk, L0_attn_Wv, L0_attn_Wo)
    g = _silu(_L0_ffn_ref(xn, L0_ffn_w_gate, L0_ffn_w_up, L0_ffn_w_down))
    x = x + s * g
    xn = _layernorm(x, axis=-1)
    s = _L1_attn_ref(xn, L1_attn_Wq, L1_attn_Wk, L1_attn_Wv, L1_attn_Wo)
    g = _silu(_L1_ffn_ref(xn, L1_ffn_qweight, L1_ffn_qzeros, L1_ffn_scales, L1_ffn_g_idx, L1_ffn_bias))
    x = x + s * g
    xn = _layernorm(x, axis=-1)
    s = _L2_attn_ref(xn, L2_attn_Wq, L2_attn_Wk, L2_attn_Wv, L2_attn_Wo)
    g = _silu(_L2_ffn_ref(xn, L2_ffn_w1, L2_ffn_w1_scale, L2_ffn_w3, L2_ffn_w3_scale, L2_ffn_w2, L2_ffn_w2_scale))
    x = x + s * g
    xn = _layernorm(x, axis=-1)
    s = _L3_attn_ref(xn, L3_attn_Wq, L3_attn_Wk, L3_attn_Wv, L3_attn_Wo)
    g = _silu(_L3_ffn_ref(xn, L3_ffn_U1, L3_ffn_V1, L3_ffn_U2, L3_ffn_V2, L3_ffn_b1, L3_ffn_b2))
    x = x + s * g
    return x

_drawn_inputs = setup_inputs


def setup_inputs(seed=0):
    import zlib

    import numpy as np

    out = dict(_drawn_inputs(seed))
    spreads = {}
    factors = {}
    for name, (base, spread) in spreads.items():
        noise = np.random.default_rng([zlib.crc32(name.encode()), seed]).standard_normal(out[name].shape)
        drawn = base * np.exp(spread * noise) if base else spread * noise
        out[name] = jnp.asarray(drawn.astype(out[name].dtype))
    for name, factor in factors.items():
        out[name] = (out[name] * factor).astype(out[name].dtype)
    return out
```

```python
from contextlib import ExitStack

import concourse.bass as bass
import numpy as np
from concourse import mybir

F32 = mybir.dt.float32
F32R = mybir.dt.float32r
BF16 = mybir.dt.bfloat16
F16 = mybir.dt.float16
I32 = mybir.dt.int32
ALU = mybir.AluOpType
ACT = mybir.ActivationFunctionType
AX = mybir.AxisListType

P = 128
D = 512
KC = D // P
SEQS, SEQ = 4, 256
TILES = SEQS * SEQ // P
HEADS, HD = 32, 16
UNITS = 2 * SEQS
UH = 16
GROUPS = UH // 4
LAYERS = 4
GQA = [True, False, True, True]
CAUSAL = [True, False, True, True]
ROPE = [True, False, True, True]
ROPE_BASE = {0: 10000.0, 2: 500000.0, 3: 10000.0}
EPS = 1e-5
SPLIT = 16
STACK = 3 * SPLIT
NEG = -1.0e30
ROUND = 1.5 * 2.0 ** 23
HID0, HC0 = 1360, 11
HC2 = 14
HC3 = 11
INTER3 = 1376
OCT = 8


def octonion_table():
    s = np.zeros((8, 8, 8), np.float32)
    s[0, 0, 0] = 1.0
    for i in range(1, 8):
        s[0, i, i] = 1.0
        s[i, 0, i] = 1.0
        s[i, i, 0] = -1.0
    for a, b, c in [(1, 2, 3), (1, 4, 5), (1, 7, 6), (2, 4, 6), (2, 5, 7), (3, 4, 7), (3, 6, 5)]:
        for x, y, z in ((a, b, c), (b, c, a), (c, a, b)):
            s[x, y, z] = 1.0
            s[y, x, z] = -1.0
    which = np.abs(s).argmax(axis=0)
    sign = np.take_along_axis(s, which[None], axis=0)[0]
    return which, sign


class Mark:

    def __init__(self, nc, ctx, name, per_layer):
        self.sem = ctx.enter_context(nc.semaphore(name))
        self.per_layer = per_layer

    def at(self, layer, n):
        return self.sem, sum(self.per_layer[:layer]) + n


class Banks:

    def __init__(self, nc, ctx):
        self.ps = [ctx.enter_context(nc.psum_tensor(f"bank{i}", [P, 512], F32)) for i in range(8)]
        self.full = [ctx.enter_context(nc.semaphore(f"bank{i}_filled")) for i in range(8)]
        self.free = [ctx.enter_context(nc.semaphore(f"bank{i}_emptied")) for i in range(8)]
        self.uses = [0] * 8
        self.where = {}

    def claim(self, key, bank):
        self.where[key] = (bank, self.uses[bank])
        self.uses[bank] += 1
        return self.ps[bank], self.uses[bank] > 1

    def before(self, key):
        bank, n = self.where[key]
        return self.free[bank], n

    def tensor(self, key):
        return self.ps[self.where[key][0]]

    def filled(self, key):
        bank, n = self.where[key]
        return self.full[bank], n + 1

    def emptied(self, key):
        bank, n = self.where[key]
        return self.free[bank], n + 1

    def fills(self, key):
        return self.full[self.where[key][0]]

    def empties(self, key):
        return self.free[self.where[key][0]]


def program(nc, a, out):
    ctx = ExitStack()
    with ctx:
        def sem(name):
            return ctx.enter_context(nc.semaphore(name))

        base = 16512
        top = [base]
        names = {}

        def place(name, shape, dt, at=None):
            size = 2 if dt in (BF16, F16) else 4
            n = size
            for s in shape[1:]:
                n *= s
            n = (n + 31) // 32 * 32
            off = top[0] if at is None else at[0]
            t = nc.alloc_sbuf_tensor_at(name, shape, dt, offset=off)
            if at is None:
                top[0] += n
            else:
                at[0] += n
            names[name] = (off, n)
            return t

        x = place("x", [P, TILES, D], F32)
        xT = place("xT", [P, KC, TILES * P], F32)
        gate = place("gate", [P, TILES, D], F32)
        xn = [nc.alloc_sbuf_tensor_at(f"xn{i}", [P, D], F32, offset=names["gate"][0] + (4 + i) * D * 4) for i in range(4)]
        ident = place("ident", [P, P], F32)
        identb = place("identb", [P, P], BF16)
        mask = place("mask", [P, 2 * P], BF16)
        maskf = place("maskf", [P, 2 * P], F32)
        cosT = {l: place(f"cos{l}", [P, 2, HD], F32) for l in (0, 2, 3)}
        sinT = {l: place(f"sin{l}", [P, 2, HD], F32) for l in (0, 2, 3)}
        ones = place("ones", [P, P], F32)
        stats = place("stats", [P, TILES, 6], F32)
        moments = place("moments", [P, TILES, 2], F32)
        vareps = place("vareps", [P, TILES], F32)
        minus_half = place("minus_half", [P, TILES], F32)
        rstd = place("rstd", [P, TILES], F32)
        Wqkv = place("Wqkv", [P, KC, 2, 768], F32)
        Wo = place("Wo", [P, KC, D], F32)
        shared = top[0]

        at = [shared]
        qT = [place(f"qT{i}", [P, UH // 2, SEQ], F32R, at) for i in range(2)]
        kT = [place(f"kT{i}", [P, UH // 2, SEQ], F32R, at) for i in range(2)]
        qstack = [place(f"qstack{i}", [P, UH, 64], F32, at) for i in range(2)]
        kstack = [place(f"kstack{i}", [P, UH, 64], F32, at) for i in range(2)]
        qk = [place(f"qk{i}", [P, 2 * UH, HD], F32, at) for i in range(2)]
        rc = [place(f"rope_cos{i}", [P, 20, HD], F32, at) for i in range(2)]
        rs = [place(f"rope_sin{i}", [P, 20, HD], F32, at) for i in range(2)]
        qkr = [place(f"qk_roped{i}", [P, 20, HD], F32, at) for i in range(2)]
        V = [place(f"V{i}", [P, 2, UH, 32], F32, at) for i in range(4)]
        probs = [place(f"probs{i}", [P, 2, 4, SEQ], F32, at) for i in range(2)]
        pv = [place(f"pv{i}", [P, SEQ], F32, at) for i in range(2)]
        ctxr = [place(f"ctx{i}", [P, 2, D], F32, at) for i in range(2)]
        ctxT = [place(f"ctxT{i}", [P, KC, P], F32, at) for i in range(2)]
        gated = [place(f"gated{i}", [P, D], F32, at) for i in range(2)]
        negmax = [place(f"negmax{i}", [P, 2, UH], F32, at) for i in range(2)]
        negmaxT = [place(f"negmaxT{i}", [UH, SEQ], F32R, at) for i in range(2)]
        recip = [place(f"recip{i}", [P, 2, 4], F32, at) for i in range(2)]
        assert at[0] <= 229344, at[0]

        at = [shared]
        hT = place("hT", [P, HC2, 512], F32, at)
        silu = [place(f"silu{i}", [P, 512], F32, at) for i in range(2)]
        weights_from = at[0]
        Wgu0 = [place(f"W{n}0", [P, KC, HC0 * P], F32, at) for n in ("gate", "up")]
        Wd0 = place("Wdown0", [P, HC0, D], F32, at)
        sign_in = place("sign_in", [P, KC, OCT], F32, at)
        sign_hid = place("sign_hid", [P, HC0, OCT], F32, at)
        absum = place("absum", [P, 3], F32, at)
        tscale = place("tscale", [P, 3], F32, at)
        tinv = place("tinv", [P, 3], F32, at)
        assert at[0] <= 229344, at[0]
        at = [weights_from]
        W1q = place("W1q", [P, KC, D], I32, at)
        W1n = place("W1n", [P, KC, D], I32, at)
        W1f = place("W1f", [P, D], F32, at)
        W1h = place("W1h", [P, KC, D], F16, at)
        W1 = place("W1", [P, KC, D], F32, at)
        zq = place("zq", [4, 64], I32, at)
        zn = place("zn", [4, 64, 8], I32, at)
        zf = place("zf", [4, D], F32, at)
        sh = place("sh", [4, D], F16, at)
        sf = place("sf", [4, D], F32, at)
        gidx = place("gidx", [4, D], I32, at)
        onehot = place("onehot", [4, D], F32, at)
        four = place("four", [4, 1], F32, at)
        bias1 = place("bias1", [1, D], F16, at)
        ones16 = place("ones16", [1, P], F16, at)
        zr = place("zr", [P, D], F32, at)
        at = [weights_from]
        W2gu = [place(f"W{n}2", [P, HC2, KC, P], F32, at) for n in ("gate", "up")]
        W2d = place("Wdown2", [P, HC2, D], F32, at)
        s2 = [place(f"wscale{i}", [P, HC2, KC], F32, at) for i in range(3)]
        assert at[0] <= 229344, at[0]
        at = [weights_from]
        U1 = place("U1", [P, KC, P], F32, at)
        V1 = place("V1", [P, 2, HC3, P], F32, at)
        U2 = place("U2", [P, HC3, P], F32, at)
        V2 = place("V2", [P, D], F32, at)
        b1 = place("b1", [P, 2, HC3], F32, at)
        b2 = place("b2", [P, D], F32, at)
        PT = place("PT", [P, 2, 512], F32, at)
        ZT = place("ZT", [P, 2, 512], F32, at)
        outb = [place(f"outb{i}", [P, D], F32, at) for i in range(2)]

        B = Banks(nc, ctx)
        x_in = [sem(f"x_loaded{i}") for i in range(SEQS)]
        const_in = sem("constants_loaded")
        att_in = sem("attention_weights_loaded")
        ffn_in = [sem(f"ffn_weights_loaded{i}") for i in range(3)]
        w2_in = [sem(f"ffn2_chunk_loaded{i}") for i in range(HC2)]
        m_rows = [sem(f"max_rows_placed{i}") for i in range(2)]
        out_done = sem("output_stored")

        def mark(name, per_layer):
            return Mark(nc, ctx, name, per_layer)

        ones_set = mark("ones_set", [2, 0, 0, 0])
        mask_set = mark("mask_set", [2, 0, 0, 0])
        ln_stat = mark("row_stats", [TILES] * 4)
        ln_mom = mark("row_moments", [TILES] * 4)
        ln_var = mark("row_variance", [SEQS] * 4)
        ln_rstd = mark("row_rstd", [SEQS] * 4)
        xn_ready = mark("rows_normalised", [TILES] * 4)
        tern = mark("ternary_steps", [100, 0, 0, 0])
        deq = mark("dequant_steps", [0, 100, 0, 0])
        deq_done = mark("dequantised", [0, KC, 0, 0])
        w_scaled = mark("weights_scaled", [0, 0, 3 * HC2, 0])
        gate_ready = mark("gate_ready", [0, 0, 0, TILES])
        rope_part = mark("rope_parts", [48, 0, 48, 48])
        rope_done = mark("rope_done", [16, 0, 16, 16])
        hi_ops = [3, 2, 3, 3]
        stack_hi = mark("stack_hi", [16 * n for n in hi_ops])
        stack_lo = mark("stack_lo", [32] * 4)
        pads = mark("pads_set", [2 * 3 + 4 * 2] * 4)
        PADS = 2 * 3 + 4 * 2
        causal_cut = mark("causal_cut", [64, 0, 64, 64])
        rs_ready = mark("reciprocal_ready", [32] * 4)
        x_done = mark("x_updated", [TILES] * 4)

        last_out = {l: ("out", l, TILES - 1) for l in range(LAYERS)}

        def pairs_slot(l, g, pair):
            return g if GQA[l] else pair

        block = ctx.enter_context(nc.Block())

        @block.tensor
        def _(pe):
            misc = [0]
            ring_s = [0]
            ring_t = [0]
            mm = nc.tensor.matmul

            def misc_bank():
                misc[0] += 1
                return 6 + misc[0] % 2

            def transposes(l):
                for t in range(TILES):
                    key = ("xT", l, t)
                    ps, again = B.claim(key, 4 + t % 4)
                    if again:
                        pe.wait_ge(*B.before(key))
                    pe.wait_ge(*xn_ready.at(l, t + 1))
                    for c in range(KC):
                        ins = nc.tensor.transpose(ps[:, c * P:(c + 1) * P], xn[t % 4][:, c * P:(c + 1) * P], ident[:])
                    ins.then_inc(B.fills(key), 1)

            def hidden(l, n, chunks, wait_weights, lhs, rhs):
                for j in range(chunks):
                    slot = (n * chunks + j) % 2
                    for which in range(2):
                        key = (("gate", "up")[which], l, n, j)
                        ps, again = B.claim(key, 2 * slot + which)
                        if again:
                            pe.wait_ge(*B.before(key))
                        if n == 0:
                            wait_weights(j, which)
                        terms = rhs(n)
                        for c, r in enumerate(terms):
                            ins = mm(ps[:], lhs(which, c, j), r, start=(c == 0), stop=(c == len(terms) - 1))
                        ins.then_inc(B.fills(key), 1)

            def out_tile(l, t, terms):
                key = ("out", l, t)
                ps, again = B.claim(key, 4 + t % 4)
                if again:
                    pe.wait_ge(*B.before(key))
                for c, (lh, rh) in enumerate(terms):
                    ins = mm(ps[:], lh, rh, start=(c == 0), stop=(c == len(terms) - 1))
                ins.then_inc(B.fills(key), 1)

            def x_terms(n):
                return [xT[:, c, n * 512:(n + 1) * 512] for c in range(KC)]

            def ffn(l):
                if l == 0:
                    pe.wait_ge(*ones_set.at(0, 2))
                    for m in range(3):
                        key = ("wsum", m)
                        ps, again = B.claim(key, m)
                        pe.wait_ge(*tern.at(0, 5 * m + 1))
                        mm(ps[:, 0:1], ones[:], absum[:, m:m + 1], start=True, stop=True).then_inc(B.fills(key), 1)
                if l == 1:
                    pe.wait_ge(*deq.at(1, 12))
                    for c in range(KC):
                        for which, src in ((0, zf), (1, sf)):
                            key = ("group", c, which)
                            ps, again = B.claim(key, (2 * c + which) % 4)
                            if again:
                                pe.wait_ge(*B.before(key))
                            mm(ps[:], onehot[:, c * P:(c + 1) * P], src[:], start=True, stop=True).then_inc(B.fills(key), 1)
                if l == 3:
                    pe.wait_ge(ffn_in[0], 16 * LOADS[3])
                for n in range(2):
                    pe.wait_ge(*B.emptied(("xT", l, 4 * n + 3)))
                    if l in (0, 2):
                        chunks = HC0 if l == 0 else HC2

                        def wait_weights(j, which):
                            if l == 0 and j == 0:
                                pe.wait_ge(*tern.at(0, 5 * (which + 1)))
                            if l == 2:
                                pe.wait_ge(*w_scaled.at(2, 3 * j + which + 1))

                        def lhs(which, c, j):
                            if l == 0:
                                return Wgu0[which][:, c, j * P:(j + 1) * P]
                            return W2gu[which][:, j, c, :]

                        hidden(l, n, chunks, wait_weights, lhs, x_terms)
                        pe.wait_ge(*B.emptied(("up", l, n, chunks - 1)))
                        if l == 0:
                            pe.wait_ge(*tern.at(0, 15))
                        else:
                            pe.wait_ge(*w_scaled.at(2, 3 * HC2))
                        Wd = Wd0 if l == 0 else W2d
                        for t in range(4 * n, 4 * n + 4):
                            out_tile(l, t, [(hT[:, c, (t % 4) * P:(t % 4 + 1) * P], Wd[:, c, :]) for c in range(chunks)])
                    if l == 1:
                        pe.wait_ge(*deq_done.at(1, KC))
                        for t in range(4 * n, 4 * n + 4):
                            out_tile(l, t, [(xT[:, c, t * P:(t + 1) * P], W1[:, c, :]) for c in range(KC)]
                                     + [(ones16[:], bias1[:])])
                    if l == 3:
                        key = ("low", n)
                        ps, again = B.claim(key, n)
                        if again:
                            pe.wait_ge(*B.before(key))
                        for c, r in enumerate(x_terms(n)):
                            ins = mm(ps[:], U1[:, c, :], r, start=(c == 0), stop=(c == KC - 1))
                        ins.then_inc(B.fills(key), 1)
                        pe.wait_ge(*B.emptied(key))
                        hidden(l, n, HC3, lambda j, which: None, lambda which, c, j: V1[:, which, j, :],
                               lambda n: [PT[:, n, :]])
                        pe.wait_ge(*B.emptied(("up", l, n, HC3 - 1)))
                        key = ("low2", n)
                        ps, again = B.claim(key, n)
                        pe.wait_ge(*B.before(key))
                        for c in range(HC3):
                            ins = mm(ps[:], U2[:, c, :], hT[:, c, :], start=(c == 0), stop=(c == HC3 - 1))
                        ins.then_inc(B.fills(key), 1)
                        pe.wait_ge(*B.emptied(key))
                        for t in range(4 * n, 4 * n + 4):
                            out_tile(l, t, [(ZT[:, n, (t % 4) * P:(t % 4 + 1) * P], V2[:])])

            def project(l, u, tau):
                t, hh = 2 * (u // 2) + tau, u % 2
                if u == 0 and tau == 0:
                    pe.wait_ge(att_in, 32 * (l + 1))
                    pe.wait_ge(*mask_set.at(0, 2))
                for key, c0, width in ([(("qkv", l, u, tau), 0, 384)] if GQA[l] else
                                       [(("qkv", l, u, tau), 0, 512), (("v", l, u, tau), 512, 256)]):
                    ps, again = B.claim(key, misc_bank())
                    pe.wait_ge(*B.before(key))
                    for c in range(KC):
                        ins = mm(ps[:, 0:width], xT[:, c, t * P:(t + 1) * P], Wqkv[:, c, hh, c0:c0 + width],
                                 start=(c == 0), stop=(c == KC - 1))
                    ins.then_inc(B.fills(key), 1)

            def turn_stacks(l, u, tau):
                i = 2 * u + tau
                pe.wait_ge(*pads.at(l, PADS))
                pe.wait_ge(*stack_hi.at(l, hi_ops[l] * (i + 1)))
                pe.wait_ge(*stack_lo.at(l, 2 * (i + 1)))
                for name, stack, banks in (("qT", qstack, 2), ("kT", kstack, 1 if GQA[l] else 2)):
                    for w in range(banks):
                        key = (name, l, u, tau, w)
                        ps, again = B.claim(key, misc_bank())
                        pe.wait_ge(*B.before(key))
                        for p in range(4):
                            src = stack[i % 2][:, 2 * (4 * w + p):2 * (4 * w + p) + 2, :].rearrange("p a b -> p (a b)")
                            ins = nc.tensor.transpose(ps[:, p * P:(p + 1) * P], src, ident[:])
                        ins.then_inc(B.fills(key), 1)

            def scores_rows(l, u, g):
                if g == 0:
                    for tau in range(2):
                        pe.wait_ge(*B.emptied(("qT", l, u, tau, 1)))
                        pe.wait_ge(*B.emptied(("kT", l, u, tau, 0 if GQA[l] else 1)))
                for qb in range(2):
                    nk = (qb + 1) * P if CAUSAL[l] else SEQ
                    for par in range(2):
                        key = ("S", l, u, g, qb, par)
                        ring_s[0] += 1
                        ps, again = B.claim(key, ring_s[0] % 3)
                        pe.wait_ge(*B.before(key))
                        r = 64 * par
                        for pl in range(2):
                            pair = 2 * g + pl
                            ins = mm(ps[:, pl * nk:(pl + 1) * nk],
                                     qT[u % 2][r:r + STACK, pair, qb * P:(qb + 1) * P],
                                     kT[u % 2][r:r + STACK, pairs_slot(l, g, pair), 0:nk],
                                     start=(pl == 0), stop=not CAUSAL[l], skip_group_check=True)
                        if CAUSAL[l]:
                            dst = ps[:, 0:2 * nk].rearrange("p (h k) -> p h k", h=2)[:, :, nk - P:nk]
                            ins = mm(dst, identb[:], mask[:].rearrange("p (h k) -> p h k", h=2),
                                     start=False, stop=True, skip_group_check=True)
                        ins.then_inc(B.fills(key), 1)

            def turn_max(l, u):
                key = ("mT", l, u)
                ps, again = B.claim(key, misc_bank())
                pe.wait_ge(*B.before(key))
                pe.wait_ge(*B.emptied(("S", l, u, GROUPS - 1, 1, 1)))
                for qb in range(2):
                    ins = nc.tensor.transpose(ps[0:UH, qb * P:(qb + 1) * P], negmax[u % 2][:, qb, :], ident[:])
                ins.then_inc(B.fills(key), 1)

            def scores_cols(l, u, g):
                if g == 0:
                    pe.wait_ge(m_rows[u % 2], 32 * (4 * l + u // 2 + 1))
                for kb in range(2):
                    q0 = kb * P if CAUSAL[l] else 0
                    nq = SEQ - q0
                    for par in range(2):
                        key = ("ST", l, u, g, kb, par)
                        ring_t[0] += 1
                        ps, again = B.claim(key, 3 + ring_t[0] % 3)
                        pe.wait_ge(*B.before(key))
                        r = 64 * par
                        for pl in range(2):
                            pair = 2 * g + pl
                            ins = mm(ps[:, pl * nq:(pl + 1) * nq],
                                     kT[u % 2][r:r + STACK + 1, pairs_slot(l, g, pair), kb * P:(kb + 1) * P],
                                     qT[u % 2][r:r + STACK + 1, pair, q0:SEQ], start=True, stop=True)
                        ins.then_inc(B.fills(key), 1)

            def weigh_values(l, gi):
                u, g = gi // GROUPS, gi % GROUPS
                key = ("PV", l, gi)
                ps, again = B.claim(key, misc_bank())
                pe.wait_ge(*B.before(key))
                if CAUSAL[l]:
                    pe.wait_ge(*causal_cut.at(l, 2 * (gi + 1)))
                else:
                    pe.wait_ge(*B.emptied(("ST", l, u, g, 1, 1)))
                for tau in range(2):
                    pe.wait_ge(*B.emptied(("qkv" if GQA[l] else "v", l, u, tau)))
                for kb in range(2):
                    q0 = kb * P if CAUSAL[l] else 0
                    for i in range(4):
                        kv = g if GQA[l] else 4 * g + i
                        ins = mm(ps[32 * i:32 * i + 32, q0:SEQ], V[u % 4][:, kb, kv, :], probs[gi % 2][:, kb, i, q0:SEQ],
                                 start=(kb == 0), stop=(kb == 1))
                ins.then_inc(B.fills(key), 1)

            def turn_context(l, gi):
                key = ("ctx", l, gi)
                ps, again = B.claim(key, misc_bank())
                pe.wait_ge(*B.before(key))
                pe.wait_ge(*B.emptied(("PV", l, gi)))
                for qb in range(2):
                    ins = nc.tensor.transpose(ps[:, qb * P:(qb + 1) * P], pv[gi % 2][:, qb * P:(qb + 1) * P], ident[:])
                ins.then_inc(B.fills(key), 1)

            def turn_rows(l, b):
                for tau in range(2):
                    key = ("ctxT", l, b, tau)
                    ps, again = B.claim(key, misc_bank())
                    pe.wait_ge(*B.before(key))
                    pe.wait_ge(*B.emptied(("ctx", l, 8 * b + 7)))
                    for c in range(KC):
                        ins = nc.tensor.transpose(ps[:, c * P:(c + 1) * P], ctxr[b % 2][:, tau, c * P:(c + 1) * P], ident[:])
                    ins.then_inc(B.fills(key), 1)

            def project_out(l, b):
                for tau in range(2):
                    key = ("O", l, b, tau)
                    ps, again = B.claim(key, misc_bank())
                    pe.wait_ge(*B.before(key))
                    pe.wait_ge(*B.emptied(("ctxT", l, b, tau)))
                    for c in range(KC):
                        ins = mm(ps[:], ctxT[tau][:, c, :], Wo[:, c, :], start=(c == 0), stop=(c == KC - 1))
                    ins.then_inc(B.fills(key), 1)

            def attention(l):
                for u in range(2):
                    for tau in range(2):
                        project(l, u, tau)
                for tau in range(2):
                    turn_stacks(l, 0, tau)
                for g in range(GROUPS):
                    scores_rows(l, 0, g)
                for tau in range(2):
                    turn_stacks(l, 1, tau)
                turn_max(l, 0)
                for u in range(UNITS):
                    if u + 2 < UNITS:
                        for tau in range(2):
                            project(l, u + 2, tau)
                    for g in range(GROUPS):
                        gi = GROUPS * u + g
                        scores_cols(l, u, g)
                        if u + 1 < UNITS:
                            scores_rows(l, u + 1, g)
                        if gi >= 1:
                            weigh_values(l, gi - 1)
                        if gi >= 2:
                            turn_context(l, gi - 2)
                        if u % 2 == 0 and u > 0 and g == 2:
                            turn_rows(l, u // 2 - 1)
                        if u % 2 == 0 and u > 0 and g == 3:
                            project_out(l, u // 2 - 1)
                    if u + 1 < UNITS:
                        turn_max(l, u + 1)
                    if u + 2 < UNITS:
                        for tau in range(2):
                            turn_stacks(l, u + 2, tau)
                weigh_values(l, 31)
                turn_context(l, 30)
                turn_context(l, 31)
                turn_rows(l, SEQS - 1)
                project_out(l, SEQS - 1)

            pe.wait_ge(const_in, 16 * CONSTS)
            for l in range(LAYERS):
                transposes(l)
                ffn(l)
                attention(l)

        @block.scalar
        def _(act):
            copy = ACT.Copy

            def empty(key, dst, src, func=copy, **kw):
                act.wait_ge(*B.filled(key))
                return nc.scalar.activation(dst, src, func, **kw)

            def transposes(l):
                for t in range(TILES):
                    key = ("xT", l, t)
                    act.wait_ge(*B.filled(key))
                    nc.scalar.activation(xT[:, :, t * P:(t + 1) * P], B.tensor(key)[:].rearrange("p (c t) -> p c t", c=KC),
                                         copy).then_inc(B.empties(key), 1)

            def hidden(l, n, chunks):
                for j in range(chunks):
                    e = n * chunks + j
                    key = ("gate", l, n, j)
                    act.wait_ge(*B.filled(key))
                    if e >= 2:
                        act.wait_ge(*B.emptied(("up", l, (e - 2) // chunks, (e - 2) % chunks)))
                    kw = {}
                    if l == 0:
                        kw = {"scale": tscale[:, 0:1]}
                    if l == 3:
                        kw = {"bias": b1[:, 0, j:j + 1]}
                    nc.scalar.activation(silu[e % 2][:], B.tensor(key)[:], ACT.Silu, **kw).then_inc(B.empties(key), 1)

            def out_tiles(l, n):
                for t in range(4 * n, 4 * n + 4):
                    key = ("out", l, t)
                    if l == 3:
                        act.wait_ge(*B.emptied(key))
                        nc.scalar.activation(gate[:, t, :], outb[t % 2][:], ACT.Silu).then_inc(gate_ready.sem, 1)
                        continue
                    act.wait_ge(*B.filled(key))
                    kw = {"scale": tscale[:, 2:3]} if l == 0 else {}
                    nc.scalar.activation(gate[:, t, :], B.tensor(key)[:], ACT.Silu, **kw).then_inc(B.empties(key), 1)

            def ffn(l):
                for n in range(2):
                    if l == 0 and n == 0:
                        act.wait_ge(*tern.at(0, 15))
                    if l == 3:
                        key = ("low", n)
                        act.wait_ge(*B.filled(key))
                        nc.scalar.activation(PT[:, n, :], B.tensor(key)[:], copy).then_inc(B.empties(key), 1)
                    if l != 1:
                        hidden(l, n, {0: HC0, 2: HC2, 3: HC3}[l])
                    if l == 3:
                        key = ("low2", n)
                        act.wait_ge(*B.filled(key))
                        nc.scalar.activation(ZT[:, n, :], B.tensor(key)[:], copy).then_inc(B.empties(key), 1)
                    out_tiles(l, n)

            def take_projection(l, u, tau):
                i = 2 * u + tau
                key = ("qkv", l, u, tau)
                ps = B.tensor(key)
                nqk = 20 if GQA[l] else 32
                act.wait_ge(*B.filled(key))
                if i >= 2 and GQA[l]:
                    act.wait_ge(*rope_part.at(l, 3 * (i - 1)))
                if i >= 2 and not GQA[l]:
                    act.wait_ge(*stack_lo.at(l, 2 * (i - 1)))
                ins = nc.scalar.activation(qk[i % 2][:, 0:nqk, :], ps[:, 0:nqk * HD].rearrange("p (h d) -> p h d", d=HD), copy)
                if GQA[l]:
                    nc.scalar.activation(V[u % 4][:, tau, 0:4, 0:HD], ps[:, 320:384].rearrange("p (h d) -> p h d", d=HD),
                                         copy).then_inc(B.empties(key), 1)
                else:
                    ins.then_inc(B.empties(key), 1)
                    key = ("v", l, u, tau)
                    act.wait_ge(*B.filled(key))
                    nc.scalar.activation(V[u % 4][:, tau, :, 0:HD],
                                         B.tensor(key)[:, 0:256].rearrange("p (h d) -> p h d", d=HD),
                                         copy).then_inc(B.empties(key), 1)

            def stack_high(l, u, tau):
                i = 2 * u + tau
                if ROPE[l]:
                    act.wait_ge(*rope_done.at(l, i + 1))
                    src = qkr[i % 2]
                else:
                    act.wait_ge(*B.emptied(("qkv", l, u, tau)))
                    src = qk[i % 2]
                qs = qstack[i % 2][:].bitcast(F32R)
                ks = kstack[i % 2][:].bitcast(F32R)
                if i >= 2:
                    act.wait_ge(*B.filled(("kT", l, u - 1, tau, 0 if GQA[l] else 1)))
                    act.wait_ge(*B.filled(("qT", l, u - 1, tau, 1)))
                dst = qs[:, :, 0:48].rearrange("p h (s d) -> p h s d", d=SPLIT)[:, :, 0:3:2, :]
                nc.scalar.activation(dst, src[:, 0:UH, :].unsqueeze(2).to_broadcast([P, UH, 2, HD]), copy).then_inc(stack_hi.sem, 1)
                if GQA[l]:
                    kd = ks[:, 0:8, 0:32].rearrange("p (g c) (s d) -> p g c s d", c=2, d=SPLIT)
                    for dup in range(2):
                        nc.scalar.activation(kd[:, :, dup], src[:, UH:UH + 4, :].unsqueeze(2).to_broadcast([P, 4, 2, HD]),
                                             copy).then_inc(stack_hi.sem, 1)
                else:
                    kd = ks[:, :, 0:32].rearrange("p h (s d) -> p h s d", d=SPLIT)
                    nc.scalar.activation(kd, src[:, UH:2 * UH, :].unsqueeze(2).to_broadcast([P, UH, 2, HD]),
                                         copy).then_inc(stack_hi.sem, 1)

            def take_stacks(l, u, tau):
                for name, dst, banks in (("qT", qT, 2), ("kT", kT, 1 if GQA[l] else 2)):
                    for w in range(banks):
                        key = (name, l, u, tau, w)
                        act.wait_ge(*B.filled(key))
                        nc.scalar.activation(dst[u % 2][:, 4 * w:4 * w + 4, tau * P:(tau + 1) * P],
                                             B.tensor(key)[:].rearrange("p (a t) -> p a t", a=4),
                                             copy).then_inc(B.empties(key), 1)

            def exponentials(l, u, g):
                gi = GROUPS * u + g
                if gi >= 2:
                    act.wait_ge(*B.filled(("PV", l, gi - 2)))
                for kb in range(2):
                    q0 = kb * P if CAUSAL[l] else 0
                    nq = SEQ - q0
                    for par in range(2):
                        key = ("ST", l, u, g, kb, par)
                        act.wait_ge(*B.filled(key))
                        nc.scalar.activation(probs[gi % 2][:, kb, par:4:2, q0:SEQ],
                                             B.tensor(key)[:, 0:2 * nq].rearrange("p (h q) -> p h q", h=2),
                                             ACT.Exp, scale=0.25).then_inc(B.empties(key), 1)

            def take_pv(l, gi):
                key = ("PV", l, gi)
                act.wait_ge(*B.filled(key))
                nc.scalar.activation(pv[gi % 2][:], B.tensor(key)[:, 0:SEQ], copy).then_inc(B.empties(key), 1)

            def take_rows(l, b):
                for tau in range(2):
                    key = ("ctxT", l, b, tau)
                    act.wait_ge(*B.filled(key))
                    nc.scalar.activation(ctxT[tau][:].rearrange("p c t -> p (c t)"), B.tensor(key)[:],
                                         copy).then_inc(B.empties(key), 1)

            def attention(l):
                act.wait_ge(*(B.emptied(last_out[l]) if l != 3 else gate_ready.at(3, TILES)))
                for tau in range(2):
                    take_projection(l, 0, tau)
                for tau in range(2):
                    stack_high(l, 0, tau)
                for tau in range(2):
                    take_projection(l, 1, tau)
                for tau in range(2):
                    take_stacks(l, 0, tau)
                    stack_high(l, 1, tau)
                for tau in range(2):
                    take_stacks(l, 1, tau)
                for u in range(UNITS):
                    if u + 2 < UNITS:
                        for tau in range(2):
                            take_projection(l, u + 2, tau)
                    for g in range(GROUPS):
                        gi = GROUPS * u + g
                        exponentials(l, u, g)
                        if gi >= 1:
                            take_pv(l, gi - 1)
                        if g < 2 and u + 2 < UNITS:
                            stack_high(l, u + 2, g)
                        if u % 2 == 0 and u > 0 and g == 2:
                            take_rows(l, u // 2 - 1)
                    if u + 2 < UNITS:
                        for tau in range(2):
                            take_stacks(l, u + 2, tau)
                take_pv(l, 31)
                take_rows(l, SEQS - 1)

            for l in range(LAYERS):
                transposes(l)
                ffn(l)
                attention(l)

        @block.vector
        def _(dve):
            v = nc.vector

            def normalise(l):
                for b in range(SEQS):
                    for t in (2 * b, 2 * b + 1):
                        if l == 0:
                            dve.wait_ge(x_in[b], 16)
                        else:
                            dve.wait_ge(*x_done.at(l - 1, t + 1))
                        v.bn_stats(stats[:, t, :], x[:, t, :]).then_inc(ln_stat.sem, 1)
                    for t in (2 * b, 2 * b + 1):
                        dve.wait_ge(*ln_stat.at(l, t + 1))
                        v.bn_aggr(moments[:, t, :], stats[:, t, :]).then_inc(ln_mom.sem, 1)
                    dve.wait_ge(*ln_mom.at(l, 2 * b + 2))
                    v.tensor_scalar(vareps[:, 2 * b:2 * b + 2], moments[:, 2 * b:2 * b + 2, 1], EPS, None,
                                    ALU.add).then_inc(ln_var.sem, 1)
                    if b >= 1:
                        scale_rows(l, b - 1)
                scale_rows(l, SEQS - 1)

            def scale_rows(l, b):
                dve.wait_ge(*ln_rstd.at(l, b + 1))
                for t in (2 * b, 2 * b + 1):
                    if t >= 4:
                        dve.wait_ge(*B.filled(("xT", l, t - 4)))
                    dst, src = xn[t % 4][:], x[:, t, :]
                    if l == 1:
                        dst = xn[t % 4][:].rearrange("p (s r) -> p r s", s=8)
                        src = x[:, t, :].rearrange("p (r s) -> p r s", s=8)
                    v.tensor_scalar(dst, src, moments[:, t, 0:1], rstd[:, t:t + 1], ALU.subtract,
                                    ALU.mult).then_inc(xn_ready.sem, 1)

            def ternary():
                mats = [(Wgu0[0], 170, KC, HID0, sign_in), (Wgu0[1], 170, KC, HID0, sign_in), (Wd0, 64, HC0, D, sign_hid)]
                steps = [0]

                def step(ins):
                    steps[0] += 1
                    ins.then_inc(tern.sem, 1)
                    dve.wait_ge(*tern.at(0, steps[0]))

                for m, (W, width, chunks, cols, signs) in enumerate(mats):
                    dve.wait_ge(ffn_in[m], 16)
                    if m == 0:
                        dve.wait_ge(const_in, 16 * CONSTS)
                    step(v.tensor_reduce(absum[:, m:m + 1], W[:, :, 0:width], AX.XY, ALU.add, apply_absolute_value=True))
                    key = ("wsum", m)
                    dve.wait_ge(*B.filled(key))
                    ins = v.tensor_scalar(tscale[:, m:m + 1], B.tensor(key)[:, 0:1], 1.0 / (HID0 * D // OCT), None, ALU.mult)
                    ins.then_inc(B.empties(key), 1)
                    dve.wait_ge(*B.emptied(key))
                    step(v.reciprocal(tinv[:, m:m + 1], tscale[:, m:m + 1]))
                    step(v.tensor_scalar(W[:, :, 0:cols], W[:, :, 0:cols], tinv[:, m:m + 1], 1.0, ALU.mult, ALU.min))
                    step(v.tensor_scalar(W[:, :, 0:cols], W[:, :, 0:cols], -1.0, ROUND, ALU.max, ALU.add))
                    for c in range(chunks):
                        w = W[:, c, 0:cols].rearrange("p (k o) -> p k o", k=OCT)
                        ins = v.scalar_tensor_tensor(w, w, ROUND, signs[:, c, :].unsqueeze(2).to_broadcast([P, OCT, width]),
                                                     ALU.subtract, ALU.mult)
                    step(ins)

            def dequantise():
                steps = [0]

                def step(ins):
                    steps[0] += 1
                    ins.then_inc(deq.sem, 1)

                dve.wait_ge(ffn_in[0], 16 * (1 + LOADS[1]))
                for s in range(8):
                    step(v.tensor_scalar(zn[:, :, s], zq[:], 4 * s, 15, ALU.logical_shift_right, ALU.bitwise_and))
                dve.wait_ge(*deq.at(1, steps[0]))
                step(v.tensor_scalar(zf[:], zn[:].rearrange("g c s -> g (c s)"), 1.0, None, ALU.add))
                step(v.tensor_copy(sf[:], sh[:]))
                step(v.tensor_scalar(onehot[:], gidx[:], four[:, 0:1], None, ALU.is_equal))
                step(v.memset(ones16[:], 1.0))
                for c in range(KC):
                    for half in range(2):
                        r = slice(64 * half, 64 * half + 64)
                        step(v.tensor_scalar(W1n[r, c, :], W1q[r, c, :], 4 * (2 * c + half), 15,
                                             ALU.logical_shift_right, ALU.bitwise_and))
                    kz, ks = ("group", c, 0), ("group", c, 1)
                    dve.wait_ge(*deq.at(1, steps[0]))
                    dve.wait_ge(*B.filled(kz))
                    v.tensor_tensor(W1f[:], W1n[:, c, :], B.tensor(kz)[:], ALU.subtract).then_inc(B.empties(kz), 1)
                    dve.wait_ge(*B.emptied(kz))
                    dve.wait_ge(*B.filled(ks))
                    v.tensor_tensor(W1h[:, c, :], W1f[:], B.tensor(ks)[:], ALU.mult).then_inc(B.empties(ks), 1)
                    dve.wait_ge(*B.emptied(ks))
                    v.tensor_copy(W1[:, c, :], W1h[:, c, :]).then_inc(deq_done.sem, 1)

            def hidden(l, n, chunks):
                for j in range(chunks):
                    e = n * chunks + j
                    key = ("up", l, n, j)
                    dve.wait_ge(*B.emptied(("gate", l, n, j)))
                    dve.wait_ge(*B.filled(key))
                    if n == 1 and j == 0:
                        dve.wait_ge(*B.filled(("out", l, 3) if l != 3 else ("low2", 0)))
                    ps, h = B.tensor(key)[:], hT[:, j, :]
                    if l == 0:
                        ins = v.scalar_tensor_tensor(h, ps, tscale[:, 1:2], silu[e % 2][:], ALU.mult, ALU.mult)
                    elif l == 3:
                        ins = v.scalar_tensor_tensor(h, ps, b1[:, 1, j:j + 1], silu[e % 2][:], ALU.add, ALU.mult)
                    else:
                        ins = v.tensor_tensor(h, ps, silu[e % 2][:], ALU.mult)
                    ins.then_inc(B.empties(key), 1)

            def ffn(l):
                if l == 1:
                    return
                for n in range(2):
                    hidden(l, n, {0: HC0, 2: HC2, 3: HC3}[l])
                    if l == 3:
                        for t in range(4 * n, 4 * n + 4):
                            key = ("out", l, t)
                            dve.wait_ge(*B.filled(key))
                            if t >= 2:
                                dve.wait_ge(*gate_ready.at(3, t - 1))
                            v.tensor_tensor(outb[t % 2][:], B.tensor(key)[:], b2[:], ALU.add).then_inc(B.empties(key), 1)

            def rope(l, u, tau):
                i = 2 * u + tau
                dve.wait_ge(*B.emptied(("qkv", l, u, tau)))
                if i >= 2:
                    dve.wait_ge(*rope_done.at(l, i - 1))
                src, tc, ts = qk[i % 2], rc[i % 2], rs[i % 2]
                half = HD // 2
                v.tensor_tensor(tc[:], src[:, 0:20, :], cosT[l][:, tau, :].unsqueeze(1).to_broadcast([P, 20, HD]),
                                ALU.mult).then_inc(rope_part.sem, 1)
                v.tensor_tensor(ts[:, :, 0:half], src[:, 0:20, half:HD],
                                sinT[l][:, tau, 0:half].unsqueeze(1).to_broadcast([P, 20, half]), ALU.mult).then_inc(rope_part.sem, 1)
                v.tensor_tensor(ts[:, :, half:HD], src[:, 0:20, 0:half],
                                sinT[l][:, tau, half:HD].unsqueeze(1).to_broadcast([P, 20, half]), ALU.mult).then_inc(rope_part.sem, 1)
                dve.wait_ge(*rope_part.at(l, 3 * (i + 1)))
                if i >= 2:
                    dve.wait_ge(*stack_hi.at(l, hi_ops[l] * (i - 1)))
                    dve.wait_ge(*stack_lo.at(l, 2 * (i - 1)))
                v.tensor_tensor(qkr[i % 2][:], tc[:], ts[:], ALU.add).then_inc(rope_done.sem, 1)

            def row_max(l, u, g):
                for qb in range(2):
                    nk = (qb + 1) * P if CAUSAL[l] else SEQ
                    for par in range(2):
                        key = ("S", l, u, g, qb, par)
                        dve.wait_ge(*B.filled(key))
                        v.tensor_reduce(negmax[u % 2][:, qb, par * 8 + 2 * g:par * 8 + 2 * g + 2],
                                        B.tensor(key)[:, 0:2 * nk].rearrange("p (h k) -> p h k", h=2),
                                        AX.X, ALU.max, negate=True).then_inc(B.empties(key), 1)

            def take_max(l, u):
                key = ("mT", l, u)
                dve.wait_ge(*B.filled(key))
                v.tensor_copy(negmaxT[u % 2][:], B.tensor(key)[0:UH, 0:SEQ]).then_inc(B.empties(key), 1)

            def context(l, gi):
                u, g = gi // GROUPS, gi % GROUPS
                b, hh = u // 2, u % 2
                key = ("ctx", l, gi)
                dve.wait_ge(*B.filled(key))
                ps = B.tensor(key)[:, 0:2 * P].rearrange("p (q i r) -> p q i r", q=2, i=4)
                if gi >= 2:
                    dve.wait_ge(*B.emptied(("ctx", l, gi - 2)))
                v.reciprocal(recip[gi % 2][:], ps[:, :, :, HD]).then_inc(rs_ready.sem, 1)
                dve.wait_ge(*rs_ready.at(l, gi + 1))
                c0 = (UH * hh + 4 * g) * HD
                v.tensor_tensor(ctxr[b % 2][:, :, c0:c0 + 4 * HD].rearrange("p q (i d) -> p q i d", i=4), ps[:, :, :, 0:HD],
                                recip[gi % 2][:].unsqueeze(3).to_broadcast([P, 2, 4, HD]), ALU.mult).then_inc(B.empties(key), 1)

            def residual(l, b):
                for tau in range(2):
                    t = 2 * b + tau
                    key = ("O", l, b, tau)
                    dve.wait_ge(*B.filled(key))
                    if t >= 2:
                        dve.wait_ge(*x_done.at(l, t - 1))
                    v.tensor_tensor(gated[tau][:], B.tensor(key)[:], gate[:, t, :], ALU.mult).then_inc(B.empties(key), 1)
                    dve.wait_ge(*B.emptied(key))
                    v.tensor_tensor(x[:, t, :], x[:, t, :], gated[tau][:], ALU.add).then_inc(x_done.sem, 1)

            def attention(l):
                dve.wait_ge(*(B.emptied(last_out[l]) if l != 3 else gate_ready.at(3, TILES)))
                for u in range(2):
                    for tau in range(2):
                        if ROPE[l]:
                            rope(l, u, tau)
                for g in range(GROUPS):
                    row_max(l, 0, g)
                take_max(l, 0)
                for u in range(UNITS):
                    for g in range(GROUPS):
                        gi = GROUPS * u + g
                        if g < 2 and u + 2 < UNITS and ROPE[l]:
                            rope(l, u + 2, g)
                        if u + 1 < UNITS:
                            row_max(l, u + 1, g)
                        if gi >= 2:
                            context(l, gi - 2)
                        if u % 2 == 0 and u > 0 and g == 3:
                            residual(l, u // 2 - 1)
                    if u + 1 < UNITS:
                        take_max(l, u + 1)
                context(l, 30)
                context(l, 31)
                residual(l, SEQS - 1)

            v.memset(ones[:], 1.0).then_inc(ones_set.sem, 1)
            v.memset(minus_half[:], -0.5).then_inc(ones_set.sem, 1)
            for l in range(LAYERS):
                normalise(l)
                if l == 0:
                    dve.wait_ge(const_in, 16 * CONSTS)
                    v.tensor_copy(identb[:], ident[:]).then_inc(mask_set.sem, 1)
                    v.tensor_copy(mask[:], maskf[:]).then_inc(mask_set.sem, 1)
                    ternary()
                if l == 1:
                    dequantise()
                ffn(l)
                attention(l)

        @block.gpsimd
        def _(pool):
            gp = nc.gpsimd

            def inverse_deviation(l):
                for b in range(SEQS):
                    pool.wait_ge(*ln_var.at(l, b + 1))
                    gp.tensor_tensor(rstd[:, 2 * b:2 * b + 2], vareps[:, 2 * b:2 * b + 2], minus_half[:, 0:2],
                                     ALU.pow).then_inc(ln_rstd.sem, 1)

            def scale_weights():
                for j in range(HC2):
                    pool.wait_ge(w2_in[j], 48)
                    if j == 0:
                        pool.wait_ge(ffn_in[2], 16 + 48)
                    for m in range(2):
                        w = W2gu[m][:, j, :, :]
                        gp.tensor_tensor(w, w, s2[m][:, j, :].unsqueeze(2).to_broadcast([P, KC, P]),
                                         ALU.mult).then_inc(w_scaled.sem, 1)
                    w = W2d[:, j, :].rearrange("p (n o) -> p n o", n=KC)
                    gp.tensor_tensor(w, w, s2[2][:, j, :].unsqueeze(2).to_broadcast([P, KC, P]),
                                     ALU.mult).then_inc(w_scaled.sem, 1)

            def set_pads(l):
                pool.wait_ge(*(B.emptied(last_out[l]) if l != 3 else gate_ready.at(3, TILES)))
                for i in range(2):
                    gp.memset(qstack[i][:, :, STACK:64], 0.0).then_inc(pads.sem, 1)
                    gp.memset(kstack[i][:, :, STACK:STACK + 1], 1.0).then_inc(pads.sem, 1)
                    gp.memset(kstack[i][:, :, STACK + 1:64], 0.0).then_inc(pads.sem, 1)
                for i in range(4):
                    gp.memset(V[i][:, :, :, HD:HD + 1], 1.0).then_inc(pads.sem, 1)
                    gp.memset(V[i][:, :, :, HD + 1:32], 0.0).then_inc(pads.sem, 1)

            def stack_low(l, u, tau):
                i = 2 * u + tau
                pool.wait_ge(*stack_hi.at(l, hi_ops[l] * (i + 1)))
                src = qkr[i % 2] if ROPE[l] else qk[i % 2]
                qs, ks = qstack[i % 2], kstack[i % 2]
                gp.tensor_tensor(qs[:].bitcast(F32R)[:, :, 16:32], src[:, 0:UH, :], qs[:, :, 0:16],
                                 ALU.subtract).then_inc(stack_lo.sem, 1)
                if GQA[l]:
                    kd = ks[:, 0:8, :].rearrange("p (g c) s -> p g c s", c=2)
                    kr = ks[:].bitcast(F32R)[:, 0:8, :].rearrange("p (g c) s -> p g c s", c=2)
                    gp.tensor_tensor(kr[:, :, :, 32:48], src[:, UH:UH + 4, :].unsqueeze(2).to_broadcast([P, 4, 2, HD]),
                                     kd[:, :, :, 0:16], ALU.subtract).then_inc(stack_lo.sem, 1)
                else:
                    gp.tensor_tensor(ks[:].bitcast(F32R)[:, :, 32:48], src[:, UH:2 * UH, :], ks[:, :, 0:16],
                                     ALU.subtract).then_inc(stack_lo.sem, 1)

            def cut_future(l, u, g):
                gi = GROUPS * u + g
                for kb in range(2):
                    pool.wait_ge(*B.emptied(("ST", l, u, g, kb, 1)))
                    blk = probs[gi % 2][:, kb, :, kb * P:(kb + 1) * P]
                    gp.affine_select(out=blk, in_=blk, compare_op=ALU.is_ge, fill=0.0, base=0,
                                     pattern=[[0, 4], [1, P]], channel_multiplier=-1).then_inc(causal_cut.sem, 1)

            pool.wait_ge(*ones_set.at(0, 2))
            for l in range(LAYERS):
                inverse_deviation(l)
                if l == 2:
                    scale_weights()
                set_pads(l)
                for u in range(2):
                    for tau in range(2):
                        stack_low(l, u, tau)
                for u in range(UNITS):
                    for g in range(GROUPS):
                        if CAUSAL[l]:
                            cut_future(l, u, g)
                        if g < 2 and u + 2 < UNITS:
                            stack_low(l, u + 2, g)

        @block.sync
        def _(sp):
            xv = a["x"].rearrange("(t p) d -> p t d", p=P)

            def load(dst, src, s):
                sp.dma_start(dst, src).then_inc(s, 16)

            for b in range(SEQS):
                load(x[:, 2 * b:2 * b + 2, :], xv[:, 2 * b:2 * b + 2, :], x_in[b])
            n = 0
            for dst, name in [(ident, "ident"), (maskf, "mask"), (sign_in, "sign_in"), (sign_hid, "sign_hid")] + \
                    [(cosT[l], f"cos{l}") for l in (0, 2, 3)] + [(sinT[l], f"sin{l}") for l in (0, 2, 3)]:
                load(dst[:], a[name], const_in)
                n += 1
            assert n == CONSTS

            def load_attention(l):
                if GQA[l]:
                    load(Wqkv[:, :, :, 0:384], a[f"Wqkv{l}"], att_in)
                else:
                    load(Wqkv[:], a[f"Wqkv{l}"], att_in)
                load(Wo[:], a[f"Wo{l}"], att_in)

            load(Wgu0[0][:], a["Wg0"], ffn_in[0])
            load(Wgu0[1][:], a["Wu0"], ffn_in[1])
            load(Wd0[:], a["Wd0"], ffn_in[2])
            for l in range(LAYERS):
                if l > 0:
                    sp.wait_ge(*x_done.at(l - 1, TILES))
                if l == 1:
                    for dst, name in [(W1q, "qweight"), (zq, "qzeros"), (sh, "scales"), (gidx, "g_idx"), (four, "four"),
                                      (bias1, "bias1")]:
                        load(dst[:], a[name], ffn_in[0])
                if l == 2:
                    for i, name in enumerate(("w1s", "w3s", "w2s")):
                        load(s2[i][:], a[name], ffn_in[2])
                    for j in range(HC2):
                        load(W2gu[0][:, j], a["w1"][:, j], w2_in[j])
                        load(W2gu[1][:, j], a["w3"][:, j], w2_in[j])
                        load(W2d[:, j], a["w2"][:, j], w2_in[j])
                if l == 3:
                    for dst, name in [(U1, "U1"), (V1, "V1"), (U2, "U2"), (V2, "V2"), (b1, "b1"), (b2, "b2")]:
                        load(dst[:], a[name], ffn_in[0])
                load_attention(l)
                for u in range(UNITS):
                    sp.wait_ge(*B.emptied(("mT", l, u)))
                    for par in range(2):
                        r = 64 * par + STACK
                        load(qT[u % 2][r:r + 1, :, :].bitcast(F32), negmaxT[u % 2][8 * par:8 * par + 8, :].bitcast(F32), m_rows[u % 2])
            ov = out.rearrange("(t p) d -> p t d", p=P)
            for t in range(TILES):
                sp.wait_ge(*x_done.at(LAYERS - 1, t + 1))
                sp.dma_start(ov[:, t:t + 1, :], x[:, t:t + 1, :]).then_inc(out_done, 16)
            sp.wait_ge(out_done, 16 * TILES)


CONSTS = 10
LOADS = {1: 6, 3: 1 + 6 + 6}


def layouts(inputs):
    g = {k: np.asarray(v) for k, v in inputs.items()}
    o = {"x": g["L0_attn_hidden_states"].reshape(SEQS * SEQ, D)}
    eye = np.eye(P, dtype=np.float32)
    o["ident"] = eye
    future = np.where(np.arange(P)[None, :] > np.arange(P)[:, None], np.float32(NEG), np.float32(0))
    o["mask"] = np.concatenate([future, future], axis=1)
    which, sign = octonion_table()
    i_of = np.arange(D) // 64
    o["sign_in"] = np.ascontiguousarray(sign[i_of].reshape(KC, P, OCT).transpose(1, 0, 2))
    hid = np.minimum(np.arange(HC0 * P) // 170, 7)
    o["sign_hid"] = np.ascontiguousarray(sign[hid].reshape(HC0, P, OCT).transpose(1, 0, 2))
    for l in (0, 2, 3):
        inv = (1.0 / np.float32(ROPE_BASE[l]) ** (np.arange(0, HD, 2, dtype=np.float32) / HD)).astype(np.float32)
        ang = (np.arange(SEQ, dtype=np.float32)[:, None] * inv[None, :]).astype(np.float32)
        c, s = np.cos(ang), np.sin(ang)
        o[f"cos{l}"] = np.ascontiguousarray(np.concatenate([c, c], 1).reshape(2, P, HD).transpose(1, 0, 2)).astype(np.float32)
        o[f"sin{l}"] = np.ascontiguousarray(np.concatenate([-s, s], 1).reshape(2, P, HD).transpose(1, 0, 2)).astype(np.float32)

    shift_order = np.arange(D).reshape(64, 8).T.reshape(-1)
    halves = np.concatenate([np.arange(0, HD, 2), np.arange(1, HD, 2)])
    for l in range(LAYERS):
        wq, wk, wv, wo = (g[f"L{l}_attn_{n}"] for n in ("Wq", "Wk", "Wv", "Wo"))
        if l < 2:
            wq, wk, wv, wo = wq.T, wk.T, wv.T, wo.T
        if l == 1:
            wq, wk, wv = wq[shift_order], wk[shift_order], wv[shift_order]
        q = wq.reshape(D, 2, UH, HD)
        k = wk.reshape(D, 2, -1, HD)
        if l == 0:
            q, k = q[..., halves], k[..., halves]
        v = wv.reshape(D, 2, -1, HD)
        w = np.concatenate([y.reshape(D, 2, -1) for y in (q, k, v)], axis=2)
        o[f"Wqkv{l}"] = np.ascontiguousarray(w.reshape(KC, P, 2, -1).transpose(1, 0, 2, 3))
        o[f"Wo{l}"] = np.ascontiguousarray(wo.reshape(KC, P, D).transpose(1, 0, 2))

    for name, key in (("Wg0", "w_gate"), ("Wu0", "w_up")):
        w = g[f"L0_ffn_{key}"][which]
        w = w.transpose(0, 3, 1, 2).reshape(D, HID0)
        pad = np.zeros((D, HC0 * P), np.float32)
        pad[:, :HID0] = w
        o[name] = np.ascontiguousarray(pad.reshape(KC, P, HC0 * P).transpose(1, 0, 2))
    w = g["L0_ffn_w_down"][which].transpose(0, 3, 1, 2).reshape(HID0, D)
    pad = np.zeros((HC0 * P, D), np.float32)
    pad[:HID0] = w
    o["Wd0"] = np.ascontiguousarray(pad.reshape(HC0, P, D).transpose(1, 0, 2))

    qw = g["L1_ffn_qweight"]
    o["qweight"] = np.ascontiguousarray(np.repeat(np.concatenate([qw, qw])[:, None], KC, axis=1))
    o["qzeros"] = np.ascontiguousarray(g["L1_ffn_qzeros"])
    o["scales"] = np.ascontiguousarray(g["L1_ffn_scales"])
    o["g_idx"] = np.ascontiguousarray(np.repeat(g["L1_ffn_g_idx"][shift_order][None], 4, axis=0))
    o["four"] = np.arange(4, dtype=np.float32).reshape(4, 1)
    o["bias1"] = g["L1_ffn_bias"].reshape(1, D)

    for name in ("w1", "w3"):
        w = g[f"L2_ffn_{name}"]
        o[name] = np.ascontiguousarray(w.reshape(HC2, P, KC, P).transpose(3, 0, 2, 1))
        o[name + "s"] = np.ascontiguousarray(np.repeat(g[f"L2_ffn_{name}_scale"][None], P, axis=0))
    w = g["L2_ffn_w2"]
    o["w2"] = np.ascontiguousarray(w.T.reshape(HC2, P, D).transpose(1, 0, 2))
    o["w2s"] = np.ascontiguousarray(np.repeat(g["L2_ffn_w2_scale"].T[None], P, axis=0))

    o["U1"] = np.ascontiguousarray(g["L3_ffn_U1"].reshape(KC, P, P).transpose(1, 0, 2))
    v1 = np.zeros((P, 2, HC3 * P), np.float32)
    v1[:, :, :INTER3] = g["L3_ffn_V1"].reshape(P, 2, INTER3)
    o["V1"] = v1.reshape(P, 2, HC3, P)
    u2 = np.zeros((HC3 * P, P), np.float32)
    u2[:INTER3] = g["L3_ffn_U2"]
    o["U2"] = np.ascontiguousarray(u2.reshape(HC3, P, P).transpose(1, 0, 2))
    o["V2"] = g["L3_ffn_V2"]
    bb = np.zeros((2, HC3 * P), np.float32)
    bb[:, :INTER3] = g["L3_ffn_b1"].reshape(2, INTER3)
    o["b1"] = np.ascontiguousarray(bb.reshape(2, HC3, P).transpose(2, 0, 1))
    o["b2"] = np.ascontiguousarray(np.repeat(g["L3_ffn_b2"][None], P, axis=0))
    return o


def kernel(**inputs):
    import concourse.bacc as _bacc
    from concourse import mybir as _mybir
    from concourse.bass_utils import run_bass_kernel_spmd as _run

    nc = _bacc.Bacc("TRN2", target_bir_lowering=False, num_devices=1)
    arrays, aps = {}, {}
    for name, arr in layouts(inputs).items():
        arrays[f"in_{name}"] = arr
        aps[name] = nc.dram_tensor(f"in_{name}", arr.shape, _mybir.dt.from_np(arr.dtype), kind="ExternalInput").ap()
    out = nc.dram_tensor("out_0", (SEQS, SEQ, D), _mybir.dt.float32, kind="ExternalOutput").ap()
    program(nc, aps, out.rearrange("b s d -> (b s) d"))
    r = _run(nc, [arrays], core_ids=[0])
    return r.results[0]["out_0"]
```

```python
from contextlib import ExitStack

import concourse.bass as bass
import numpy as np
from concourse import mybir

F32 = mybir.dt.float32
F32R = mybir.dt.float32r
BF16 = mybir.dt.bfloat16
F16 = mybir.dt.float16
I32 = mybir.dt.int32
ALU = mybir.AluOpType
ACT = mybir.ActivationFunctionType
AX = mybir.AxisListType

P = 128
D = 512
KC = D // P
SEQS, SEQ = 4, 256
TILES = SEQS * SEQ // P
HEADS, HD = 32, 16
UNITS = 2 * SEQS
UH = 16
GROUPS = UH // 4
LAYERS = 4
GQA = [True, False, True, True]
CAUSAL = [True, False, True, True]
ROPE = [True, False, True, True]
ROPE_BASE = {0: 10000.0, 2: 500000.0, 3: 10000.0}
EPS = 1e-5
SPLIT = 16
STACK = 3 * SPLIT
CELL = HD + 4
NEG = -1.0e30
ROUND = 1.5 * 2.0 ** 23
HID0, HC0 = 1360, 11
HC2 = 14
HC3 = 11
INTER3 = 1376
OCT = 8


def octonion_table():
    s = np.zeros((8, 8, 8), np.float32)
    s[0, 0, 0] = 1.0
    for i in range(1, 8):
        s[0, i, i] = 1.0
        s[i, 0, i] = 1.0
        s[i, i, 0] = -1.0
    for a, b, c in [(1, 2, 3), (1, 4, 5), (1, 7, 6), (2, 4, 6), (2, 5, 7), (3, 4, 7), (3, 6, 5)]:
        for x, y, z in ((a, b, c), (b, c, a), (c, a, b)):
            s[x, y, z] = 1.0
            s[y, x, z] = -1.0
    which = np.abs(s).argmax(axis=0)
    sign = np.take_along_axis(s, which[None], axis=0)[0]
    return which, sign


class Mark:

    def __init__(self, nc, ctx, name, per_layer):
        self.sem = ctx.enter_context(nc.semaphore(name))
        self.per_layer = per_layer

    def at(self, layer, n):
        return self.sem, sum(self.per_layer[:layer]) + n


class Banks:

    def __init__(self, nc, ctx):
        self.ps = [ctx.enter_context(nc.psum_tensor(f"bank{i}", [P, 512], F32)) for i in range(8)]
        self.full = [ctx.enter_context(nc.semaphore(f"bank{i}_filled")) for i in range(8)]
        self.free = [ctx.enter_context(nc.semaphore(f"bank{i}_emptied")) for i in range(8)]
        self.uses = [0] * 8
        self.where = {}

    def claim(self, key, bank):
        self.where[key] = (bank, self.uses[bank])
        self.uses[bank] += 1
        return self.ps[bank], self.uses[bank] > 1

    def before(self, key):
        bank, n = self.where[key]
        return self.free[bank], n

    def tensor(self, key):
        return self.ps[self.where[key][0]]

    def filled(self, key):
        bank, n = self.where[key]
        return self.full[bank], n + 1

    def emptied(self, key):
        bank, n = self.where[key]
        return self.free[bank], n + 1

    def fills(self, key):
        return self.full[self.where[key][0]]

    def empties(self, key):
        return self.free[self.where[key][0]]


def program(nc, a, out):
    ctx = ExitStack()
    with ctx:
        def sem(name):
            return ctx.enter_context(nc.semaphore(name))

        base = 16512
        top = [base]
        names = {}

        def place(name, shape, dt, at=None):
            size = 2 if dt in (BF16, F16) else 4
            n = size
            for s in shape[1:]:
                n *= s
            n = (n + 31) // 32 * 32
            off = top[0] if at is None else at[0]
            t = nc.alloc_sbuf_tensor_at(name, shape, dt, offset=off)
            if at is None:
                top[0] += n
            else:
                at[0] += n
            names[name] = (off, n)
            return t

        x = place("x", [P, TILES, D], F32)
        xT = place("xT", [P, KC, TILES * P], F32)
        gate = place("gate", [P, TILES, D], F32)
        xn = [nc.alloc_sbuf_tensor_at(f"xn{i}", [P, D], F32, offset=names["gate"][0] + (4 + i) * D * 4) for i in range(4)]
        ident = place("ident", [P, P], F32)
        identb = place("identb", [P, P], BF16)
        mask = place("mask", [P, 2 * P], BF16)
        cosT = {l: place(f"cos{l}", [P, 2, HD], F32) for l in (0, 2, 3)}
        sinT = {l: place(f"sin{l}", [P, 2, HD], F32) for l in (0, 2, 3)}
        ones = place("ones", [P, P], F32)
        stats = place("stats", [P, TILES, 6], F32)
        moments = place("moments", [P, TILES, 2], F32)
        vareps = place("vareps", [P, TILES], F32)
        minus_half = place("minus_half", [P, TILES], F32)
        rstd = place("rstd", [P, TILES], F32)
        Wqkv = place("Wqkv", [P, KC, 2, 768], F32)
        Wo = place("Wo", [P, KC, D], F32)
        shared = top[0]

        at = [shared]
        qT = [place(f"qT{i}", [P, UH // 2, SEQ], F32R, at) for i in range(2)]
        kT = [place(f"kT{i}", [P, UH, SEQ], F32R, at) for i in range(2)]
        qstack = [place(f"qstack{i}", [P, UH, 64], F32, at) for i in range(2)]
        kstack = [place(f"kstack{i}", [P, UH // 2, 4, 64], F32, at) for i in range(2)]
        qk = [place(f"qk{i}", [P, 2 * UH, HD], F32, at) for i in range(2)]
        rc = [place(f"rope_cos{i}", [P, 20, HD], F32, at) for i in range(2)]
        rs = [place(f"rope_sin{i}", [P, 20, HD], F32, at) for i in range(2)]
        qkr = rc
        Vflat = [place(f"V{i}", [P, 2 * UH * CELL + 32 - CELL], F32, at) for i in range(4)]
        V = [vf[:, 0:2 * UH * CELL].rearrange("p (t h c) -> p t h c", t=2, h=UH) for vf in Vflat]
        probs = [place(f"probs{i}", [P, 2, 4, SEQ], F32, at) for i in range(2)]
        pv = [place(f"pv{i}", [P, SEQ], F32, at) for i in range(2)]
        ctxr = [place(f"ctx{i}", [P, 2, D], F32, at) for i in range(2)]
        ctxT = [place(f"ctxT{i}", [P, KC, P], F32, at) for i in range(2)]
        negmax = [place(f"negmax{i}", [P, 2, UH], F32, at) for i in range(2)]
        negmaxT = [place(f"negmaxT{i}", [UH, SEQ], F32R, at) for i in range(2)]
        recip = [place(f"recip{i}", [P, 2, 4], F32, at) for i in range(2)]
        assert at[0] <= 229344, at[0]

        at = [shared]
        hT = place("hT", [P, HC2, 512], F32, at)
        silu = [place(f"silu{i}", [P, 512], F32, at) for i in range(2)]
        weights_from = at[0]
        Wgu0 = [place(f"W{n}0", [P, KC, HC0 * P], F32, at) for n in ("gate", "up")]
        Wd0 = place("Wdown0", [P, HC0, D], F32, at)
        sign_in = place("sign_in", [P, KC, OCT], F32, at)
        sign_hid = place("sign_hid", [P, HC0, OCT], F32, at)
        maskf = place("maskf", [P, 2 * P], F32, at)
        absum = place("absum", [P, 3], F32, at)
        tscale = place("tscale", [P, 3], F32, at)
        tinv = place("tinv", [P, 3], F32, at)
        assert at[0] <= 229344, at[0]
        at = [weights_from]
        W1q = place("W1q", [P, KC, D], I32, at)
        W1n = place("W1n", [P, KC, D], I32, at)
        W1f = place("W1f", [P, D], F32, at)
        W1h = place("W1h", [P, KC, D], F16, at)
        W1 = place("W1", [P, KC, D], F32, at)
        zq = place("zq", [4, 64], I32, at)
        zn = place("zn", [4, 64, 8], I32, at)
        zf = place("zf", [4, D], F32, at)
        sh = place("sh", [4, D], F16, at)
        sf = place("sf", [4, D], F32, at)
        gidx = place("gidx", [4, D], I32, at)
        onehot = place("onehot", [4, D], F32, at)
        four = place("four", [4, 1], F32, at)
        bias1 = place("bias1", [1, D], F16, at)
        ones16 = place("ones16", [1, P], F16, at)
        zr = place("zr", [P, D], F32, at)
        at = [weights_from]
        W2gu = [place(f"W{n}2", [P, HC2, KC, P], F32, at) for n in ("gate", "up")]
        W2d = place("Wdown2", [P, HC2, D], F32, at)
        s2 = [place(f"wscale{i}", [P, HC2, KC], F32, at) for i in range(3)]
        assert at[0] <= 229344, at[0]
        at = [weights_from]
        U1 = place("U1", [P, KC, P], F32, at)
        V1 = place("V1", [P, 2, HC3, P], F32, at)
        U2 = place("U2", [P, HC3, P], F32, at)
        V2 = place("V2", [P, D], F32, at)
        b1 = place("b1", [P, 2, HC3], F32, at)
        b2 = place("b2", [P, D], F32, at)
        PT = place("PT", [P, 2, 512], F32, at)
        ZT = place("ZT", [P, 2, 512], F32, at)
        outb = [place(f"outb{i}", [P, D], F32, at) for i in range(2)]

        B = Banks(nc, ctx)
        x_in = [sem(f"x_loaded{i}") for i in range(SEQS)]
        const_in = sem("constants_loaded")
        att_in = sem("attention_weights_loaded")
        ffn_in = [sem(f"ffn_weights_loaded{i}") for i in range(3)]
        w2_in = [sem(f"ffn2_chunk_loaded{i}") for i in range(HC2)]
        m_rows = [sem(f"max_rows_placed{i}") for i in range(2)]
        out_done = sem("output_stored")

        def mark(name, per_layer):
            return Mark(nc, ctx, name, per_layer)

        ones_set = mark("ones_set", [2, 0, 0, 0])
        mask_set = mark("mask_set", [2, 0, 0, 0])
        ln_stat = mark("row_stats", [TILES] * 4)
        ln_mom = mark("row_moments", [TILES] * 4)
        ln_var = mark("row_variance", [SEQS] * 4)
        ln_rstd = mark("row_rstd", [SEQS] * 4)
        xn_ready = mark("rows_normalised", [TILES] * 4)
        tern = mark("ternary_steps", [100, 0, 0, 0])
        deq = mark("dequant_steps", [0, 100, 0, 0])
        deq_done = mark("dequantised", [0, KC, 0, 0])
        w_scaled = mark("weights_scaled", [0, 0, 3 * HC2, 0])
        gate_ready = mark("gate_ready", [0, 0, 0, TILES])
        rope_part = mark("rope_parts", [48, 0, 48, 48])
        rope_done = mark("rope_done", [16, 0, 16, 16])
        HI = 3
        stack_hi = mark("stack_hi", [16 * HI] * 4)
        stack_lo = mark("stack_lo", [32] * 4)
        PADS = [2 * 4 + 4 * (4 if shared_keys else 3) for shared_keys in GQA]
        pads = mark("pads_set", PADS)
        causal_cut = mark("causal_cut", [64, 0, 64, 64])
        rs_ready = mark("reciprocal_ready", [32] * 4)
        x_done = mark("x_updated", [TILES] * 4)

        last_out = {l: ("out", l, TILES - 1) for l in range(LAYERS)}

        def stack_banks(l, half):
            return [("qT", half)] + ([("kT", half)] if GQA[l] else [("kT", 2 * half), ("kT", 2 * half + 1)])

        def key_slot(l, g, pair, par):
            return 2 * (g if GQA[l] else pair) + par

        block = ctx.enter_context(nc.Block())

        @block.tensor
        def _(pe):
            misc = [0]
            ring_s = [0]
            ring_t = [0]
            mm = nc.tensor.matmul

            def misc_bank():
                misc[0] += 1
                return 4 + misc[0] % 4

            def transposes(l):
                for t in range(TILES):
                    key = ("xT", l, t)
                    ps, again = B.claim(key, 4 + t % 4)
                    if again:
                        pe.wait_ge(*B.before(key))
                    pe.wait_ge(*xn_ready.at(l, t + 1))
                    for c in range(KC):
                        ins = nc.tensor.transpose(ps[:, c * P:(c + 1) * P], xn[t % 4][:, c * P:(c + 1) * P], ident[:])
                    ins.then_inc(B.fills(key), 1)

            def hidden(l, n, chunks, wait_weights, lhs, rhs):
                for j in range(chunks):
                    slot = (n * chunks + j) % 2
                    for which in range(2):
                        key = (("gate", "up")[which], l, n, j)
                        ps, again = B.claim(key, 2 * slot + which)
                        if again:
                            pe.wait_ge(*B.before(key))
                        if n == 0:
                            wait_weights(j, which)
                        terms = rhs(n)
                        for c, r in enumerate(terms):
                            ins = mm(ps[:], lhs(which, c, j), r, start=(c == 0), stop=(c == len(terms) - 1))
                        ins.then_inc(B.fills(key), 1)

            def out_tile(l, t, terms):
                key = ("out", l, t)
                ps, again = B.claim(key, 4 + t % 4)
                if again:
                    pe.wait_ge(*B.before(key))
                for c, (lh, rh) in enumerate(terms):
                    ins = mm(ps[:], lh, rh, start=(c == 0), stop=(c == len(terms) - 1))
                ins.then_inc(B.fills(key), 1)

            def x_terms(n):
                return [xT[:, c, n * 512:(n + 1) * 512] for c in range(KC)]

            def ffn(l):
                if l == 0:
                    pe.wait_ge(*ones_set.at(0, 2))
                    for m in range(3):
                        key = ("wsum", m)
                        ps, again = B.claim(key, m)
                        pe.wait_ge(*tern.at(0, 5 * m + 1))
                        mm(ps[:, 0:1], ones[:], absum[:, m:m + 1], start=True, stop=True).then_inc(B.fills(key), 1)
                if l == 1:
                    pe.wait_ge(*deq.at(1, 12))
                    for c in range(KC):
                        for which, src in ((0, zf), (1, sf)):
                            key = ("group", c, which)
                            ps, again = B.claim(key, (2 * c + which) % 4)
                            if again:
                                pe.wait_ge(*B.before(key))
                            mm(ps[:], onehot[:, c * P:(c + 1) * P], src[:], start=True, stop=True).then_inc(B.fills(key), 1)
                if l == 3:
                    pe.wait_ge(ffn_in[0], 16 * LOADS[3])
                for n in range(2):
                    pe.wait_ge(*B.emptied(("xT", l, 4 * n + 3)))
                    if l in (0, 2):
                        chunks = HC0 if l == 0 else HC2

                        def wait_weights(j, which):
                            if l == 0 and j == 0:
                                pe.wait_ge(*tern.at(0, 5 * (which + 1)))
                            if l == 2:
                                pe.wait_ge(*w_scaled.at(2, 3 * j + which + 1))

                        def lhs(which, c, j):
                            if l == 0:
                                return Wgu0[which][:, c, j * P:(j + 1) * P]
                            return W2gu[which][:, j, c, :]

                        hidden(l, n, chunks, wait_weights, lhs, x_terms)
                        pe.wait_ge(*B.emptied(("up", l, n, chunks - 1)))
                        if l == 0:
                            pe.wait_ge(*tern.at(0, 15))
                        else:
                            pe.wait_ge(*w_scaled.at(2, 3 * HC2))
                        Wd = Wd0 if l == 0 else W2d
                        for t in range(4 * n, 4 * n + 4):
                            out_tile(l, t, [(hT[:, c, (t % 4) * P:(t % 4 + 1) * P], Wd[:, c, :]) for c in range(chunks)])
                    if l == 1:
                        pe.wait_ge(*deq_done.at(1, KC))
                        for t in range(4 * n, 4 * n + 4):
                            out_tile(l, t, [(xT[:, c, t * P:(t + 1) * P], W1[:, c, :]) for c in range(KC)]
                                     + [(ones16[:], bias1[:])])
                    if l == 3:
                        key = ("low", n)
                        ps, again = B.claim(key, n)
                        if again:
                            pe.wait_ge(*B.before(key))
                        for c, r in enumerate(x_terms(n)):
                            ins = mm(ps[:], U1[:, c, :], r, start=(c == 0), stop=(c == KC - 1))
                        ins.then_inc(B.fills(key), 1)
                        pe.wait_ge(*B.emptied(key))
                        hidden(l, n, HC3, lambda j, which: None, lambda which, c, j: V1[:, which, j, :],
                               lambda n: [PT[:, n, :]])
                        pe.wait_ge(*B.emptied(("up", l, n, HC3 - 1)))
                        key = ("low2", n)
                        ps, again = B.claim(key, n)
                        pe.wait_ge(*B.before(key))
                        for c in range(HC3):
                            ins = mm(ps[:], U2[:, c, :], hT[:, c, :], start=(c == 0), stop=(c == HC3 - 1))
                        ins.then_inc(B.fills(key), 1)
                        pe.wait_ge(*B.emptied(key))
                        for t in range(4 * n, 4 * n + 4):
                            out_tile(l, t, [(ZT[:, n, (t % 4) * P:(t % 4 + 1) * P], V2[:])])

            def project(l, u, tau):
                t, hh = 2 * (u // 2) + tau, u % 2
                if u == 0 and tau == 0:
                    pe.wait_ge(att_in, 32 * (l + 1))
                    pe.wait_ge(*mask_set.at(0, 2))
                for key, c0, width in ([(("qkv", l, u, tau), 0, 384)] if GQA[l] else
                                       [(("qkv", l, u, tau), 0, 512), (("v", l, u, tau), 512, 256)]):
                    ps, again = B.claim(key, misc_bank())
                    pe.wait_ge(*B.before(key))
                    for c in range(KC):
                        ins = mm(ps[:, 0:width], xT[:, c, t * P:(t + 1) * P], Wqkv[:, c, hh, c0:c0 + width],
                                 start=(c == 0), stop=(c == KC - 1))
                    ins.then_inc(B.fills(key), 1)

            def turn_stacks(l, u, tau, half):
                i = 2 * u + tau
                if half == 0:
                    pe.wait_ge(*pads.at(l, PADS[l]))
                    pe.wait_ge(*stack_hi.at(l, HI * (i + 1)))
                    pe.wait_ge(*stack_lo.at(l, 2 * (i + 1)))
                for name, w in stack_banks(l, half):
                    flat = qstack[i % 2][:].rearrange("p h s -> p (h s)") if name == "qT" else \
                        kstack[i % 2][:].rearrange("p a h s -> p (a h s)")
                    key = (name, l, u, tau, w)
                    ps, again = B.claim(key, misc_bank())
                    pe.wait_ge(*B.before(key))
                    for p in range(4):
                        ins = nc.tensor.transpose(ps[:, p * P:(p + 1) * P], flat[:, (4 * w + p) * P:(4 * w + p + 1) * P],
                                                  ident[:])
                    ins.then_inc(B.fills(key), 1)

            def scores_rows(l, u, g, qb):
                if g % 2 == 0 and qb == 0:
                    for tau in range(2):
                        for name, w in stack_banks(l, g // 2):
                            pe.wait_ge(*B.emptied((name, l, u, tau, w)))
                nk = (qb + 1) * P if CAUSAL[l] else SEQ
                for pl in range(2):
                    key = ("S", l, u, g, qb, pl)
                    ring_s[0] += 1
                    ps, again = B.claim(key, ring_s[0] % 2)
                    pe.wait_ge(*B.before(key))
                    slot = key_slot(l, g, 2 * g + pl, 0)
                    ins = mm(ps[:, 0:2 * nk].rearrange("p (h k) -> p h k", h=2),
                             qT[u % 2][:, 2 * g + pl, qb * P:(qb + 1) * P],
                             kT[u % 2][:, slot:slot + 2, 0:nk], start=True, stop=not CAUSAL[l])
                    if CAUSAL[l]:
                        dst = ps[:, 0:2 * nk].rearrange("p (h k) -> p h k", h=2)[:, :, nk - P:nk]
                        ins = mm(dst, identb[:], mask[:].rearrange("p (h k) -> p h k", h=2),
                                 start=False, stop=True)
                    ins.then_inc(B.fills(key), 1)

            def turn_max(l, u):
                key = ("mT", l, u)
                ps, again = B.claim(key, misc_bank())
                pe.wait_ge(*B.before(key))
                pe.wait_ge(*B.emptied(("S", l, u, GROUPS - 1, 1, 1)))
                for qb in range(2):
                    ins = nc.tensor.transpose(ps[0:UH, qb * P:(qb + 1) * P], negmax[u % 2][:, qb, :], ident[:])
                ins.then_inc(B.fills(key), 1)

            def scores_cols(l, u, g, kb):
                if g == 0 and kb == 0:
                    pe.wait_ge(m_rows[u % 2], 32 * (4 * l + u // 2 + 1))
                q0 = kb * P if CAUSAL[l] else 0
                nq = SEQ - q0
                for par in range(2):
                    key = ("ST", l, u, g, kb, par)
                    ring_t[0] += 1
                    ps, again = B.claim(key, 2 + ring_t[0] % 2)
                    pe.wait_ge(*B.before(key))
                    for pairs in ((0, 2),) if GQA[l] else ((0, 1), (1, 2)):
                        n = pairs[1] - pairs[0]
                        ins = mm(ps[:, pairs[0] * nq:pairs[1] * nq].rearrange("p (h q) -> p h q", h=n),
                                 kT[u % 2][:, key_slot(l, g, 2 * g + pairs[0], par), kb * P:(kb + 1) * P],
                                 qT[u % 2][:, 2 * g + pairs[0]:2 * g + pairs[1], q0:SEQ], start=True, stop=True)
                    ins.then_inc(B.fills(key), 1)

            def weigh_values(l, gi):
                u, g = gi // GROUPS, gi % GROUPS
                key = ("PV", l, gi)
                ps, again = B.claim(key, misc_bank())
                pe.wait_ge(*B.before(key))
                if CAUSAL[l]:
                    pe.wait_ge(*causal_cut.at(l, 2 * (gi + 1)))
                else:
                    pe.wait_ge(*B.emptied(("ST", l, u, g, 1, 1)))
                for tau in range(2):
                    pe.wait_ge(*B.emptied(("qkv" if GQA[l] else "v", l, u, tau)))
                for kb in range(2):
                    q0 = kb * P if CAUSAL[l] else 0
                    for i in range(4):
                        kv = g if GQA[l] else 4 * g + i
                        ins = mm(ps[32 * i:32 * i + 32, q0:SEQ], Vflat[u % 4][:, (kb * UH + kv) * CELL:(kb * UH + kv) * CELL + 32],
                                 probs[gi % 2][:, kb, i, q0:SEQ],
                                 start=(kb == 0), stop=(kb == 1))
                ins.then_inc(B.fills(key), 1)

            def turn_context(l, gi):
                key = ("ctx", l, gi)
                ps, again = B.claim(key, misc_bank())
                pe.wait_ge(*B.before(key))
                pe.wait_ge(*B.emptied(("PV", l, gi)))
                for qb in range(2):
                    ins = nc.tensor.transpose(ps[:, qb * P:(qb + 1) * P], pv[gi % 2][:, qb * P:(qb + 1) * P], ident[:])
                ins.then_inc(B.fills(key), 1)

            def turn_rows(l, b):
                for tau in range(2):
                    key = ("ctxT", l, b, tau)
                    ps, again = B.claim(key, misc_bank())
                    pe.wait_ge(*B.before(key))
                    pe.wait_ge(*B.emptied(("ctx", l, 8 * b + 7)))
                    for c in range(KC):
                        ins = nc.tensor.transpose(ps[:, c * P:(c + 1) * P], ctxr[b % 2][:, tau, c * P:(c + 1) * P], ident[:])
                    ins.then_inc(B.fills(key), 1)

            def project_out(l, b):
                for tau in range(2):
                    key = ("O", l, b, tau)
                    ps, again = B.claim(key, misc_bank())
                    pe.wait_ge(*B.before(key))
                    pe.wait_ge(*B.emptied(("ctxT", l, b, tau)))
                    for c in range(KC):
                        ins = mm(ps[:], ctxT[tau][:, c, :], Wo[:, c, :], start=(c == 0), stop=(c == KC - 1))
                    ins.then_inc(B.fills(key), 1)

            def attention(l):
                for u in range(2):
                    for tau in range(2):
                        project(l, u, tau)
                for half in range(2):
                    for tau in range(2):
                        turn_stacks(l, 0, tau, half)
                for g in range(GROUPS):
                    for qb in range(2):
                        scores_rows(l, 0, g, qb)
                for tau in range(2):
                    turn_stacks(l, 1, tau, 0)
                turn_max(l, 0)
                for u in range(UNITS):
                    for g in range(GROUPS):
                        gi = GROUPS * u + g
                        if g < 2 and u + 2 < UNITS:
                            project(l, u + 2, g)
                        scores_cols(l, u, g, 0)
                        if u + 1 < UNITS and g < 2:
                            turn_stacks(l, u + 1, g, 1)
                        if u + 1 < UNITS:
                            scores_rows(l, u + 1, g, 0)
                        if gi >= 1:
                            weigh_values(l, gi - 1)
                        scores_cols(l, u, g, 1)
                        if u + 1 < UNITS:
                            scores_rows(l, u + 1, g, 1)
                        if u + 2 < UNITS and g >= 2:
                            turn_stacks(l, u + 2, g - 2, 0)
                        if gi >= 2:
                            turn_context(l, gi - 2)
                        if u % 2 == 0 and u > 0 and g == 2:
                            turn_rows(l, u // 2 - 1)
                        if u % 2 == 0 and u > 0 and g == 3:
                            project_out(l, u // 2 - 1)
                    if u + 1 < UNITS:
                        turn_max(l, u + 1)
                weigh_values(l, 31)
                turn_context(l, 30)
                turn_context(l, 31)
                turn_rows(l, SEQS - 1)
                project_out(l, SEQS - 1)

            pe.wait_ge(const_in, 16 * CONSTS)
            for l in range(LAYERS):
                transposes(l)
                ffn(l)
                attention(l)

        @block.scalar
        def _(act):
            copy = ACT.Copy

            def empty(key, dst, src, func=copy, **kw):
                act.wait_ge(*B.filled(key))
                return nc.scalar.activation(dst, src, func, **kw)

            def transposes(l):
                for t in range(TILES):
                    key = ("xT", l, t)
                    act.wait_ge(*B.filled(key))
                    nc.scalar.activation(xT[:, :, t * P:(t + 1) * P], B.tensor(key)[:].rearrange("p (c t) -> p c t", c=KC),
                                         copy).then_inc(B.empties(key), 1)

            def hidden(l, n, chunks):
                for j in range(chunks):
                    e = n * chunks + j
                    key = ("gate", l, n, j)
                    act.wait_ge(*B.filled(key))
                    if e >= 2:
                        act.wait_ge(*B.emptied(("up", l, (e - 2) // chunks, (e - 2) % chunks)))
                    kw = {}
                    if l == 0:
                        kw = {"scale": tscale[:, 0:1]}
                    if l == 3:
                        kw = {"bias": b1[:, 0, j:j + 1]}
                    nc.scalar.activation(silu[e % 2][:], B.tensor(key)[:], ACT.Silu, **kw).then_inc(B.empties(key), 1)

            def out_tiles(l, n):
                for t in range(4 * n, 4 * n + 4):
                    key = ("out", l, t)
                    if l == 3:
                        act.wait_ge(*B.emptied(key))
                        nc.scalar.activation(gate[:, t, :], outb[t % 2][:], ACT.Silu).then_inc(gate_ready.sem, 1)
                        continue
                    act.wait_ge(*B.filled(key))
                    kw = {"scale": tscale[:, 2:3]} if l == 0 else {}
                    nc.scalar.activation(gate[:, t, :], B.tensor(key)[:], ACT.Silu, **kw).then_inc(B.empties(key), 1)

            def ffn(l):
                for n in range(2):
                    if l == 0 and n == 0:
                        act.wait_ge(*tern.at(0, 15))
                    if l == 3:
                        key = ("low", n)
                        act.wait_ge(*B.filled(key))
                        nc.scalar.activation(PT[:, n, :], B.tensor(key)[:], copy).then_inc(B.empties(key), 1)
                    if l != 1:
                        hidden(l, n, {0: HC0, 2: HC2, 3: HC3}[l])
                    if l == 3:
                        key = ("low2", n)
                        act.wait_ge(*B.filled(key))
                        nc.scalar.activation(ZT[:, n, :], B.tensor(key)[:], copy).then_inc(B.empties(key), 1)
                    out_tiles(l, n)

            def take_projection(l, u, tau):
                i = 2 * u + tau
                key = ("qkv", l, u, tau)
                ps = B.tensor(key)
                nqk = 20 if GQA[l] else 32
                act.wait_ge(*B.filled(key))
                if i >= 2 and GQA[l]:
                    act.wait_ge(*rope_part.at(l, 3 * (i - 1)))
                if i >= 2 and not GQA[l]:
                    act.wait_ge(*stack_lo.at(l, 2 * (i - 1)))
                ins = nc.scalar.activation(qk[i % 2][:, 0:nqk, :], ps[:, 0:nqk * HD].rearrange("p (h d) -> p h d", d=HD), copy)
                if GQA[l]:
                    nc.scalar.activation(V[u % 4][:, tau, 0:4, 0:HD], ps[:, 320:384].rearrange("p (h d) -> p h d", d=HD),
                                         copy).then_inc(B.empties(key), 1)
                else:
                    ins.then_inc(B.empties(key), 1)
                    key = ("v", l, u, tau)
                    act.wait_ge(*B.filled(key))
                    nc.scalar.activation(V[u % 4][:, tau, :, 0:HD],
                                         B.tensor(key)[:, 0:256].rearrange("p (h d) -> p h d", d=HD),
                                         copy).then_inc(B.empties(key), 1)

            def stack_high(l, u, tau):
                i = 2 * u + tau
                if ROPE[l]:
                    act.wait_ge(*rope_done.at(l, i + 1))
                    src = qkr[i % 2]
                else:
                    act.wait_ge(*B.emptied(("qkv", l, u, tau)))
                    src = qk[i % 2]
                qs = qstack[i % 2][:].bitcast(F32R)
                ks = kstack[i % 2][:].bitcast(F32R)
                if i >= 2:
                    for name, w in stack_banks(l, 1):
                        act.wait_ge(*B.filled((name, l, u - 1, tau, w)))
                dst = qs[:, :, 0:48].rearrange("p h (s d) -> p h s d", d=SPLIT)[:, :, 0:3:2, :]
                nc.scalar.activation(dst, src[:, 0:UH, :].unsqueeze(2).to_broadcast([P, UH, 2, HD]), copy).then_inc(stack_hi.sem, 1)
                for par in range(2):
                    n = 4 if GQA[l] else 8
                    kd = ks[:, 0:n, 3 * par, 0:32].rearrange("p n (s d) -> p n s d", d=SPLIT)
                    kv = src[:, UH:UH + 4, :] if GQA[l] else src[:, UH + par:2 * UH:2, :]
                    nc.scalar.activation(kd, kv.unsqueeze(2).to_broadcast([P, n, 2, HD]), copy).then_inc(stack_hi.sem, 1)

            def take_stacks(l, u, tau, half):
                key = ("qT", l, u, tau, half)
                act.wait_ge(*B.filled(key))
                nc.scalar.activation(qT[u % 2][:, 4 * half:4 * half + 4, tau * P:(tau + 1) * P],
                                     B.tensor(key)[:].rearrange("p (a t) -> p a t", a=4), copy).then_inc(B.empties(key), 1)

            def exponentials(l, u, g, kb):
                gi = GROUPS * u + g
                if gi >= 2:
                    act.wait_ge(*B.filled(("PV", l, gi - 2)))
                q0 = kb * P if CAUSAL[l] else 0
                nq = SEQ - q0
                for par in range(2):
                    key = ("ST", l, u, g, kb, par)
                    act.wait_ge(*B.filled(key))
                    nc.scalar.activation(probs[gi % 2][:, kb, par:4:2, q0:SEQ],
                                         B.tensor(key)[:, 0:2 * nq].rearrange("p (h q) -> p h q", h=2),
                                         ACT.Exp, scale=0.25).then_inc(B.empties(key), 1)

            def take_pv(l, gi):
                key = ("PV", l, gi)
                act.wait_ge(*B.filled(key))
                nc.scalar.activation(pv[gi % 2][:], B.tensor(key)[:, 0:SEQ], copy).then_inc(B.empties(key), 1)

            def take_rows(l, b):
                for tau in range(2):
                    key = ("ctxT", l, b, tau)
                    act.wait_ge(*B.filled(key))
                    nc.scalar.activation(ctxT[tau][:].rearrange("p c t -> p (c t)"), B.tensor(key)[:],
                                         copy).then_inc(B.empties(key), 1)

            def attention(l):
                act.wait_ge(*(B.emptied(last_out[l]) if l != 3 else gate_ready.at(3, TILES)))
                for tau in range(2):
                    take_projection(l, 0, tau)
                for tau in range(2):
                    stack_high(l, 0, tau)
                for tau in range(2):
                    take_projection(l, 1, tau)
                for half in range(2):
                    for tau in range(2):
                        take_stacks(l, 0, tau, half)
                for tau in range(2):
                    stack_high(l, 1, tau)
                for tau in range(2):
                    take_stacks(l, 1, tau, 0)
                for u in range(UNITS):
                    for g in range(GROUPS):
                        gi = GROUPS * u + g
                        if g < 2 and u + 2 < UNITS:
                            take_projection(l, u + 2, g)
                        exponentials(l, u, g, 0)
                        if u + 1 < UNITS and g < 2:
                            take_stacks(l, u + 1, g, 1)
                        if gi >= 1:
                            take_pv(l, gi - 1)
                        exponentials(l, u, g, 1)
                        if g < 2 and u + 2 < UNITS:
                            stack_high(l, u + 2, g)
                        if u + 2 < UNITS and g >= 2:
                            take_stacks(l, u + 2, g - 2, 0)
                        if u % 2 == 0 and u > 0 and g == 2:
                            take_rows(l, u // 2 - 1)
                take_pv(l, 31)
                take_rows(l, SEQS - 1)

            for l in range(LAYERS):
                transposes(l)
                ffn(l)
                attention(l)

        @block.vector
        def _(dve):
            v = nc.vector

            def normalise(l):
                for b in range(SEQS):
                    for t in (2 * b, 2 * b + 1):
                        if l == 0:
                            dve.wait_ge(x_in[b], 16)
                        else:
                            dve.wait_ge(*x_done.at(l - 1, t + 1))
                        v.bn_stats(stats[:, t, :], x[:, t, :]).then_inc(ln_stat.sem, 1)
                    for t in (2 * b, 2 * b + 1):
                        dve.wait_ge(*ln_stat.at(l, t + 1))
                        v.bn_aggr(moments[:, t, :], stats[:, t, :]).then_inc(ln_mom.sem, 1)
                    dve.wait_ge(*ln_mom.at(l, 2 * b + 2))
                    v.tensor_scalar(vareps[:, 2 * b:2 * b + 2], moments[:, 2 * b:2 * b + 2, 1], EPS, None,
                                    ALU.add).then_inc(ln_var.sem, 1)
                    if b >= 1:
                        scale_rows(l, b - 1)
                scale_rows(l, SEQS - 1)

            def scale_rows(l, b):
                dve.wait_ge(*ln_rstd.at(l, b + 1))
                for t in (2 * b, 2 * b + 1):
                    if t >= 4:
                        dve.wait_ge(*B.filled(("xT", l, t - 4)))
                    dst, src = xn[t % 4][:], x[:, t, :]
                    if l == 1:
                        dst = xn[t % 4][:].rearrange("p (s r) -> p r s", s=8)
                        src = x[:, t, :].rearrange("p (r s) -> p r s", s=8)
                    v.tensor_scalar(dst, src, moments[:, t, 0:1], rstd[:, t:t + 1], ALU.subtract,
                                    ALU.mult).then_inc(xn_ready.sem, 1)

            def ternary():
                mats = [(Wgu0[0], 170, KC, HID0, sign_in), (Wgu0[1], 170, KC, HID0, sign_in), (Wd0, 64, HC0, D, sign_hid)]
                steps = [0]

                def step(ins):
                    steps[0] += 1
                    ins.then_inc(tern.sem, 1)
                    dve.wait_ge(*tern.at(0, steps[0]))

                for m, (W, width, chunks, cols, signs) in enumerate(mats):
                    dve.wait_ge(ffn_in[m], 16)
                    if m == 0:
                        dve.wait_ge(const_in, 16 * CONSTS)
                    step(v.tensor_reduce(absum[:, m:m + 1], W[:, :, 0:width], AX.XY, ALU.add, apply_absolute_value=True))
                    key = ("wsum", m)
                    dve.wait_ge(*B.filled(key))
                    ins = v.tensor_scalar(tscale[:, m:m + 1], B.tensor(key)[:, 0:1], 1.0 / (HID0 * D // OCT), None, ALU.mult)
                    ins.then_inc(B.empties(key), 1)
                    dve.wait_ge(*B.emptied(key))
                    step(v.reciprocal(tinv[:, m:m + 1], tscale[:, m:m + 1]))
                    step(v.tensor_scalar(W[:, :, 0:cols], W[:, :, 0:cols], tinv[:, m:m + 1], 1.0, ALU.mult, ALU.min))
                    step(v.tensor_scalar(W[:, :, 0:cols], W[:, :, 0:cols], -1.0, ROUND, ALU.max, ALU.add))
                    for c in range(chunks):
                        w = W[:, c, 0:cols].rearrange("p (k o) -> p k o", k=OCT)
                        ins = v.scalar_tensor_tensor(w, w, ROUND, signs[:, c, :].unsqueeze(2).to_broadcast([P, OCT, width]),
                                                     ALU.subtract, ALU.mult)
                    step(ins)

            def dequantise():
                steps = [0]

                def step(ins):
                    steps[0] += 1
                    ins.then_inc(deq.sem, 1)

                dve.wait_ge(ffn_in[0], 16 * (1 + LOADS[1]))
                for s in range(8):
                    step(v.tensor_scalar(zn[:, :, s], zq[:], 4 * s, 15, ALU.logical_shift_right, ALU.bitwise_and))
                dve.wait_ge(*deq.at(1, steps[0]))
                step(v.tensor_scalar(zf[:], zn[:].rearrange("g c s -> g (c s)"), 1.0, None, ALU.add))
                step(v.tensor_copy(sf[:], sh[:]))
                step(v.tensor_scalar(onehot[:], gidx[:], four[:, 0:1], None, ALU.is_equal))
                step(v.memset(ones16[:], 1.0))
                for c in range(KC):
                    for half in range(2):
                        r = slice(64 * half, 64 * half + 64)
                        step(v.tensor_scalar(W1n[r, c, :], W1q[r, c, :], 4 * (2 * c + half), 15,
                                             ALU.logical_shift_right, ALU.bitwise_and))
                    kz, ks = ("group", c, 0), ("group", c, 1)
                    dve.wait_ge(*deq.at(1, steps[0]))
                    dve.wait_ge(*B.filled(kz))
                    v.tensor_tensor(W1f[:], W1n[:, c, :], B.tensor(kz)[:], ALU.subtract).then_inc(B.empties(kz), 1)
                    dve.wait_ge(*B.emptied(kz))
                    dve.wait_ge(*B.filled(ks))
                    v.tensor_tensor(W1h[:, c, :], W1f[:], B.tensor(ks)[:], ALU.mult).then_inc(B.empties(ks), 1)
                    dve.wait_ge(*B.emptied(ks))
                    v.tensor_copy(W1[:, c, :], W1h[:, c, :]).then_inc(deq_done.sem, 1)

            def hidden(l, n, chunks):
                for j in range(chunks):
                    e = n * chunks + j
                    key = ("up", l, n, j)
                    dve.wait_ge(*B.emptied(("gate", l, n, j)))
                    dve.wait_ge(*B.filled(key))
                    if n == 1 and j == 0:
                        dve.wait_ge(*B.filled(("out", l, 3) if l != 3 else ("low2", 0)))
                    ps, h = B.tensor(key)[:], hT[:, j, :]
                    if l == 0:
                        ins = v.scalar_tensor_tensor(h, ps, tscale[:, 1:2], silu[e % 2][:], ALU.mult, ALU.mult)
                    elif l == 3:
                        ins = v.scalar_tensor_tensor(h, ps, b1[:, 1, j:j + 1], silu[e % 2][:], ALU.add, ALU.mult)
                    else:
                        ins = v.tensor_tensor(h, ps, silu[e % 2][:], ALU.mult)
                    ins.then_inc(B.empties(key), 1)

            def ffn(l):
                if l == 1:
                    return
                for n in range(2):
                    hidden(l, n, {0: HC0, 2: HC2, 3: HC3}[l])
                    if l == 3:
                        for t in range(4 * n, 4 * n + 4):
                            key = ("out", l, t)
                            dve.wait_ge(*B.filled(key))
                            if t >= 2:
                                dve.wait_ge(*gate_ready.at(3, t - 1))
                            v.tensor_tensor(outb[t % 2][:], B.tensor(key)[:], b2[:], ALU.add).then_inc(B.empties(key), 1)

            def rope(l, u, tau):
                i = 2 * u + tau
                dve.wait_ge(*B.emptied(("qkv", l, u, tau)))
                if i >= 2:
                    dve.wait_ge(*rope_done.at(l, i - 1))
                    dve.wait_ge(*stack_hi.at(l, HI * (i - 1)))
                    dve.wait_ge(*stack_lo.at(l, 2 * (i - 1)))
                src, tc, ts = qk[i % 2], rc[i % 2], rs[i % 2]
                half = HD // 2
                v.tensor_tensor(tc[:], src[:, 0:20, :], cosT[l][:, tau, :].unsqueeze(1).to_broadcast([P, 20, HD]),
                                ALU.mult).then_inc(rope_part.sem, 1)
                v.tensor_tensor(ts[:, :, 0:half], src[:, 0:20, half:HD],
                                sinT[l][:, tau, 0:half].unsqueeze(1).to_broadcast([P, 20, half]), ALU.mult).then_inc(rope_part.sem, 1)
                v.tensor_tensor(ts[:, :, half:HD], src[:, 0:20, 0:half],
                                sinT[l][:, tau, half:HD].unsqueeze(1).to_broadcast([P, 20, half]), ALU.mult).then_inc(rope_part.sem, 1)
                dve.wait_ge(*rope_part.at(l, 3 * (i + 1)))
                v.tensor_tensor(qkr[i % 2][:], tc[:], ts[:], ALU.add).then_inc(rope_done.sem, 1)

            def row_max(l, u, g, qb):
                nk = (qb + 1) * P if CAUSAL[l] else SEQ
                for pl in range(2):
                    key = ("S", l, u, g, qb, pl)
                    dve.wait_ge(*B.filled(key))
                    v.tensor_reduce(negmax[u % 2][:, qb, 2 * g + pl:2 * g + pl + 9:8],
                                    B.tensor(key)[:, 0:2 * nk].rearrange("p (h k) -> p h k", h=2),
                                    AX.X, ALU.max, negate=True).then_inc(B.empties(key), 1)

            def take_key_stacks(l, u, tau, half):
                for name, w in stack_banks(l, half)[1:]:
                    key = (name, l, u, tau, w)
                    dve.wait_ge(*B.filled(key))
                    v.tensor_copy(kT[u % 2][:, 4 * w:4 * w + 4, tau * P:(tau + 1) * P],
                                  B.tensor(key)[:].rearrange("p (a t) -> p a t", a=4)).then_inc(B.empties(key), 1)

            def take_max(l, u):
                key = ("mT", l, u)
                dve.wait_ge(*B.filled(key))
                v.tensor_copy(negmaxT[u % 2][:], B.tensor(key)[0:UH, 0:SEQ]).then_inc(B.empties(key), 1)

            def context(l, gi):
                u, g = gi // GROUPS, gi % GROUPS
                b, hh = u // 2, u % 2
                key = ("ctx", l, gi)
                dve.wait_ge(*B.filled(key))
                ps = B.tensor(key)[:, 0:2 * P].rearrange("p (q i r) -> p q i r", q=2, i=4)
                if gi >= 2:
                    dve.wait_ge(*B.emptied(("ctx", l, gi - 2)))
                v.reciprocal(recip[gi % 2][:], ps[:, :, :, HD]).then_inc(rs_ready.sem, 1)
                dve.wait_ge(*rs_ready.at(l, gi + 1))
                c0 = (UH * hh + 4 * g) * HD
                v.tensor_tensor(ctxr[b % 2][:, :, c0:c0 + 4 * HD].rearrange("p q (i d) -> p q i d", i=4), ps[:, :, :, 0:HD],
                                recip[gi % 2][:].unsqueeze(3).to_broadcast([P, 2, 4, HD]), ALU.mult).then_inc(B.empties(key), 1)

            def residual(l, b):
                for tau in range(2):
                    t = 2 * b + tau
                    key = ("O", l, b, tau)
                    dve.wait_ge(*B.filled(key))
                    v.tensor_tensor(ctxr[b % 2][:, tau, :], B.tensor(key)[:], gate[:, t, :], ALU.mult).then_inc(B.empties(key), 1)
                    dve.wait_ge(*B.emptied(key))
                    v.tensor_tensor(x[:, t, :], x[:, t, :], ctxr[b % 2][:, tau, :], ALU.add).then_inc(x_done.sem, 1)

            def attention(l):
                dve.wait_ge(*(B.emptied(last_out[l]) if l != 3 else gate_ready.at(3, TILES)))
                for u in range(2):
                    for tau in range(2):
                        if ROPE[l]:
                            rope(l, u, tau)
                for half in range(2):
                    for tau in range(2):
                        take_key_stacks(l, 0, tau, half)
                for g in range(GROUPS):
                    for qb in range(2):
                        row_max(l, 0, g, qb)
                for tau in range(2):
                    take_key_stacks(l, 1, tau, 0)
                take_max(l, 0)
                for u in range(UNITS):
                    for g in range(GROUPS):
                        gi = GROUPS * u + g
                        if u + 1 < UNITS and g < 2:
                            take_key_stacks(l, u + 1, g, 1)
                        if u + 1 < UNITS:
                            row_max(l, u + 1, g, 0)
                        if g < 2 and u + 2 < UNITS and ROPE[l]:
                            rope(l, u + 2, g)
                        if u + 1 < UNITS:
                            row_max(l, u + 1, g, 1)
                        if u + 2 < UNITS and g >= 2:
                            take_key_stacks(l, u + 2, g - 2, 0)
                        if gi >= 2:
                            context(l, gi - 2)
                        if u % 2 == 0 and u > 0 and g == 3:
                            residual(l, u // 2 - 1)
                    if u + 1 < UNITS:
                        take_max(l, u + 1)
                context(l, 30)
                context(l, 31)
                residual(l, SEQS - 1)

            v.memset(ones[:], 1.0).then_inc(ones_set.sem, 1)
            v.memset(minus_half[:], -0.5).then_inc(ones_set.sem, 1)
            for l in range(LAYERS):
                normalise(l)
                if l == 0:
                    dve.wait_ge(const_in, 16 * CONSTS)
                    v.tensor_copy(identb[:], ident[:]).then_inc(mask_set.sem, 1)
                    v.tensor_copy(mask[:], maskf[:]).then_inc(mask_set.sem, 1)
                    ternary()
                if l == 1:
                    dequantise()
                ffn(l)
                attention(l)

        @block.gpsimd
        def _(pool):
            gp = nc.gpsimd

            def inverse_deviation(l):
                for b in range(SEQS):
                    pool.wait_ge(*ln_var.at(l, b + 1))
                    gp.tensor_tensor(rstd[:, 2 * b:2 * b + 2], vareps[:, 2 * b:2 * b + 2], minus_half[:, 0:2],
                                     ALU.pow).then_inc(ln_rstd.sem, 1)

            def scale_weights():
                for j in range(HC2):
                    pool.wait_ge(w2_in[j], 48)
                    if j == 0:
                        pool.wait_ge(ffn_in[2], 16 + 48)
                    for m in range(2):
                        w = W2gu[m][:, j, :, :]
                        gp.tensor_tensor(w, w, s2[m][:, j, :].unsqueeze(2).to_broadcast([P, KC, P]),
                                         ALU.mult).then_inc(w_scaled.sem, 1)
                    w = W2d[:, j, :].rearrange("p (n o) -> p n o", n=KC)
                    gp.tensor_tensor(w, w, s2[2][:, j, :].unsqueeze(2).to_broadcast([P, KC, P]),
                                     ALU.mult).then_inc(w_scaled.sem, 1)

            def set_pads(l):
                pool.wait_ge(*(B.emptied(last_out[l]) if l != 3 else gate_ready.at(3, TILES)))
                for i in range(2):
                    gp.memset(qstack[i][:, :, STACK:64], 0.0).then_inc(pads.sem, 1)
                    gp.memset(kstack[i][:, :, 0:4:3, STACK:STACK + 1], 1.0).then_inc(pads.sem, 1)
                    gp.memset(kstack[i][:, :, 0:4:3, STACK + 1:64], 0.0).then_inc(pads.sem, 1)
                    gp.memset(kstack[i][:, :, 1:3, :], 0.0).then_inc(pads.sem, 1)
                for i in range(4):
                    gp.memset(V[i][:, :, :, HD:HD + 1], 1.0).then_inc(pads.sem, 1)
                    gp.memset(V[i][:, :, :, HD + 1:CELL], 0.0).then_inc(pads.sem, 1)
                    gp.memset(Vflat[i][:, 2 * UH * CELL:], 0.0).then_inc(pads.sem, 1)
                    if GQA[l]:
                        gp.memset(V[i][:, :, 4, 0:HD], 0.0).then_inc(pads.sem, 1)

            def stack_low(l, u, tau):
                i = 2 * u + tau
                pool.wait_ge(*stack_hi.at(l, HI * (i + 1)))
                src = qkr[i % 2] if ROPE[l] else qk[i % 2]
                qs, ks = qstack[i % 2], kstack[i % 2]
                gp.tensor_tensor(qs[:].bitcast(F32R)[:, :, 16:32], src[:, 0:UH, :], qs[:, :, 0:16],
                                 ALU.subtract).then_inc(stack_lo.sem, 1)
                n = 4 if GQA[l] else 8
                if GQA[l]:
                    kv = src[:, UH:UH + 4, :].unsqueeze(2).to_broadcast([P, 4, 2, HD])
                else:
                    kv = src[:, UH:2 * UH, :].rearrange("p (n c) d -> p n c d", c=2)
                gp.tensor_tensor(ks[:].bitcast(F32R)[:, 0:n, 0:4:3, 32:48], kv, ks[:, 0:n, 0:4:3, 0:16],
                                 ALU.subtract).then_inc(stack_lo.sem, 1)

            def cut_future(l, u, g):
                gi = GROUPS * u + g
                for kb in range(2):
                    pool.wait_ge(*B.emptied(("ST", l, u, g, kb, 1)))
                    blk = probs[gi % 2][:, kb, :, kb * P:(kb + 1) * P]
                    gp.affine_select(out=blk, in_=blk, compare_op=ALU.is_ge, fill=0.0, base=0,
                                     pattern=[[0, 4], [1, P]], channel_multiplier=-1).then_inc(causal_cut.sem, 1)

            pool.wait_ge(*ones_set.at(0, 2))
            for l in range(LAYERS):
                inverse_deviation(l)
                if l == 2:
                    scale_weights()
                set_pads(l)
                for u in range(2):
                    for tau in range(2):
                        stack_low(l, u, tau)
                for u in range(UNITS):
                    for g in range(GROUPS):
                        if CAUSAL[l]:
                            cut_future(l, u, g)
                        if g < 2 and u + 2 < UNITS:
                            stack_low(l, u + 2, g)

        @block.sync
        def _(sp):
            xv = a["x"].rearrange("(t p) d -> p t d", p=P)

            def load(dst, src, s):
                sp.dma_start(dst, src).then_inc(s, 16)

            for b in range(SEQS):
                load(x[:, 2 * b:2 * b + 2, :], xv[:, 2 * b:2 * b + 2, :], x_in[b])
            n = 0
            for dst, name in [(ident, "ident"), (maskf, "mask"), (sign_in, "sign_in"), (sign_hid, "sign_hid")] + \
                    [(cosT[l], f"cos{l}") for l in (0, 2, 3)] + [(sinT[l], f"sin{l}") for l in (0, 2, 3)]:
                load(dst[:], a[name], const_in)
                n += 1
            assert n == CONSTS

            def load_attention(l):
                if GQA[l]:
                    load(Wqkv[:, :, :, 0:384], a[f"Wqkv{l}"], att_in)
                else:
                    load(Wqkv[:], a[f"Wqkv{l}"], att_in)
                load(Wo[:], a[f"Wo{l}"], att_in)

            load(Wgu0[0][:], a["Wg0"], ffn_in[0])
            load(Wgu0[1][:], a["Wu0"], ffn_in[1])
            load(Wd0[:], a["Wd0"], ffn_in[2])
            for l in range(LAYERS):
                if l > 0:
                    sp.wait_ge(*x_done.at(l - 1, TILES))
                if l == 1:
                    for dst, name in [(W1q, "qweight"), (zq, "qzeros"), (sh, "scales"), (gidx, "g_idx"), (four, "four"),
                                      (bias1, "bias1")]:
                        load(dst[:], a[name], ffn_in[0])
                if l == 2:
                    for i, name in enumerate(("w1s", "w3s", "w2s")):
                        load(s2[i][:], a[name], ffn_in[2])
                    for j in range(HC2):
                        load(W2gu[0][:, j], a["w1"][:, j], w2_in[j])
                        load(W2gu[1][:, j], a["w3"][:, j], w2_in[j])
                        load(W2d[:, j], a["w2"][:, j], w2_in[j])
                if l == 3:
                    for dst, name in [(U1, "U1"), (V1, "V1"), (U2, "U2"), (V2, "V2"), (b1, "b1"), (b2, "b2")]:
                        load(dst[:], a[name], ffn_in[0])
                load_attention(l)
                for u in range(UNITS):
                    sp.wait_ge(*B.emptied(("mT", l, u)))
                    for par in range(2):
                        r = 64 * par + STACK
                        load(qT[u % 2][r:r + 1, :, :].bitcast(F32), negmaxT[u % 2][8 * par:8 * par + 8, :].bitcast(F32), m_rows[u % 2])
            ov = out.rearrange("(t p) d -> p t d", p=P)
            for t in range(TILES):
                sp.wait_ge(*x_done.at(LAYERS - 1, t + 1))
                sp.dma_start(ov[:, t:t + 1, :], x[:, t:t + 1, :]).then_inc(out_done, 16)
            sp.wait_ge(out_done, 16 * TILES)


CONSTS = 10
LOADS = {1: 6, 3: 1 + 6 + 6}


def layouts(inputs):
    g = {k: np.asarray(v) for k, v in inputs.items()}
    o = {"x": g["L0_attn_hidden_states"].reshape(SEQS * SEQ, D)}
    eye = np.eye(P, dtype=np.float32)
    o["ident"] = eye
    future = np.where(np.arange(P)[None, :] > np.arange(P)[:, None], np.float32(NEG), np.float32(0))
    o["mask"] = np.concatenate([future, future], axis=1)
    which, sign = octonion_table()
    i_of = np.arange(D) // 64
    o["sign_in"] = np.ascontiguousarray(sign[i_of].reshape(KC, P, OCT).transpose(1, 0, 2))
    hid = np.minimum(np.arange(HC0 * P) // 170, 7)
    o["sign_hid"] = np.ascontiguousarray(sign[hid].reshape(HC0, P, OCT).transpose(1, 0, 2))
    for l in (0, 2, 3):
        inv = (1.0 / np.float32(ROPE_BASE[l]) ** (np.arange(0, HD, 2, dtype=np.float32) / HD)).astype(np.float32)
        ang = (np.arange(SEQ, dtype=np.float32)[:, None] * inv[None, :]).astype(np.float32)
        c, s = np.cos(ang), np.sin(ang)
        o[f"cos{l}"] = np.ascontiguousarray(np.concatenate([c, c], 1).reshape(2, P, HD).transpose(1, 0, 2)).astype(np.float32)
        o[f"sin{l}"] = np.ascontiguousarray(np.concatenate([-s, s], 1).reshape(2, P, HD).transpose(1, 0, 2)).astype(np.float32)

    shift_order = np.arange(D).reshape(64, 8).T.reshape(-1)
    halves = np.concatenate([np.arange(0, HD, 2), np.arange(1, HD, 2)])
    for l in range(LAYERS):
        wq, wk, wv, wo = (g[f"L{l}_attn_{n}"] for n in ("Wq", "Wk", "Wv", "Wo"))
        if l < 2:
            wq, wk, wv, wo = wq.T, wk.T, wv.T, wo.T
        if l == 1:
            wq, wk, wv = wq[shift_order], wk[shift_order], wv[shift_order]
        q = wq.reshape(D, 2, UH, HD)
        k = wk.reshape(D, 2, -1, HD)
        if l == 0:
            q, k = q[..., halves], k[..., halves]
        v = wv.reshape(D, 2, -1, HD)
        w = np.concatenate([y.reshape(D, 2, -1) for y in (q, k, v)], axis=2)
        o[f"Wqkv{l}"] = np.ascontiguousarray(w.reshape(KC, P, 2, -1).transpose(1, 0, 2, 3))
        o[f"Wo{l}"] = np.ascontiguousarray(wo.reshape(KC, P, D).transpose(1, 0, 2))

    for name, key in (("Wg0", "w_gate"), ("Wu0", "w_up")):
        w = g[f"L0_ffn_{key}"][which]
        w = w.transpose(0, 3, 1, 2).reshape(D, HID0)
        pad = np.zeros((D, HC0 * P), np.float32)
        pad[:, :HID0] = w
        o[name] = np.ascontiguousarray(pad.reshape(KC, P, HC0 * P).transpose(1, 0, 2))
    w = g["L0_ffn_w_down"][which].transpose(0, 3, 1, 2).reshape(HID0, D)
    pad = np.zeros((HC0 * P, D), np.float32)
    pad[:HID0] = w
    o["Wd0"] = np.ascontiguousarray(pad.reshape(HC0, P, D).transpose(1, 0, 2))

    qw = g["L1_ffn_qweight"]
    o["qweight"] = np.ascontiguousarray(np.repeat(np.concatenate([qw, qw])[:, None], KC, axis=1))
    o["qzeros"] = np.ascontiguousarray(g["L1_ffn_qzeros"])
    o["scales"] = np.ascontiguousarray(g["L1_ffn_scales"])
    o["g_idx"] = np.ascontiguousarray(np.repeat(g["L1_ffn_g_idx"][shift_order][None], 4, axis=0))
    o["four"] = np.arange(4, dtype=np.float32).reshape(4, 1)
    o["bias1"] = g["L1_ffn_bias"].reshape(1, D)

    for name in ("w1", "w3"):
        w = g[f"L2_ffn_{name}"]
        o[name] = np.ascontiguousarray(w.reshape(HC2, P, KC, P).transpose(3, 0, 2, 1))
        o[name + "s"] = np.ascontiguousarray(np.repeat(g[f"L2_ffn_{name}_scale"][None], P, axis=0))
    w = g["L2_ffn_w2"]
    o["w2"] = np.ascontiguousarray(w.T.reshape(HC2, P, D).transpose(1, 0, 2))
    o["w2s"] = np.ascontiguousarray(np.repeat(g["L2_ffn_w2_scale"].T[None], P, axis=0))

    o["U1"] = np.ascontiguousarray(g["L3_ffn_U1"].reshape(KC, P, P).transpose(1, 0, 2))
    v1 = np.zeros((P, 2, HC3 * P), np.float32)
    v1[:, :, :INTER3] = g["L3_ffn_V1"].reshape(P, 2, INTER3)
    o["V1"] = v1.reshape(P, 2, HC3, P)
    u2 = np.zeros((HC3 * P, P), np.float32)
    u2[:INTER3] = g["L3_ffn_U2"]
    o["U2"] = np.ascontiguousarray(u2.reshape(HC3, P, P).transpose(1, 0, 2))
    o["V2"] = g["L3_ffn_V2"]
    bb = np.zeros((2, HC3 * P), np.float32)
    bb[:, :INTER3] = g["L3_ffn_b1"].reshape(2, INTER3)
    o["b1"] = np.ascontiguousarray(bb.reshape(2, HC3, P).transpose(2, 0, 1))
    o["b2"] = np.ascontiguousarray(np.repeat(g["L3_ffn_b2"][None], P, axis=0))
    return o


def kernel(**inputs):
    import concourse.bacc as _bacc
    from concourse import mybir as _mybir
    from concourse.bass_utils import run_bass_kernel_spmd as _run

    nc = _bacc.Bacc("TRN2", target_bir_lowering=False, num_devices=1)
    arrays, aps = {}, {}
    for name, arr in layouts(inputs).items():
        arrays[f"in_{name}"] = arr
        aps[name] = nc.dram_tensor(f"in_{name}", arr.shape, _mybir.dt.from_np(arr.dtype), kind="ExternalInput").ap()
    out = nc.dram_tensor("out_0", (SEQS, SEQ, D), _mybir.dt.float32, kind="ExternalOutput").ap()
    program(nc, aps, out.rearrange("b s d -> (b s) d"))
    r = _run(nc, [arrays], core_ids=[0])
    return r.results[0]["out_0"]
```

```python
from contextlib import ExitStack

import concourse.bass as bass
import numpy as np
from concourse import mybir

F32 = mybir.dt.float32
F32R = mybir.dt.float32r
BF16 = mybir.dt.bfloat16
F16 = mybir.dt.float16
I32 = mybir.dt.int32
ALU = mybir.AluOpType
ACT = mybir.ActivationFunctionType
AX = mybir.AxisListType

P = 128
D = 512
KC = D // P
SEQS, SEQ = 4, 256
TILES = SEQS * SEQ // P
HEADS, HD = 32, 16
UNITS = 2 * SEQS
UH = 16
GROUPS = UH // 4
LEAD = GROUPS + 1
LAYERS = 4
GQA = [True, False, True, True]
CAUSAL = [True, False, True, True]
ROPE = [True, False, True, True]
ROPE_BASE = {0: 10000.0, 2: 500000.0, 3: 10000.0}
EPS = 1e-5
SPLIT = 16
STACK = 3 * SPLIT
CELL = HD + 4
NEG = -1.0e30
ROUND = 1.5 * 2.0 ** 23
WIDTH0 = 1366 // 8
HID0, HC0 = 8 * WIDTH0, 11
HC2 = 14
HC3 = 11
INTER3 = 1376
OCT = 8
HBUFS = 5
W2BUFS = 4
HIDDEN_CHUNKS = {0: HC0, 2: HC2, 3: HC3}
LATE_TILES = (TILES - 2, TILES - 1)
LAG = {0: 3, 2: 1, 3: 3}


def octonion_table():
    s = np.zeros((8, 8, 8), np.float32)
    s[0, 0, 0] = 1.0
    for i in range(1, 8):
        s[0, i, i] = 1.0
        s[i, 0, i] = 1.0
        s[i, i, 0] = -1.0
    for a, b, c in [(1, 2, 3), (1, 4, 5), (1, 7, 6), (2, 4, 6), (2, 5, 7), (3, 4, 7), (3, 6, 5)]:
        for x, y, z in ((a, b, c), (b, c, a), (c, a, b)):
            s[x, y, z] = 1.0
            s[y, x, z] = -1.0
    which = np.abs(s).argmax(axis=0)
    sign = np.take_along_axis(s, which[None], axis=0)[0]
    return which, sign


def ternary_pieces():
    pieces, gate_up, down, steps = [], [], [], []
    q = 0
    for j in range(HC0 + LAG[0]):
        while q < OCT // 2 and 2 * q * WIDTH0 < (j + 1) * P:
            pieces += [(0, q), (1, q)]
            q += 1
        gate_up.append(len(pieces))
        if j >= LAG[0]:
            pieces.append((2, j - LAG[0]))
            down.append(len(pieces))
        steps.append(len(pieces))
    return pieces, gate_up, down, steps


class AttentionBuffers:
    pass


class Mark:

    def __init__(self, nc, ctx, name, per_layer):
        self.sem = ctx.enter_context(nc.semaphore(name))
        self.per_layer = per_layer

    def at(self, layer, n):
        return self.sem, sum(self.per_layer[:layer]) + n


class Banks:

    def __init__(self, nc, ctx):
        self.ps = [ctx.enter_context(nc.psum_tensor(f"bank{i}", [P, 512], F32)) for i in range(8)]
        self.full = [ctx.enter_context(nc.semaphore(f"bank{i}_filled")) for i in range(8)]
        self.free = [ctx.enter_context(nc.semaphore(f"bank{i}_emptied")) for i in range(8)]
        self.uses = [0] * 8
        self.where = {}

    def claim(self, key, bank):
        self.where[key] = (bank, self.uses[bank])
        self.uses[bank] += 1
        return self.ps[bank], self.uses[bank] > 1

    def before(self, key):
        bank, n = self.where[key]
        return self.free[bank], n

    def tensor(self, key):
        return self.ps[self.where[key][0]]

    def filled(self, key):
        bank, n = self.where[key]
        return self.full[bank], n + 1

    def emptied(self, key):
        bank, n = self.where[key]
        return self.free[bank], n + 1

    def fills(self, key):
        return self.full[self.where[key][0]]

    def empties(self, key):
        return self.free[self.where[key][0]]


def program(nc, a, out):
    ctx = ExitStack()
    with ctx:
        def sem(name):
            return ctx.enter_context(nc.semaphore(name))

        base = 16512
        top = [base]
        names = {}

        def place(name, shape, dt, at=None):
            size = 2 if dt in (BF16, F16) else 4
            n = size
            for s in shape[1:]:
                n *= s
            n = (n + 31) // 32 * 32
            off = top[0] if at is None else at[0]
            t = nc.alloc_sbuf_tensor_at(name, shape, dt, offset=off)
            if at is None:
                top[0] += n
            else:
                at[0] += n
            names[name] = (off, n)
            return t

        def place_both(name, shape, at=None):
            whole = place(f"{name}_whole", shape, F32, at)
            return whole, nc.alloc_sbuf_tensor_at(name, shape, F32R, offset=names[f"{name}_whole"][0])

        x = place("x", [P, TILES, D], F32)
        gate = place("gate", [P, TILES, D], F32)
        xn = [nc.alloc_sbuf_tensor_at(f"xn{i}", [P, D], F32, offset=names["gate"][0] + i * D * 4) for i in range(4)]
        ident = place("ident", [P, P], F32)
        ident_r = place("ident_r", [P, P], F32R)
        identb = place("identb", [P, P], BF16)
        mask = place("mask", [P, 2 * P], BF16)
        cosT = {l: place(f"cos{l}", [P, 2, HD], F32) for l in (0, 2, 3)}
        sinT = {l: place(f"sin{l}", [P, 2, HD], F32) for l in (0, 2, 3)}
        ones = place("ones", [P, P], F32)
        stats = place("stats", [P, TILES, 6], F32)
        moments = place("moments", [P, TILES, 2], F32)
        vareps = place("vareps", [P, TILES], F32)
        minus_half = place("minus_half", [P, TILES], F32)
        rstd = place("rstd", [P, TILES], F32)
        xT_hi = place("xT_hi", [P, KC, TILES * P], F32R)
        xT_whole = nc.alloc_sbuf_tensor_at("xT_whole", [P, KC, TILES * P], F32, offset=names["xT_hi"][0])
        Wqkv1 = place("Wqkv1", [P, KC, 2, 768], F32)
        Wqkv_hi = nc.alloc_sbuf_tensor_at("Wqkv_hi", [P, KC, 2, 384], F32R, offset=names["Wqkv1"][0])
        Wqkv_whole, Wqkv_lo = (nc.alloc_sbuf_tensor_at(n, [P, KC, 2, 384], dt, offset=names["Wqkv1"][0] + KC * 768 * 4)
                               for n, dt in (("Wqkv_whole", F32), ("Wqkv_lo", F32R)))
        compact0 = [nc.alloc_sbuf_tensor_at(f"compact{m}", [P, OCT, WIDTH0], F32,
                                            offset=names["Wqkv1"][0] + m * OCT * WIDTH0 * 4) for m in range(2)]
        assert 2 * OCT * WIDTH0 <= KC * 768
        Wo_whole, Wo_lo = place_both("Wo_lo", [P, KC, D])
        Vflat_shared = [place(f"Vs{i}", [P, 2 * 5 * CELL + 32 - CELL], F32) for i in range(4)]
        whole_from = top[0]
        Wo_hi = place("Wo_hi", [P, KC, D], F32R)
        xT_lo = place("xT_lo", [P, KC, TILES * P], F32R)
        shared = top[0]

        def attention_set(tag, shared_keys, start):
            at = [start]
            w = AttentionBuffers()
            kh = 4 if shared_keys else UH
            vh = kh + 1 if shared_keys else UH
            w.kn = kh if shared_keys else kh // 2
            w.vh = vh
            pair = range(2)
            w.qstack = [place(f"qstack{tag}{i}", [P, UH, 64], F32R, at) for i in pair]
            w.kstack = [place(f"kstack{tag}{i}", [P, w.kn, 4, 64], F32R, at) for i in pair]
            w.qk = [place(f"qk{tag}{i}", [P, UH + kh, HD], F32, at) for i in pair]
            if shared_keys:
                w.rc = [place(f"rope_cos{tag}{i}", [P, UH + kh, HD], F32, at) for i in pair]
                w.rs = [place(f"rope_sin{tag}{i}", [P, UH + kh, HD], F32, at) for i in pair]
                w.qkr = w.rc
            w.stacks_end = at[0]
            w.qT, w.kT = [], []
            for i in pair:
                w.qT.append(place(f"qT{tag}{i}", [P, UH // 2, SEQ], F32R, at))
                w.kT.append(place(f"kT{tag}{i}", [P, 2 * w.kn, SEQ], F32R, at))
                if i == 0:
                    w.early_end = at[0]
            if shared_keys:
                w.ctxT_lo = [place(f"ctxT_lo{tag}{i}", [P, KC, P], F32R, at) for i in pair]
            w.Vflat = Vflat_shared if shared_keys else \
                [place(f"V{tag}{i}", [P, 2 * vh * CELL + 32 - CELL], F32, at) for i in range(4)]
            w.V = [vf[:, 0:2 * vh * CELL].rearrange("p (t h c) -> p t h c", t=2, h=vh) for vf in w.Vflat]
            w.probs = [place(f"probs{tag}{i}", [P, 2, 4, SEQ], F32, at) for i in pair]
            w.pv = [place(f"pv{tag}{i}", [P, SEQ], F32, at) for i in pair]
            w.ctxr = [place(f"ctx{tag}{i}", [P, 2, D], F32, at) for i in pair]
            w.ctxT = [place(f"ctxT{tag}{i}", [P, KC, P], F32R if shared_keys else F32, at) for i in pair]
            w.negmax = [place(f"negmax{tag}{i}", [P, 2, UH], F32, at) for i in pair]
            w.negmaxT = [place(f"negmaxT{tag}{i}", [UH, SEQ], F32R, at) for i in pair]
            w.recip = [place(f"recip{tag}{i}", [P, 2, 4], F32, at) for i in pair]
            assert at[0] <= 229344, at[0]
            return w

        set_shared = attention_set("s", True, shared)
        set_whole = attention_set("w", False, whole_from)
        A = [set_shared if shared_keys else set_whole for shared_keys in GQA]

        SBUF_END = 229344
        hidden_from = SBUF_END - (2 + 2 * HBUFS) * 512 * 4
        at = [hidden_from]
        silu = [place(f"silu{i}", [P, 512], F32, at) for i in range(2)]
        h_hi = place("h_hi", [P, HBUFS, 512], F32R, at)
        h_whole, h_lo = place_both("h_lo", [P, HBUFS, 512], at)
        assert at[0] <= SBUF_END
        at = [shared]
        W0_whole, W0 = zip(place_both("Wgate0", [P, KC, HC0 * P], at), place_both("Wup0", [P, KC, HC0 * P], at),
                           place_both("Wdown0", [P, HC0, D], at))
        sign_in = place("sign_in", [P, KC, OCT], F32, at)
        sign_hid = place("sign_hid", [P, HC0, OCT], F32, at)
        maskf = place("maskf", [P, 2 * P], F32, at)
        absum = place("absum", [P, 3], F32, at)
        tscale = place("tscale", [P, 3], F32, at)
        tinv = place("tinv", [P, 3], F32, at)
        rounder = place("rounder", [P, 1], F32, at)
        assert at[0] <= hidden_from, at[0]
        at = [shared]
        x1_hi = place("x1_hi", [P, KC, TILES * P], F32R, at)
        W1q = place("W1q", [P, D], I32, at)
        zq = place("zq", [4, 64], I32, at)
        sh = place("sh", [4, D], F16, at)
        gidx = place("gidx", [4, D], I32, at)
        four = place("four", [4, 1], F32, at)
        bias1 = place("bias1", [1, D], F16, at)
        W1n = place("W1n", [P, KC, D], I32, at)
        zn = place("zn", [4, 64, 8], I32, at)
        zf = place("zf", [4, D], F32R, at)
        sf = place("sf", [4, D], F32R, at)
        onehot = place("onehot", [4, D], F32R, at)
        ones16 = place("ones16", [1, P], F16, at)
        assert at[0] <= set_shared.early_end
        W1f = [place(f"W1f{i}", [P, D], F32, at) for i in range(2)]
        W1h = place("W1h", [P, KC, D], F16, at)
        W1 = place("W1", [P, KC, D], F32R, at)
        assert at[0] <= hidden_from, at[0]
        at = [shared]
        s2 = place("block_scales", [P, HC2, 3 * KC], F32, at)
        W2_hi, W2_whole, W2_lo = [], [], []
        for i in range(W2BUFS):
            W2_hi.append(place(f"W2_hi{i}", [P, 3 * KC, P], F32R, at))
            whole, lo = place_both(f"W2_lo{i}", [P, 3 * KC, P], at)
            W2_whole.append(whole)
            W2_lo.append(lo)
            if i == 1:
                assert set_shared.stacks_end <= at[0] <= set_whole.early_end
        assert at[0] <= hidden_from, at[0]
        at = [shared]
        shapes3 = {"U1": [P, KC, P], "V1": [P, 2, HC3, P], "U2": [P, HC3, P], "V2": [P, D]}
        W3_hi, W3_whole, W3_lo = {}, {}, {}
        for n in ("U1", "V1"):
            W3_whole[n], W3_lo[n] = place_both(f"{n}_lo", shapes3[n], at)
            W3_hi[n] = place(f"{n}_hi", shapes3[n], F32R, at)
        assert at[0] >= set_shared.stacks_end
        for n in ("U2", "V2"):
            W3_whole[n], W3_lo[n] = place_both(f"{n}_lo", shapes3[n], at)
        b1 = place("b1", [P, 2, HC3], F32, at)
        b2 = place("b2", [P, D], F32, at)
        assert at[0] <= set_shared.early_end
        for n in ("U2", "V2"):
            W3_hi[n] = place(f"{n}_hi", shapes3[n], F32R, at)
        PT_hi, PT_lo = (place(f"PT_{n}", [P, 2, 512], F32R, at) for n in ("hi", "lo"))
        ZT_hi, ZT_lo = (place(f"ZT_{n}", [P, 2, 512], F32R, at) for n in ("hi", "lo"))
        outb = [place(f"outb{i}", [P, D], F32, at) for i in range(2)]
        assert at[0] <= hidden_from, at[0]

        splits3 = [("U1", slice(None)), ("V1", slice(0, 4)), ("U2", slice(None)), ("V1", slice(4, 8)),
                   ("V1", slice(8, HC3)), ("V2", slice(None))]

        def part3(W, i):
            name, chunks = splits3[i]
            return W[name][:, :, chunks, :] if name == "V1" else W[name][:]

        B = Banks(nc, ctx)
        x_in = [sem(f"x_loaded{i}") for i in range(SEQS)]
        ident_in = sem("identity_loaded")
        signs_in = sem("signs_loaded")
        const_in = sem("constants_loaded")
        att_in = sem("attention_weights_loaded")
        ffn_in = [sem(f"ffn_weights_loaded{i}") for i in range(3)]
        scales2_in = sem("block_scales_loaded")
        w2_in = [sem(f"ffn2_chunk_loaded{i}") for i in range(W2BUFS)]
        m_rows = [sem(f"max_rows_placed{i}") for i in range(2)]
        out_done = sem("output_stored")

        def mark(name, per_layer):
            return Mark(nc, ctx, name, per_layer)

        ones_set = mark("ones_set", [3, 0, 0, 0])
        mask_set = mark("mask_set", [3, 0, 0, 0])
        ln_stat = mark("row_stats", [TILES] * 4)
        ln_mom = mark("row_moments", [TILES] * 4)
        ln_var = mark("row_variance", [SEQS] * 4)
        ln_rstd = mark("row_rstd", [SEQS] * 4)
        xn_ready = mark("rows_normalised", [TILES] * 4)
        xT_high = mark("xT_high", [TILES] * 4)
        pieces0, need_gate_up, need_down, after_step = ternary_pieces()
        abs_summed = mark("weights_abs_summed", [3, 0, 0, 0])
        inverse_mean = mark("inverse_mean", [3, 0, 0, 0])
        tern_rounded = mark("ternary_rounded", [2 + HC0, 0, 0, 0])
        tern_clipped = mark("ternary_clipped", [2 + HC0, 0, 0, 0])
        padding_set = mark("padding_set", [2, 0, 0, 0])
        tern_ready = mark("ternary_ready", [len(pieces0), 0, 0, 0])
        deq = mark("dequant_steps", [0, 12 + 2 * KC, 0, 0])
        deq_done = mark("dequantised", [0, KC, 0, 0])
        w_scaled = mark("weights_scaled", [0, 0, 2 * HC2, 0])
        w_high = mark("weights_high", [0, 0, 2 * HC2, len(splits3)])
        w_low = mark("weights_low", [0, 0, 2 * HC2, len(splits3)])
        h_high = mark("hidden_high", [2 * HC0, 0, 2 * HC2, 2 * HC3])
        h_low = mark("hidden_low", [2 * HC0, 0, 2 * HC2, 2 * HC3])
        h_used = mark("hidden_used", [2 * (HC0 - 1), 0, 2 * (HC2 - 1), 2 * (HC3 - 1)])
        pz_high = mark("low_rank_high", [0, 0, 0, 4])
        att_high = mark("attention_weights_high", [2 * KC, 0, 2 * KC, 2 * KC])
        wqkv_low = mark("wqkv_low", [KC, 0, KC, KC])
        wo_low = mark("wo_low", [KC, 0, KC, KC])
        ctxT_high = mark("context_high", [TILES, 0, TILES, TILES])
        gate_ready = mark("gate_ready", [0, 0, 0, TILES])
        rope_part = mark("rope_parts", [48, 0, 48, 48])
        rope_done = mark("rope_done", [16, 0, 16, 16])
        HI = 3
        stack_hi = mark("stack_hi", [16 * HI] * 4)
        stack_lo = mark("stack_lo", [32] * 4)
        PADS = [2 * 4 + 4 * n for n in (4, 3, 0, 0)]
        pads = mark("pads_set", PADS)
        causal_cut = mark("causal_cut", [64, 0, 64, 64])
        rs_ready = mark("reciprocal_ready", [32] * 4)
        x_done = mark("x_updated", [TILES] * 4)

        last_out = {l: ("out", l, TILES - 1) for l in range(LAYERS)}

        def chunk_used(l, e):
            n, j = divmod(e, HIDDEN_CHUNKS[l])
            if j == HIDDEN_CHUNKS[l] - 1:
                return B.filled(("out", l, 4 * n + 3) if l != 3 else ("low2", n))
            return h_used.at(l, n * (HIDDEN_CHUNKS[l] - 1) + j + 1)

        def ternary_source(i):
            return compact0[i][:] if i < 2 else W0_whole[2][:, i - 2, :].rearrange("p (k o) -> p k o", k=OCT)

        def attention_weight_piece(p):
            return [W[:, p // 2] for W in ((Wqkv_hi, Wqkv_whole, Wqkv_lo) if p % 2 == 0 else (Wo_hi, Wo_whole, Wo_lo))]

        def stack_banks(l, half):
            return [("qT", half)] + ([("kT", half)] if GQA[l] else [("kT", 2 * half), ("kT", 2 * half + 1)])

        def key_slot(l, g, pair, par):
            return 2 * (g if GQA[l] else pair) + par

        block = ctx.enter_context(nc.Block())

        @block.tensor
        def _(pe):
            misc = [0]
            ring_s = [0]
            ring_t = [0]
            mm = nc.tensor.matmul

            def misc_bank():
                misc[0] += 1
                return 4 + misc[0] % 4

            def transposes(l, tiles, banks=None):
                for t in tiles:
                    key = ("xT", l, t)
                    ps, again = B.claim(key, misc_bank() if banks is None else banks[t % 2])
                    if again:
                        pe.wait_ge(*B.before(key))
                    pe.wait_ge(*xn_ready.at(l, t + 1))
                    for c in range(KC):
                        ins = nc.tensor.transpose(ps[:, c * P:(c + 1) * P], xn[t % 4][:, c * P:(c + 1) * P], ident[:])
                    ins.then_inc(B.fills(key), 1)

            def gate_up(l, e):
                n, j = divmod(e, HIDDEN_CHUNKS[l])
                tok = slice(n * 512, (n + 1) * 512)
                if l != 3 and j == 0:
                    pe.wait_ge(*B.emptied(("xT", l, 4 * n + 3)))
                if l == 0 and n == 0:
                    pe.wait_ge(*tern_ready.at(0, need_gate_up[j]))
                    if j == HC0 - 1:
                        pe.wait_ge(*padding_set.at(0, 2))
                if l == 2:
                    pe.wait_ge(*w_low.at(2, e + 1))
                if l == 3 and n == 0 and j % 4 == 0:
                    pe.wait_ge(*w_low.at(3, (2, 4, 5)[j // 4]))
                for which in range(2):
                    key = (("gate", "up")[which], l, n, j)
                    ps, again = B.claim(key, 2 * (e % 2) + which)
                    if again:
                        pe.wait_ge(*B.before(key))
                    terms = []
                    for c in range(KC):
                        hi, lo = xT_hi[:, c, tok], xT_lo[:, c, tok]
                        if l == 0:
                            w = W0[which][:, c, j * P:(j + 1) * P]
                            terms += [(w, hi), (w, lo)]
                        if l == 2:
                            w = W2_hi[e % W2BUFS][:, KC * which + c, :]
                            terms += [(w, hi), (w, lo), (W2_lo[e % W2BUFS][:, KC * which + c, :], hi)]
                    if l == 3:
                        w = W3_hi["V1"][:, which, j, :]
                        terms = [(w, PT_hi[:, n, :]), (w, PT_lo[:, n, :]), (W3_lo["V1"][:, which, j, :], PT_hi[:, n, :])]
                    for c, (lh, rh) in enumerate(terms):
                        ins = mm(ps[:], lh, rh, start=(c == 0), stop=(c == len(terms) - 1))
                    ins.then_inc(B.fills(key), 1)

            def down(l, e):
                C = HIDDEN_CHUNKS[l]
                n, j = divmod(e, C)
                pe.wait_ge(*h_low.at(l, e + 1))
                if l == 0 and n == 0:
                    pe.wait_ge(*tern_ready.at(0, need_down[j]))
                if l == 3 and e == 0:
                    pe.wait_ge(*w_low.at(3, 3))
                hh, hl = h_hi[:, e % HBUFS, :], h_lo[:, e % HBUFS, :]
                for t in range(4) if l != 3 else range(1):
                    tok = slice(t * P, (t + 1) * P)
                    if l == 3:
                        key, bank = ("low2", n), 4 + n
                        w = W3_hi["U2"][:, j, :]
                        terms = [(w, hh), (w, hl), (W3_lo["U2"][:, j, :], hh)]
                    else:
                        key, bank = ("out", l, 4 * n + t), 4 + t
                    if l == 0:
                        w = W0[2][:, j, :]
                        terms = [(hh[:, tok], w), (hl[:, tok], w)]
                    if l == 2:
                        w, wl = (y[e % W2BUFS][:, 2 * KC:3 * KC, :].rearrange("p n o -> p (n o)") for y in (W2_hi, W2_lo))
                        terms = [(hh[:, tok], w), (hh[:, tok], wl), (hl[:, tok], w)]
                    if j == 0:
                        B.claim(key, bank)
                        pe.wait_ge(*B.before(key))
                    for c, (lh, rh) in enumerate(terms):
                        ins = mm(B.tensor(key)[:], lh, rh, start=(j == 0 and c == 0), stop=(j == C - 1 and c == len(terms) - 1))
                    if j == C - 1:
                        ins.then_inc(B.fills(key), 1)
                if j != C - 1:
                    ins.then_inc(h_used.sem, 1)

            def out_tile(l, t, terms, bank):
                key = ("out", l, t)
                ps, again = B.claim(key, bank)
                pe.wait_ge(*B.before(key))
                for c, (lh, rh) in enumerate(terms):
                    ins = mm(ps[:], lh, rh, start=(c == 0), stop=(c == len(terms) - 1))
                ins.then_inc(B.fills(key), 1)

            def weight_sum(m):
                key = ("wsum", m)
                ps, again = B.claim(key, (0, 1, 4)[m])
                if again:
                    pe.wait_ge(*B.before(key))
                pe.wait_ge(*abs_summed.at(0, m + 1))
                mm(ps[:, 0:1], ones[:], absum[:, m:m + 1], start=True, stop=True).then_inc(B.fills(key), 1)

            def low_rank_in(n):
                key = ("low", n)
                ps, again = B.claim(key, n)
                pe.wait_ge(*B.before(key))
                pe.wait_ge(*B.emptied(("xT", 3, 4 * n + 3)))
                pe.wait_ge(*w_low.at(3, 1))
                tok = slice(n * 512, (n + 1) * 512)
                for c in range(KC):
                    terms = [(W3_hi["U1"], xT_hi), (W3_hi["U1"], xT_lo), (W3_lo["U1"], xT_hi)]
                    for k, (w, xs) in enumerate(terms):
                        ins = mm(ps[:], w[:, c, :], xs[:, c, tok], start=(c == 0 and k == 0), stop=(c == KC - 1 and k == 2))
                ins.then_inc(B.fills(key), 1)

            def low_rank_out(n):
                pe.wait_ge(*B.emptied(("low2", n)))
                pe.wait_ge(*w_low.at(3, len(splits3)))
                for t in range(4 * n, 4 * n + 4):
                    tok = slice((t % 4) * P, (t % 4 + 1) * P)
                    zh, zl = ZT_hi[:, n, tok], ZT_lo[:, n, tok]
                    out_tile(3, t, [(zh, W3_hi["V2"][:]), (zh, W3_lo["V2"][:]), (zl, W3_hi["V2"][:])], 6 + t % 2)

            def ffn(l):
                if l == 1:
                    pe.wait_ge(*deq.at(1, 12))
                    for c in range(KC):
                        for which, src in ((0, zf), (1, sf)):
                            key = ("group", c, which)
                            ps, again = B.claim(key, (2 * c + which) % 4)
                            pe.wait_ge(*B.before(key))
                            mm(ps[:], onehot[:, c * P:(c + 1) * P], src[:], start=True, stop=True).then_inc(B.fills(key), 1)
                        if c == 1:
                            transposes(l, LATE_TILES)
                    for t0 in (0, 4):
                        for c in range(KC):
                            for t in range(t0, t0 + 4):
                                key = ("out", l, t)
                                if c == 0:
                                    B.claim(key, 4 + t % 4)
                                    pe.wait_ge(*B.before(key))
                                    if t == t0:
                                        pe.wait_ge(*B.emptied(("xT", l, t0 + 3)))
                                if t == 0:
                                    pe.wait_ge(*deq_done.at(1, c + 1))
                                tok = slice(t * P, (t + 1) * P)
                                for xs in (x1_hi, xT_lo):
                                    ins = mm(B.tensor(key)[:], xs[:, c, tok], W1[:, c, :],
                                             start=(c == 0 and xs is x1_hi), stop=False)
                                if c == KC - 1:
                                    mm(B.tensor(key)[:], ones16[:], bias1[:], start=False, stop=True).then_inc(B.fills(key), 1)
                    return
                C = HIDDEN_CHUNKS[l]
                if l == 3:
                    low_rank_in(0)
                    transposes(l, LATE_TILES)
                    low_rank_in(1)
                for e in range(2 * C):
                    gate_up(l, e)
                    if l == 2 and e == 1:
                        transposes(l, LATE_TILES)
                    if l == 0 and e == 1:
                        weight_sum(2)
                    if l == 3 and e == C + LAG[3] + 1:
                        low_rank_out(0)
                    if e >= LAG[l]:
                        down(l, e - LAG[l])
                first = [(0, 0), (0, 1), (1, 0), (1, 1)]
                if LAG[l] == 1:
                    project(l, *first[0], bank=0)
                    project(l, *first[1], bank=1)
                for i, e in enumerate(range(2 * C - LAG[l], 2 * C)):
                    down(l, e)
                    if LAG[l] > 1:
                        project(l, *first[i], bank=(0, 1, 2)[i])
                for i in range(3 if LAG[l] > 1 else 2, 4):
                    project(l, *first[i], bank=(0, 1, 2, 3)[i])
                if l == 3:
                    low_rank_out(1)

            def project(l, u, tau, bank=None):
                t, hh = 2 * (u // 2) + tau, u % 2
                if u == 0 and tau == 0:
                    if GQA[l]:
                        pe.wait_ge(*wqkv_low.at(l, KC))
                    else:
                        pe.wait_ge(att_in, 32 * (l + 1))
                    pe.wait_ge(*mask_set.at(0, 3))
                for key, c0, width in ([(("qkv", l, u, tau), 0, 384)] if GQA[l] else
                                       [(("qkv", l, u, tau), 0, 512), (("v", l, u, tau), 512, 256)]):
                    ps, again = B.claim(key, misc_bank() if bank is None else bank)
                    pe.wait_ge(*B.before(key))
                    terms = []
                    for c in range(KC):
                        tok = slice(t * P, (t + 1) * P)
                        if GQA[l]:
                            wh, wl = Wqkv_hi[:, c, hh, :], Wqkv_lo[:, c, hh, :]
                            xh, xl = xT_hi[:, c, tok], xT_lo[:, c, tok]
                            terms += [(xh, wh), (xh, wl), (xl, wh)]
                        else:
                            terms += [(xT_whole[:, c, tok], Wqkv1[:, c, hh, c0:c0 + width])]
                    for c, (lh, rh) in enumerate(terms):
                        ins = mm(ps[:, 0:width], lh, rh, start=(c == 0), stop=(c == len(terms) - 1))
                    ins.then_inc(B.fills(key), 1)

            def turn_stacks(l, u, tau, half):
                i = 2 * u + tau
                if half == 0:
                    pe.wait_ge(*pads.at(l, PADS[l]))
                    pe.wait_ge(*stack_hi.at(l, HI * (i + 1)))
                    pe.wait_ge(*stack_lo.at(l, 2 * (i + 1)))
                for name, w in stack_banks(l, half):
                    flat = A[l].qstack[i % 2][:].rearrange("p h s -> p (h s)") if name == "qT" else \
                        A[l].kstack[i % 2][:].rearrange("p a h s -> p (a h s)")
                    key = (name, l, u, tau, w)
                    ps, again = B.claim(key, misc_bank())
                    pe.wait_ge(*B.before(key))
                    for p in range(4):
                        ins = nc.tensor.transpose(ps[:, p * P:(p + 1) * P].bitcast(F32R),
                                                  flat[:, (4 * w + p) * P:(4 * w + p + 1) * P], ident_r[:])
                    ins.then_inc(B.fills(key), 1)

            def scores_rows(l, gi, qb):
                u, g = divmod(gi, GROUPS)
                if g % 2 == 0 and qb == 0:
                    for tau in range(2):
                        for name, w in stack_banks(l, g // 2):
                            pe.wait_ge(*B.emptied((name, l, u, tau, w)))
                nk = (qb + 1) * P if CAUSAL[l] else SEQ
                for pl in range(2):
                    key = ("S", l, u, g, qb, pl)
                    ring_s[0] += 1
                    ps, again = B.claim(key, ring_s[0] % (2 if u > 0 else 4))
                    pe.wait_ge(*B.before(key))
                    slot = key_slot(l, g, 2 * g + pl, 0)
                    ins = mm(ps[:, 0:2 * nk].rearrange("p (h k) -> p h k", h=2),
                             A[l].qT[u % 2][:, 2 * g + pl, qb * P:(qb + 1) * P],
                             A[l].kT[u % 2][:, slot:slot + 2, 0:nk], start=True, stop=not CAUSAL[l])
                    if CAUSAL[l]:
                        dst = ps[:, 0:2 * nk].rearrange("p (h k) -> p h k", h=2)[:, :, nk - P:nk]
                        ins = mm(dst, identb[:], mask[:].rearrange("p (h k) -> p h k", h=2),
                                 start=False, stop=True)
                    ins.then_inc(B.fills(key), 1)

            def turn_max(l, u):
                key = ("mT", l, u)
                ps, again = B.claim(key, misc_bank())
                pe.wait_ge(*B.before(key))
                pe.wait_ge(*B.emptied(("S", l, u, GROUPS - 1, 1, 1)))
                for qb in range(2):
                    ins = nc.tensor.transpose(ps[0:UH, qb * P:(qb + 1) * P], A[l].negmax[u % 2][:, qb, :], ident[:])
                ins.then_inc(B.fills(key), 1)

            def scores_cols(l, u, g, kb):
                if g == 0 and kb == 0:
                    pe.wait_ge(m_rows[u % 2], 32 * (4 * l + u // 2 + 1))
                q0 = kb * P if CAUSAL[l] else 0
                nq = SEQ - q0
                for par in range(2):
                    key = ("ST", l, u, g, kb, par)
                    ring_t[0] += 1
                    ps, again = B.claim(key, 2 + ring_t[0] % 2 if u < UNITS - 1 or l + 1 < LAYERS else ring_t[0] % 4)
                    pe.wait_ge(*B.before(key))
                    for pairs in ((0, 2),) if GQA[l] else ((0, 1), (1, 2)):
                        n = pairs[1] - pairs[0]
                        ins = mm(ps[:, pairs[0] * nq:pairs[1] * nq].rearrange("p (h q) -> p h q", h=n),
                                 A[l].kT[u % 2][:, key_slot(l, g, 2 * g + pairs[0], par), kb * P:(kb + 1) * P],
                                 A[l].qT[u % 2][:, 2 * g + pairs[0]:2 * g + pairs[1], q0:SEQ], start=True, stop=True)
                    ins.then_inc(B.fills(key), 1)

            def weigh_values(l, gi):
                u, g = gi // GROUPS, gi % GROUPS
                key = ("PV", l, gi)
                ps, again = B.claim(key, misc_bank())
                pe.wait_ge(*B.before(key))
                if CAUSAL[l]:
                    pe.wait_ge(*causal_cut.at(l, 2 * (gi + 1)))
                else:
                    pe.wait_ge(*B.emptied(("ST", l, u, g, 1, 1)))
                for tau in range(2):
                    pe.wait_ge(*B.emptied(("qkv" if GQA[l] else "v", l, u, tau)))
                for kb in range(2):
                    q0 = kb * P if CAUSAL[l] else 0
                    for i in range(4):
                        kv = g if GQA[l] else 4 * g + i
                        ins = mm(ps[32 * i:32 * i + 32, q0:SEQ], A[l].Vflat[u % 4][:, (kb * A[l].vh + kv) * CELL:(kb * A[l].vh + kv) * CELL + 32],
                                 A[l].probs[gi % 2][:, kb, i, q0:SEQ],
                                 start=(kb == 0), stop=(kb == 1))
                ins.then_inc(B.fills(key), 1)

            def turn_context(l, gi):
                key = ("ctx", l, gi)
                ps, again = B.claim(key, misc_bank())
                pe.wait_ge(*B.before(key))
                pe.wait_ge(*B.emptied(("PV", l, gi)))
                for qb in range(2):
                    ins = nc.tensor.transpose(ps[:, qb * P:(qb + 1) * P], A[l].pv[gi % 2][:, qb * P:(qb + 1) * P], ident[:])
                ins.then_inc(B.fills(key), 1)

            def turn_rows(l, b):
                for tau in range(2):
                    key = ("ctxT", l, b, tau)
                    ps, again = B.claim(key, misc_bank())
                    pe.wait_ge(*B.before(key))
                    pe.wait_ge(*B.emptied(("ctx", l, 8 * b + 7)))
                    for c in range(KC):
                        ins = nc.tensor.transpose(ps[:, c * P:(c + 1) * P], A[l].ctxr[b % 2][:, tau, c * P:(c + 1) * P], ident[:])
                    ins.then_inc(B.fills(key), 1)

            def project_out(l, b):
                if GQA[l] and b == 0:
                    pe.wait_ge(*wo_low.at(l, KC))
                for tau in range(2):
                    key = ("O", l, b, tau)
                    ps, again = B.claim(key, misc_bank())
                    pe.wait_ge(*B.before(key))
                    pe.wait_ge(*B.emptied(("ctxT", l, b, tau)))
                    terms = []
                    for c in range(KC):
                        ch = A[l].ctxT[tau][:, c, :]
                        if GQA[l]:
                            wh, wl = Wo_hi[:, c, :], Wo_lo[:, c, :]
                            terms += [(ch, wh), (ch, wl), (A[l].ctxT_lo[tau][:, c, :], wh)]
                        else:
                            terms += [(ch, Wo_whole[:, c, :])]
                    for c, (lh, rh) in enumerate(terms):
                        ins = mm(ps[:], lh, rh, start=(c == 0), stop=(c == len(terms) - 1))
                    ins.then_inc(B.fills(key), 1)

            def attention(l):
                if not GQA[l]:
                    for u in range(2):
                        for tau in range(2):
                            project(l, u, tau)
                for half in range(2):
                    for tau in range(2):
                        turn_stacks(l, 0, tau, half)
                project(l, 2, 0)
                for gi in range(GROUPS):
                    for qb in range(2):
                        scores_rows(l, gi, qb)
                for tau in range(2):
                    turn_stacks(l, 1, tau, 0)
                turn_max(l, 0)
                for qb in range(2):
                    scores_rows(l, GROUPS, qb)
                for gi in range(GROUPS * UNITS):
                    u, g = divmod(gi, GROUPS)
                    ahead = gi + LEAD < GROUPS * UNITS
                    if g == 0 and u + 2 < UNITS:
                        project(l, u + 2, 1)
                    if g == 3 and u + 3 < UNITS:
                        project(l, u + 3, 0)
                    if g == 3 and u + 1 < UNITS:
                        turn_max(l, u + 1)
                    scores_cols(l, u, g, 0)
                    if g == 0 and u + 1 < UNITS:
                        turn_stacks(l, u + 1, 0, 1)
                    if g == 2 and u + 2 < UNITS:
                        turn_stacks(l, u + 2, 0, 0)
                    if ahead and g != 1:
                        scores_rows(l, gi + LEAD, 0)
                    if gi >= 1:
                        weigh_values(l, gi - 1)
                    if ahead and g == 1:
                        scores_rows(l, gi + LEAD, 0)
                    scores_cols(l, u, g, 1)
                    if g == 0 and u + 1 < UNITS:
                        turn_stacks(l, u + 1, 1, 1)
                    if g == 2 and u + 2 < UNITS:
                        turn_stacks(l, u + 2, 1, 0)
                    if ahead:
                        scores_rows(l, gi + LEAD, 1)
                    if gi >= 2:
                        turn_context(l, gi - 2)
                    if u % 2 == 0 and u > 0 and g == 2:
                        turn_rows(l, u // 2 - 1)
                    if u % 2 == 0 and u > 0 and g == 3:
                        project_out(l, u // 2 - 1)
                    if l + 1 < LAYERS and u == UNITS - 1 and g > 0:
                        transposes(l + 1, (2 * g - 2, 2 * g - 1), banks=(0, 1))
                weigh_values(l, 31)
                turn_context(l, 30)
                turn_context(l, 31)
                turn_rows(l, SEQS - 1)
                project_out(l, SEQS - 1)

            pe.wait_ge(ident_in, 16)
            transposes(0, range(6))
            weight_sum(0)
            weight_sum(1)
            transposes(0, (6, 7))
            for l in range(LAYERS):
                ffn(l)
                attention(l)

        @block.scalar
        def _(act):
            copy = ACT.Copy

            def split3(i):
                act.wait_ge(ffn_in[0], 16 * (1 + LOADS[1] + LOADS[3]))
                nc.scalar.activation(part3(W3_hi, i), part3(W3_whole, i), copy).then_inc(w_high.sem, 1)

            def transposes(l, tiles):
                for t in tiles:
                    key = ("xT", l, t)
                    act.wait_ge(*B.filled(key))
                    ps = B.tensor(key)[:].rearrange("p (c t) -> p c t", c=KC)
                    tok = slice(t * P, (t + 1) * P)
                    if l == 1:
                        nc.scalar.activation(xT_whole[:, :, tok], ps, copy)
                        nc.scalar.activation(x1_hi[:, :, tok], ps, copy).then_inc(xT_high.sem, 1)
                    else:
                        nc.scalar.activation(xT_hi[:, :, tok], ps, copy).then_inc(xT_high.sem, 1)

            def round_source(i):
                act.wait_ge(*inverse_mean.at(0, min(i, 2) + 1))
                w = ternary_source(i)
                nc.scalar.activation(w, w, ACT.Identity, bias=rounder[:, 0:1],
                                     scale=tinv[:, min(i, 2):min(i, 2) + 1]).then_inc(tern_rounded.sem, 1)

            def weights_high(e):
                act.wait_ge(*w_scaled.at(2, e + 1))
                nc.scalar.activation(W2_hi[e % W2BUFS][:], W2_whole[e % W2BUFS][:], copy).then_inc(w_high.sem, 1)

            def hidden(l, e):
                n, j = divmod(e, HIDDEN_CHUNKS[l])
                key = ("gate", l, n, j)
                act.wait_ge(*B.filled(key))
                if e >= 2:
                    act.wait_ge(*B.emptied(("up", l) + divmod(e - 2, HIDDEN_CHUNKS[l])))
                kw = {}
                if l == 0:
                    kw = {"scale": tscale[:, 0:1]}
                if l == 3:
                    kw = {"bias": b1[:, 0, j:j + 1]}
                nc.scalar.activation(silu[e % 2][:], B.tensor(key)[:], ACT.Silu, **kw).then_inc(B.empties(key), 1)
                if l != 3:
                    hidden_high(l, e)
                elif e > 0:
                    hidden_high(l, e - 1)

            def hidden_high(l, e):
                act.wait_ge(*B.emptied(("up", l) + divmod(e, HIDDEN_CHUNKS[l])))
                nc.scalar.activation(h_hi[:, e % HBUFS, :], h_whole[:, e % HBUFS, :], copy).then_inc(h_high.sem, 1)

            def out_tiles(l, n):
                for t in range(4 * n, 4 * n + 4):
                    key = ("out", l, t)
                    if l == 3:
                        act.wait_ge(*B.emptied(key))
                        nc.scalar.activation(gate[:, t, :], outb[t % 2][:], ACT.Silu).then_inc(gate_ready.sem, 1)
                        continue
                    act.wait_ge(*B.filled(key))
                    kw = {"scale": tscale[:, 2:3]} if l == 0 else {}
                    nc.scalar.activation(gate[:, t, :], B.tensor(key)[:], ACT.Silu, **kw).then_inc(B.empties(key), 1)

            def low_rank_high(key, dst):
                act.wait_ge(*B.filled(key))
                nc.scalar.activation(dst, B.tensor(key)[:], copy).then_inc(pz_high.sem, 1)

            def ffn(l):
                if l == 1:
                    transposes(l, LATE_TILES)
                    out_tiles(l, 0)
                    out_tiles(l, 1)
                    return
                C = HIDDEN_CHUNKS[l]
                if l == 3:
                    split3(2)
                    low_rank_high(("low", 0), PT_hi[:, 0, :])
                    split3(3)
                    transposes(l, LATE_TILES)
                    low_rank_high(("low", 1), PT_hi[:, 1, :])
                for e in range(2 * C):
                    if l == 0 and e + 2 < C + LAG[0]:
                        for m, j in pieces0[after_step[e + 1]:after_step[e + 2]]:
                            if m == 2:
                                round_source(2 + j)
                    if l == 2 and e + 2 < 2 * C:
                        weights_high(e + 2)
                    if l == 3 and e in (0, 1):
                        split3(4 + e)
                    hidden(l, e)
                    if l == 2 and e == 0:
                        transposes(l, LATE_TILES)
                    if e == C - 1 + LAG[l]:
                        if l == 3:
                            low_rank_high(("low2", 0), ZT_hi[:, 0, :])
                        else:
                            out_tiles(l, 0)
                    if l == 3 and e == C + LAG[3]:
                        out_tiles(3, 0)
                    if C < e <= C + 2 * KC:
                        if e == C + 1:
                            act.wait_ge(att_in, 32 * (l + 1))
                        hi, whole, lo = attention_weight_piece(e - C - 1)
                        nc.scalar.activation(hi, whole, copy).then_inc(att_high.sem, 1)
                if l == 3:
                    hidden_high(l, 2 * C - 1)
                act.wait_ge(*B.filled(("up", l, 1, C - 1)))
                for tau in range(2):
                    take_projection(l, 0, tau)
                if l == 3:
                    low_rank_high(("low2", 1), ZT_hi[:, 1, :])
                for tau in range(2):
                    stack_high(l, 0, tau)
                out_tiles(l, 1)

            def take_projection(l, u, tau):
                i = 2 * u + tau
                key = ("qkv", l, u, tau)
                ps = B.tensor(key)
                nqk = 20 if GQA[l] else 32
                act.wait_ge(*B.filled(key))
                if i >= 2 and GQA[l]:
                    act.wait_ge(*rope_part.at(l, 3 * (i - 1)))
                if i >= 2 and not GQA[l]:
                    act.wait_ge(*stack_lo.at(l, 2 * (i - 1)))
                ins = nc.scalar.activation(A[l].qk[i % 2][:, 0:nqk, :], ps[:, 0:nqk * HD].rearrange("p (h d) -> p h d", d=HD), copy)
                if GQA[l]:
                    nc.scalar.activation(A[l].V[u % 4][:, tau, 0:4, 0:HD], ps[:, 320:384].rearrange("p (h d) -> p h d", d=HD),
                                         copy).then_inc(B.empties(key), 1)
                else:
                    ins.then_inc(B.empties(key), 1)
                    key = ("v", l, u, tau)
                    act.wait_ge(*B.filled(key))
                    nc.scalar.activation(A[l].V[u % 4][:, tau, :, 0:HD],
                                         B.tensor(key)[:, 0:256].rearrange("p (h d) -> p h d", d=HD),
                                         copy).then_inc(B.empties(key), 1)

            def stack_high(l, u, tau):
                i = 2 * u + tau
                if ROPE[l]:
                    act.wait_ge(*rope_done.at(l, i + 1))
                    src = A[l].qkr[i % 2]
                else:
                    act.wait_ge(*B.emptied(("qkv", l, u, tau)))
                    src = A[l].qk[i % 2]
                qs = A[l].qstack[i % 2][:]
                ks = A[l].kstack[i % 2][:]
                if i >= 2:
                    for name, w in stack_banks(l, 1):
                        act.wait_ge(*B.filled((name, l, u - 1, tau, w)))
                dst = qs[:, :, 0:48].rearrange("p h (s d) -> p h s d", d=SPLIT)[:, :, 0:3:2, :]
                nc.scalar.activation(dst, src[:, 0:UH, :].unsqueeze(2).to_broadcast([P, UH, 2, HD]), copy).then_inc(stack_hi.sem, 1)
                for par in range(2):
                    n = 4 if GQA[l] else 8
                    kd = ks[:, 0:n, 3 * par, 0:32].rearrange("p n (s d) -> p n s d", d=SPLIT)
                    kv = src[:, UH:UH + 4, :] if GQA[l] else src[:, UH + par:2 * UH:2, :]
                    nc.scalar.activation(kd, kv.unsqueeze(2).to_broadcast([P, n, 2, HD]), copy).then_inc(stack_hi.sem, 1)

            def take_stacks(l, u, tau, half):
                key = ("qT", l, u, tau, half)
                act.wait_ge(*B.filled(key))
                nc.scalar.activation(A[l].qT[u % 2][:, 4 * half:4 * half + 4, tau * P:(tau + 1) * P],
                                     B.tensor(key)[:].rearrange("p (a t) -> p a t", a=4), copy).then_inc(B.empties(key), 1)

            def exponentials(l, u, g, kb):
                gi = GROUPS * u + g
                if gi >= 2:
                    act.wait_ge(*B.filled(("PV", l, gi - 2)))
                q0 = kb * P if CAUSAL[l] else 0
                nq = SEQ - q0
                for par in range(2):
                    key = ("ST", l, u, g, kb, par)
                    act.wait_ge(*B.filled(key))
                    nc.scalar.activation(A[l].probs[gi % 2][:, kb, par:4:2, q0:SEQ],
                                         B.tensor(key)[:, 0:2 * nq].rearrange("p (h q) -> p h q", h=2),
                                         ACT.Exp, scale=0.25).then_inc(B.empties(key), 1)

            def take_pv(l, gi):
                key = ("PV", l, gi)
                act.wait_ge(*B.filled(key))
                nc.scalar.activation(A[l].pv[gi % 2][:], B.tensor(key)[:, 0:SEQ], copy).then_inc(B.empties(key), 1)

            def take_rows(l, b):
                for tau in range(2):
                    key = ("ctxT", l, b, tau)
                    act.wait_ge(*B.filled(key))
                    nc.scalar.activation(A[l].ctxT[tau][:].rearrange("p c t -> p (c t)"), B.tensor(key)[:],
                                         copy).then_inc(ctxT_high.sem if GQA[l] else B.empties(key), 1)

            def attention(l):
                act.wait_ge(*(B.emptied(last_out[l]) if l != 3 else gate_ready.at(3, TILES)))
                if not GQA[l]:
                    for tau in range(2):
                        take_projection(l, 0, tau)
                    for tau in range(2):
                        stack_high(l, 0, tau)
                for tau in range(2):
                    take_projection(l, 1, tau)
                for half in range(2):
                    for tau in range(2):
                        take_stacks(l, 0, tau, half)
                for tau in range(2):
                    stack_high(l, 1, tau)
                take_projection(l, 2, 0)
                for tau in range(2):
                    take_stacks(l, 1, tau, 0)
                for gi in range(GROUPS * UNITS):
                    u, g = divmod(gi, GROUPS)
                    if g == 0 and u + 2 < UNITS:
                        take_projection(l, u + 2, 1)
                    if g == 3 and u + 3 < UNITS:
                        take_projection(l, u + 3, 0)
                    exponentials(l, u, g, 0)
                    if g == 0 and u + 1 < UNITS:
                        take_stacks(l, u + 1, 0, 1)
                    if g == 2 and u + 2 < UNITS:
                        take_stacks(l, u + 2, 0, 0)
                    if gi >= 1:
                        take_pv(l, gi - 1)
                    exponentials(l, u, g, 1)
                    if g == 0 and u + 1 < UNITS:
                        take_stacks(l, u + 1, 1, 1)
                    if g == 2 and u + 2 < UNITS:
                        take_stacks(l, u + 2, 1, 0)
                    if g < 2 and u + 2 < UNITS:
                        stack_high(l, u + 2, g)
                    if u % 2 == 0 and u > 0 and g == 2:
                        take_rows(l, u // 2 - 1)
                    if l + 1 < LAYERS and u == UNITS - 1 and g > 0:
                        transposes(l + 1, (2 * g - 2, 2 * g - 1))
                if l + 1 == 2:
                    weights_high(0)
                    weights_high(1)
                if l + 1 == 3:
                    split3(0)
                    split3(1)
                take_pv(l, 31)
                take_rows(l, SEQS - 1)

            act.wait_ge(*ones_set.at(0, 3))
            transposes(0, range(6))
            round_source(0)
            round_source(1)
            transposes(0, (6, 7))
            for l in range(LAYERS):
                ffn(l)
                attention(l)

        @block.vector
        def _(dve):
            v = nc.vector

            def row_statistics(l, b):
                for t in (2 * b, 2 * b + 1):
                    if l == 0:
                        dve.wait_ge(x_in[b], 16)
                    else:
                        dve.wait_ge(*x_done.at(l - 1, t + 1))
                    v.bn_stats(stats[:, t, :], x[:, t, :]).then_inc(ln_stat.sem, 1)
                for t in (2 * b, 2 * b + 1):
                    dve.wait_ge(*ln_stat.at(l, t + 1))
                    v.bn_aggr(moments[:, t, :], stats[:, t, :]).then_inc(ln_mom.sem, 1)
                dve.wait_ge(*ln_mom.at(l, 2 * b + 2))
                v.tensor_scalar(vareps[:, 2 * b:2 * b + 2], moments[:, 2 * b:2 * b + 2, 1], EPS, None,
                                ALU.add).then_inc(ln_var.sem, 1)

            def normalise_next(l, gi):
                u, g = divmod(gi, GROUPS)
                if u == UNITS - 1 and g < 2:
                    for b in ((0, 1), (2,))[g]:
                        row_statistics(l, b)
                if u == UNITS - 1 and g > 0:
                    transposed_low(l, g - 1)

            def transposed_low(l, b):
                for t in (2 * b, 2 * b + 1):
                    key = ("xT", l, t)
                    tok = slice(t * P, (t + 1) * P)
                    high = (x1_hi if l == 1 else xT_hi)[:, :, tok].bitcast(F32)
                    dve.wait_ge(*xT_high.at(l, t + 1))
                    v.tensor_tensor(xT_lo[:, :, tok], B.tensor(key)[:].rearrange("p (c t) -> p c t", c=KC), high,
                                    ALU.subtract).then_inc(B.empties(key), 1)

            def scale_rows(l, b):
                dve.wait_ge(*ln_rstd.at(l, b + 1))
                for t in (2 * b, 2 * b + 1):
                    if t >= 4:
                        dve.wait_ge(*B.filled(("xT", l, t - 4)))
                    dst, src = xn[t % 4][:], x[:, t, :]
                    if l == 1:
                        dst = xn[t % 4][:].rearrange("p (s r) -> p r s", s=8)
                        src = x[:, t, :].rearrange("p (r s) -> p r s", s=8)
                    v.tensor_scalar(dst, src, moments[:, t, 0:1], rstd[:, t:t + 1], ALU.subtract,
                                    ALU.mult).then_inc(xn_ready.sem, 1)

            def weight_mean(m):
                key = ("wsum", m)
                dve.wait_ge(*B.filled(key))
                copies = 1 if m == 2 else 2
                ins = v.tensor_scalar(tscale[:, m:m + 1], B.tensor(key)[:, 0:1], 1.0 / (copies * HID0 * D // OCT), None, ALU.mult)
                ins.then_inc(B.empties(key), 1)
                dve.wait_ge(*B.emptied(key))
                v.reciprocal(tinv[:, m:m + 1], tscale[:, m:m + 1]).then_inc(inverse_mean.sem, 1)

            def weight_sum(m):
                dve.wait_ge(ffn_in[m], 16)
                W = compact0[m][:] if m < 2 else W0_whole[2][:, :, 0:D // OCT]
                v.tensor_reduce(absum[:, m:m + 1], W, AX.XY, ALU.add,
                                apply_absolute_value=True).then_inc(abs_summed.sem, 1)

            def clip_source(i):
                dve.wait_ge(*tern_rounded.at(0, i + 1))
                w = ternary_source(i)
                v.tensor_scalar(w, w, ROUND - 1.0, ROUND + 1.0, ALU.max, ALU.min).then_inc(tern_clipped.sem, 1)

            def ternary(i0, i1):
                for m, k in pieces0[i0:i1]:
                    if m == 2:
                        clip_source(2 + k)
                for m, k in pieces0[i0:i1]:
                    dve.wait_ge(*tern_clipped.at(0, m + 1 if m < 2 else 3 + k))
                    if m == 2:
                        w = ternary_source(2 + k)
                        v.scalar_tensor_tensor(W0[2][:, k, :].rearrange("p (k o) -> p k o", k=OCT), w, ROUND,
                                               sign_hid[:, k, :].unsqueeze(2).to_broadcast(list(w.shape)),
                                               ALU.subtract, ALU.mult).then_inc(tern_ready.sem, 1)
                        continue
                    for c in range(KC):
                        j = 2 * (c ^ k)
                        dst = W0[m][:, c, 2 * k * WIDTH0:(2 * k + 2) * WIDTH0].rearrange("p (k o) -> p k o", k=2)
                        ins = v.scalar_tensor_tensor(dst, compact0[m][:, j:j + 2, :], ROUND,
                                                     sign_in[:, c, 2 * k:2 * k + 2].unsqueeze(2).to_broadcast([P, 2, WIDTH0]),
                                                     ALU.subtract, ALU.mult)
                    ins.then_inc(tern_ready.sem, 1)

            def unpack():
                steps = [0]

                def step(ins):
                    steps[0] += 1
                    ins.then_inc(deq.sem, 1)

                dve.wait_ge(ffn_in[0], 16 * (1 + LOADS[1]))
                for s in range(8):
                    step(v.tensor_scalar(zn[:, :, s], zq[:], 4 * s, 15, ALU.logical_shift_right, ALU.bitwise_and))
                dve.wait_ge(*deq.at(1, steps[0]))
                step(v.tensor_scalar(zf[:], zn[:].rearrange("g c s -> g (c s)"), 1.0, None, ALU.add))
                step(v.tensor_copy(sf[:], sh[:]))
                step(v.tensor_scalar(onehot[:], gidx[:], four[:, 0:1], None, ALU.is_equal))
                step(v.memset(ones16[:], 1.0))
                for c in range(KC):
                    for half in range(2):
                        r = slice(64 * half, 64 * half + 64)
                        step(v.tensor_scalar(W1n[r, c, :], W1q[r, :], 4 * (2 * c + half), 15,
                                             ALU.logical_shift_right, ALU.bitwise_and))

            def dequantise(c):
                kz, ks = ("group", c, 0), ("group", c, 1)
                dve.wait_ge(*deq.at(1, 12 + 2 * KC))
                dve.wait_ge(*B.filled(kz))
                v.tensor_tensor(W1f[c % 2][:], W1n[:, c, :], B.tensor(kz)[:], ALU.subtract).then_inc(B.empties(kz), 1)
                dve.wait_ge(*B.emptied(kz))
                dve.wait_ge(*B.filled(ks))
                v.tensor_tensor(W1h[:, c, :], W1f[c % 2][:], B.tensor(ks)[:], ALU.mult).then_inc(B.empties(ks), 1)
                dve.wait_ge(*B.emptied(ks))
                v.tensor_copy(W1[:, c, :], W1h[:, c, :]).then_inc(deq_done.sem, 1)

            def scale_weights(e):
                dve.wait_ge(w2_in[e % W2BUFS], 16 * (e // W2BUFS + 1))
                if e == 0:
                    dve.wait_ge(scales2_in, 16)
                w = W2_whole[e % W2BUFS][:]
                v.tensor_tensor(w, w, s2[:, e % HC2, :].unsqueeze(2).to_broadcast([P, 3 * KC, P]),
                                ALU.mult).then_inc(w_scaled.sem, 1)

            def hidden(l, e):
                n, j = divmod(e, HIDDEN_CHUNKS[l])
                key = ("up", l, n, j)
                dve.wait_ge(*B.emptied(("gate", l, n, j)))
                dve.wait_ge(*B.filled(key))
                if e >= HBUFS:
                    dve.wait_ge(*chunk_used(l, e - HBUFS))
                ps, h = B.tensor(key)[:], h_whole[:, e % HBUFS, :]
                if l == 0:
                    ins = v.scalar_tensor_tensor(h, ps, tscale[:, 1:2], silu[e % 2][:], ALU.mult, ALU.mult)
                elif l == 3:
                    ins = v.scalar_tensor_tensor(h, ps, b1[:, 1, j:j + 1], silu[e % 2][:], ALU.add, ALU.mult)
                else:
                    ins = v.tensor_tensor(h, ps, silu[e % 2][:], ALU.mult)
                ins.then_inc(B.empties(key), 1)
                if l != 3:
                    dve.wait_ge(*h_high.at(l, e + 1))
                    v.tensor_tensor(h_lo[:, e % HBUFS, :], h, h_hi[:, e % HBUFS, :].bitcast(F32),
                                    ALU.subtract).then_inc(h_low.sem, 1)

            def low_rank_low(i, key, high, dst):
                dve.wait_ge(*pz_high.at(3, i + 1))
                v.tensor_tensor(dst, B.tensor(key)[:], high.bitcast(F32), ALU.subtract).then_inc(B.empties(key), 1)

            def add_bias(n):
                for t in range(4 * n, 4 * n + 4):
                    key = ("out", 3, t)
                    dve.wait_ge(*B.filled(key))
                    if t >= 2:
                        dve.wait_ge(*gate_ready.at(3, t - 1))
                    v.tensor_tensor(outb[t % 2][:], B.tensor(key)[:], b2[:], ALU.add).then_inc(B.empties(key), 1)

            def ffn(l):
                C = HIDDEN_CHUNKS[l]
                if l == 0:
                    clip_source(0)
                    clip_source(1)
                    dve.wait_ge(signs_in, 32)
                    ternary(0, after_step[1])
                    transposed_low(0, 2)
                    transposed_low(0, 3)
                if l == 3:
                    low_rank_low(0, ("low", 0), PT_hi[:, 0, :], PT_lo[:, 0, :])
                    transposed_low(l, SEQS - 1)
                    low_rank_low(1, ("low", 1), PT_hi[:, 1, :], PT_lo[:, 1, :])
                for e in range(2 * C):
                    if l == 0 and e == 1:
                        weight_sum(2)
                        weight_mean(2)
                    if l == 0 and e == 2:
                        dve.wait_ge(const_in, 16 * CONSTS)
                        v.tensor_copy(identb[:], ident[:]).then_inc(mask_set.sem, 1)
                        v.tensor_copy(ident_r[:], ident[:]).then_inc(mask_set.sem, 1)
                        v.tensor_copy(mask[:], maskf[:]).then_inc(mask_set.sem, 1)
                    if l == 0 and e + 2 < C + LAG[0]:
                        ternary(after_step[e + 1], after_step[e + 2])
                    if l == 2 and e + 2 < 2 * C:
                        scale_weights(e + 2)
                    hidden(l, e)
                    if l == 2 and e == 0:
                        transposed_low(l, SEQS - 1)
                    if l == 3 and e == C - 1 + LAG[3]:
                        low_rank_low(2, ("low2", 0), ZT_hi[:, 0, :], ZT_lo[:, 0, :])
                    if l == 3 and e == C + LAG[3]:
                        add_bias(0)
                    p = e - C - 2
                    if 0 <= p < 2 * KC and p % 2 == 0:
                        hi, whole, lo = attention_weight_piece(p)
                        dve.wait_ge(*att_high.at(l, p + 1))
                        v.tensor_tensor(lo, whole, hi.bitcast(F32), ALU.subtract).then_inc(wqkv_low.sem, 1)
                rope(l, 0, 0)
                if l == 3:
                    low_rank_low(3, ("low2", 1), ZT_hi[:, 1, :], ZT_lo[:, 1, :])
                rope(l, 0, 1)
                if l == 3:
                    add_bias(1)

            def context_low(l, b):
                for tau in range(2):
                    key = ("ctxT", l, b, tau)
                    dve.wait_ge(*ctxT_high.at(l, 2 * b + tau + 1))
                    v.tensor_tensor(A[l].ctxT_lo[tau][:].rearrange("p c t -> p (c t)"), B.tensor(key)[:],
                                    A[l].ctxT[tau][:].bitcast(F32).rearrange("p c t -> p (c t)"),
                                    ALU.subtract).then_inc(B.empties(key), 1)

            def rope(l, u, tau):
                i = 2 * u + tau
                dve.wait_ge(*B.emptied(("qkv", l, u, tau)))
                if i >= 2:
                    dve.wait_ge(*rope_done.at(l, i - 1))
                    dve.wait_ge(*stack_hi.at(l, HI * (i - 1)))
                    dve.wait_ge(*stack_lo.at(l, 2 * (i - 1)))
                src, tc, ts = A[l].qk[i % 2], A[l].rc[i % 2], A[l].rs[i % 2]
                half = HD // 2
                v.tensor_tensor(tc[:], src[:, 0:20, :], cosT[l][:, tau, :].unsqueeze(1).to_broadcast([P, 20, HD]),
                                ALU.mult).then_inc(rope_part.sem, 1)
                v.tensor_tensor(ts[:, :, 0:half], src[:, 0:20, half:HD],
                                sinT[l][:, tau, 0:half].unsqueeze(1).to_broadcast([P, 20, half]), ALU.mult).then_inc(rope_part.sem, 1)
                v.tensor_tensor(ts[:, :, half:HD], src[:, 0:20, 0:half],
                                sinT[l][:, tau, half:HD].unsqueeze(1).to_broadcast([P, 20, half]), ALU.mult).then_inc(rope_part.sem, 1)
                dve.wait_ge(*rope_part.at(l, 3 * (i + 1)))
                v.tensor_tensor(A[l].qkr[i % 2][:], tc[:], ts[:], ALU.add).then_inc(rope_done.sem, 1)

            def row_max(l, gi, qb):
                u, g = divmod(gi, GROUPS)
                nk = (qb + 1) * P if CAUSAL[l] else SEQ
                for pl in range(2):
                    key = ("S", l, u, g, qb, pl)
                    dve.wait_ge(*B.filled(key))
                    v.tensor_reduce(A[l].negmax[u % 2][:, qb, 2 * g + pl:2 * g + pl + 9:8],
                                    B.tensor(key)[:, 0:2 * nk].rearrange("p (h k) -> p h k", h=2),
                                    AX.X, ALU.max, negate=True).then_inc(B.empties(key), 1)

            def take_key_stacks(l, u, tau, half):
                for name, w in stack_banks(l, half)[1:]:
                    key = (name, l, u, tau, w)
                    dve.wait_ge(*B.filled(key))
                    v.tensor_copy(A[l].kT[u % 2][:, 4 * w:4 * w + 4, tau * P:(tau + 1) * P],
                                  B.tensor(key)[:].rearrange("p (a t) -> p a t", a=4)).then_inc(B.empties(key), 1)

            def take_max(l, u):
                key = ("mT", l, u)
                dve.wait_ge(*B.filled(key))
                v.tensor_copy(A[l].negmaxT[u % 2][:], B.tensor(key)[0:UH, 0:SEQ]).then_inc(B.empties(key), 1)

            def context(l, gi):
                u, g = gi // GROUPS, gi % GROUPS
                b, hh = u // 2, u % 2
                key = ("ctx", l, gi)
                dve.wait_ge(*B.filled(key))
                ps = B.tensor(key)[:, 0:2 * P].rearrange("p (q i r) -> p q i r", q=2, i=4)
                if gi >= 2:
                    dve.wait_ge(*B.emptied(("ctx", l, gi - 2)))
                v.reciprocal(A[l].recip[gi % 2][:], ps[:, :, :, HD]).then_inc(rs_ready.sem, 1)
                dve.wait_ge(*rs_ready.at(l, gi + 1))
                c0 = (UH * hh + 4 * g) * HD
                v.tensor_tensor(A[l].ctxr[b % 2][:, :, c0:c0 + 4 * HD].rearrange("p q (i d) -> p q i d", i=4), ps[:, :, :, 0:HD],
                                A[l].recip[gi % 2][:].unsqueeze(3).to_broadcast([P, 2, 4, HD]), ALU.mult).then_inc(B.empties(key), 1)

            def residual(l, b):
                for tau in range(2):
                    t = 2 * b + tau
                    key = ("O", l, b, tau)
                    dve.wait_ge(*B.filled(key))
                    v.tensor_tensor(A[l].ctxr[b % 2][:, tau, :], B.tensor(key)[:], gate[:, t, :], ALU.mult).then_inc(B.empties(key), 1)
                    dve.wait_ge(*B.emptied(key))
                    v.tensor_tensor(x[:, t, :], x[:, t, :], A[l].ctxr[b % 2][:, tau, :], ALU.add).then_inc(x_done.sem, 1)

            def attention(l):
                dve.wait_ge(*(B.emptied(last_out[l]) if l != 3 else gate_ready.at(3, TILES)))
                if ROPE[l]:
                    for tau in range(2):
                        rope(l, 1, tau)
                for half in range(2):
                    for tau in range(2):
                        take_key_stacks(l, 0, tau, half)
                for gi in range(GROUPS):
                    for qb in range(2):
                        row_max(l, gi, qb)
                for tau in range(2):
                    take_key_stacks(l, 1, tau, 0)
                take_max(l, 0)
                for qb in range(2):
                    row_max(l, GROUPS, qb)
                if ROPE[l]:
                    rope(l, 2, 0)
                for gi in range(GROUPS * UNITS):
                    u, g = divmod(gi, GROUPS)
                    ahead = gi + LEAD < GROUPS * UNITS
                    if l + 1 < LAYERS and u == UNITS - 1 and g > 0:
                        scale_rows(l + 1, g - 1)
                    if g == 3 and u + 1 < UNITS:
                        take_max(l, u + 1)
                    if g == 0 and u + 1 < UNITS:
                        take_key_stacks(l, u + 1, 0, 1)
                    if g == 2 and u + 2 < UNITS:
                        take_key_stacks(l, u + 2, 0, 0)
                    if ahead:
                        row_max(l, gi + LEAD, 0)
                    if ROPE[l] and g == 0 and u + 2 < UNITS:
                        rope(l, u + 2, 1)
                    if ROPE[l] and g == 3 and u + 3 < UNITS:
                        rope(l, u + 3, 0)
                    if g == 0 and u + 1 < UNITS:
                        take_key_stacks(l, u + 1, 1, 1)
                    if g == 2 and u + 2 < UNITS:
                        take_key_stacks(l, u + 2, 1, 0)
                    if ahead:
                        row_max(l, gi + LEAD, 1)
                    if gi >= 2:
                        context(l, gi - 2)
                    if GQA[l] and u % 2 == 0 and u > 0 and g == 2:
                        context_low(l, u // 2 - 1)
                    if u % 2 == 0 and u > 0 and g == 3:
                        residual(l, u // 2 - 1)
                    if l + 1 < LAYERS:
                        normalise_next(l + 1, gi)
                if l + 1 == 2:
                    scale_weights(0)
                    scale_weights(1)
                if l + 1 == 1:
                    unpack()
                context(l, 30)
                context(l, 31)
                if GQA[l]:
                    context_low(l, SEQS - 1)
                residual(l, SEQS - 1)

            v.memset(ones[:], 1.0).then_inc(ones_set.sem, 1)
            v.memset(minus_half[:], -0.5).then_inc(ones_set.sem, 1)
            v.memset(rounder[:], ROUND).then_inc(ones_set.sem, 1)
            row_statistics(0, 0)
            row_statistics(0, 1)
            scale_rows(0, 0)
            row_statistics(0, 2)
            scale_rows(0, 1)
            transposed_low(0, 0)
            row_statistics(0, 3)
            weight_sum(0)
            scale_rows(0, 2)
            weight_sum(1)
            transposed_low(0, 1)
            weight_mean(0)
            weight_mean(1)
            scale_rows(0, 3)
            for l in range(LAYERS):
                if l > 0:
                    row_statistics(l, SEQS - 1)
                    scale_rows(l, SEQS - 1)
                if l == 1:
                    dequantise(0)
                    transposed_low(l, SEQS - 1)
                    for c in range(1, KC):
                        dequantise(c)
                else:
                    ffn(l)
                attention(l)

        @block.gpsimd
        def _(pool):
            gp = nc.gpsimd

            def inverse_deviation(l, b):
                pool.wait_ge(*ln_var.at(l, b + 1))
                gp.tensor_tensor(rstd[:, 2 * b:2 * b + 2], vareps[:, 2 * b:2 * b + 2], minus_half[:, 0:2],
                                 ALU.pow).then_inc(ln_rstd.sem, 1)

            def weights_low(l, i):
                pool.wait_ge(*w_high.at(l, i + 1))
                if l == 2:
                    hi, whole, lo = (W[i % W2BUFS][:] for W in (W2_hi, W2_whole, W2_lo))
                else:
                    hi, whole, lo = (part3(W, i) for W in (W3_hi, W3_whole, W3_lo))
                gp.tensor_tensor(lo, whole, hi.bitcast(F32), ALU.subtract).then_inc(w_low.sem, 1)

            def hidden_low(e):
                pool.wait_ge(*h_high.at(3, e + 1))
                gp.tensor_tensor(h_lo[:, e % HBUFS, :], h_whole[:, e % HBUFS, :], h_hi[:, e % HBUFS, :].bitcast(F32),
                                 ALU.subtract).then_inc(h_low.sem, 1)

            def wo_low_part(l, c):
                hi, whole, lo = attention_weight_piece(2 * c + 1)
                pool.wait_ge(*att_high.at(l, 2 * c + 2))
                gp.tensor_tensor(lo, whole, hi.bitcast(F32), ALU.subtract).then_inc(wo_low.sem, 1)

            def set_pads(l):
                pool.wait_ge(*(B.filled(("up", l, 1, HIDDEN_CHUNKS[l] - 1)) if GQA[l] else B.emptied(last_out[l])))
                for i in range(2):
                    gp.memset(A[l].qstack[i][:, :, STACK:64].bitcast(F32), 0.0).then_inc(pads.sem, 1)
                    gp.memset(A[l].kstack[i][:, :, 0:4:3, STACK:STACK + 1].bitcast(F32), 1.0).then_inc(pads.sem, 1)
                    gp.memset(A[l].kstack[i][:, :, 0:4:3, STACK + 1:64].bitcast(F32), 0.0).then_inc(pads.sem, 1)
                    gp.memset(A[l].kstack[i][:, :, 1:3, :].bitcast(F32), 0.0).then_inc(pads.sem, 1)
                if l > 1:
                    return
                for i in range(4):
                    gp.memset(A[l].V[i][:, :, :, HD:HD + 1], 1.0).then_inc(pads.sem, 1)
                    gp.memset(A[l].V[i][:, :, :, HD + 1:CELL], 0.0).then_inc(pads.sem, 1)
                    gp.memset(A[l].Vflat[i][:, 2 * A[l].vh * CELL:], 0.0).then_inc(pads.sem, 1)
                    if GQA[l]:
                        gp.memset(A[l].V[i][:, :, 4, 0:HD], 0.0).then_inc(pads.sem, 1)

            def stack_low(l, u, tau):
                i = 2 * u + tau
                pool.wait_ge(*stack_hi.at(l, HI * (i + 1)))
                src = A[l].qkr[i % 2] if ROPE[l] else A[l].qk[i % 2]
                qs, ks = A[l].qstack[i % 2], A[l].kstack[i % 2]
                gp.tensor_tensor(qs[:, :, 16:32], src[:, 0:UH, :], qs[:].bitcast(F32)[:, :, 0:16],
                                 ALU.subtract).then_inc(stack_lo.sem, 1)
                n = 4 if GQA[l] else 8
                if GQA[l]:
                    kv = src[:, UH:UH + 4, :].unsqueeze(2).to_broadcast([P, 4, 2, HD])
                else:
                    kv = src[:, UH:2 * UH, :].rearrange("p (n c) d -> p n c d", c=2)
                gp.tensor_tensor(ks[:, 0:n, 0:4:3, 32:48], kv, ks[:].bitcast(F32)[:, 0:n, 0:4:3, 0:16],
                                 ALU.subtract).then_inc(stack_lo.sem, 1)

            def cut_future(l, u, g):
                gi = GROUPS * u + g
                for kb in range(2):
                    pool.wait_ge(*B.emptied(("ST", l, u, g, kb, 1)))
                    blk = A[l].probs[gi % 2][:, kb, :, kb * P:(kb + 1) * P]
                    gp.affine_select(out=blk, in_=blk, compare_op=ALU.is_ge, fill=0.0, base=0,
                                     pattern=[[0, 4], [1, P]], channel_multiplier=-1).then_inc(causal_cut.sem, 1)

            pool.wait_ge(*ones_set.at(0, 3))
            for b in range(SEQS):
                inverse_deviation(0, b)
            for m in range(2):
                gp.memset(W0[m][:, :, HID0:].bitcast(F32), 0.0).then_inc(padding_set.sem, 1)
            for l in range(LAYERS):
                if l > 0:
                    inverse_deviation(l, SEQS - 1)
                if l >= 2:
                    for i in range(2, 2 * HC2 if l == 2 else 4):
                        weights_low(l, i)
                if l == 3:
                    for e in range(2 * HC3):
                        hidden_low(e)
                        if e in (1, 3):
                            weights_low(3, 4 + e // 2)
                set_pads(l)
                for tau in range(2):
                    stack_low(l, 0, tau)
                if GQA[l]:
                    for c in range(KC):
                        wo_low_part(l, c)
                for tau in range(2):
                    stack_low(l, 1, tau)
                for u in range(UNITS):
                    for g in range(GROUPS):
                        if CAUSAL[l]:
                            cut_future(l, u, g)
                        if l + 1 < LAYERS and u == UNITS - 1 and g < 2:
                            for b in ((0, 1), (2,))[g]:
                                inverse_deviation(l + 1, b)
                        if g < 2 and u + 2 < UNITS:
                            stack_low(l, u + 2, g)
                if l + 1 in (2, 3):
                    weights_low(l + 1, 0)
                    weights_low(l + 1, 1)

        @block.sync
        def _(sp):
            xv = a["x"].rearrange("(t p) d -> p t d", p=P)

            def load(dst, src, s):
                sp.dma_start(dst, src).then_inc(s, 16)

            load(ident[:], a["ident"], ident_in)
            for b in range(SEQS):
                load(x[:, 2 * b:2 * b + 2, :], xv[:, 2 * b:2 * b + 2, :], x_in[b])
            load(compact0[0][:], a["Wg0"], ffn_in[0])
            load(compact0[1][:], a["Wu0"], ffn_in[1])
            load(sign_in[:], a["sign_in"], signs_in)
            load(sign_hid[:], a["sign_hid"], signs_in)
            load(W0_whole[2][:], a["Wd0"], ffn_in[2])
            n = 0
            for dst, name in [(maskf, "mask")] + [(cosT[l], f"cos{l}") for l in (0, 2, 3)] + \
                    [(sinT[l], f"sin{l}") for l in (0, 2, 3)]:
                load(dst[:], a[name], const_in)
                n += 1
            assert n == CONSTS

            def load_chunk(e):
                if e >= W2BUFS:
                    sp.wait_ge(*chunk_used(2, e - W2BUFS))
                load(W2_whole[e % W2BUFS][:], a["w123"][:, e % HC2], w2_in[e % W2BUFS])

            def load_early(l):
                if l > 0:
                    sp.wait_ge(*B.filled(("ST", l - 1, UNITS - 2, GROUPS - 1, 1, 1)))
                if l == 1:
                    for dst, name in [(W1q, "qweight"), (zq, "qzeros"), (sh, "scales"), (gidx, "g_idx"), (four, "four"),
                                      (bias1, "bias1")]:
                        load(dst[:], a[name], ffn_in[0])
                if l == 2:
                    load(s2[:], a["w123s"], scales2_in)
                    load_chunk(0)
                    load_chunk(1)
                if l == 3:
                    for dst, name in [(W3_whole[n], n) for n in shapes3] + [(b1, "b1"), (b2, "b2")]:
                        load(dst[:], a[name], ffn_in[0])
                load(Wqkv_whole[:] if GQA[l] else Wqkv1[:], a[f"Wqkv{l}"], att_in)

            def load_late(l):
                if l > 0:
                    sp.wait_ge(*x_done.at(l - 1, TILES))
                if l == 2:
                    load_chunk(2)
                    load_chunk(3)
                load(Wo_whole[:], a[f"Wo{l}"], att_in)
                if l == 2:
                    for e in range(W2BUFS, 2 * HC2):
                        load_chunk(e)

            load_early(0)
            for l in range(LAYERS):
                load_late(l)
                for u in range(UNITS):
                    sp.wait_ge(*B.emptied(("mT", l, u)))
                    for par in range(2):
                        r = 64 * par + STACK
                        load(A[l].qT[u % 2][r:r + 1, :, :].bitcast(F32), A[l].negmaxT[u % 2][8 * par:8 * par + 8, :].bitcast(F32), m_rows[u % 2])
                if l + 1 < LAYERS:
                    load_early(l + 1)
            ov = out.rearrange("(t p) d -> p t d", p=P)
            for t in range(TILES):
                sp.wait_ge(*x_done.at(LAYERS - 1, t + 1))
                sp.dma_start(ov[:, t:t + 1, :], x[:, t:t + 1, :]).then_inc(out_done, 16)
            sp.wait_ge(out_done, 16 * TILES)


CONSTS = 7
LOADS = {1: 6, 3: 6}


def layouts(inputs):
    g = {k: np.asarray(v) for k, v in inputs.items()}
    o = {"x": g["L0_attn_hidden_states"].reshape(SEQS * SEQ, D)}
    eye = np.eye(P, dtype=np.float32)
    o["ident"] = eye
    future = np.where(np.arange(P)[None, :] > np.arange(P)[:, None], np.float32(NEG), np.float32(0))
    o["mask"] = np.concatenate([future, future], axis=1)
    which, sign = octonion_table()
    i_of = np.arange(D) // 64
    o["sign_in"] = np.ascontiguousarray(sign[i_of].reshape(KC, P, OCT).transpose(1, 0, 2))
    hid = np.minimum(np.arange(HC0 * P) // 170, 7)
    o["sign_hid"] = np.ascontiguousarray(sign[hid].reshape(HC0, P, OCT).transpose(1, 0, 2))
    for l in (0, 2, 3):
        inv = (1.0 / np.float32(ROPE_BASE[l]) ** (np.arange(0, HD, 2, dtype=np.float32) / HD)).astype(np.float32)
        ang = (np.arange(SEQ, dtype=np.float32)[:, None] * inv[None, :]).astype(np.float32)
        c, s = np.cos(ang), np.sin(ang)
        o[f"cos{l}"] = np.ascontiguousarray(np.concatenate([c, c], 1).reshape(2, P, HD).transpose(1, 0, 2)).astype(np.float32)
        o[f"sin{l}"] = np.ascontiguousarray(np.concatenate([-s, s], 1).reshape(2, P, HD).transpose(1, 0, 2)).astype(np.float32)

    shift_order = np.arange(D).reshape(64, 8).T.reshape(-1)
    halves = np.concatenate([np.arange(0, HD, 2), np.arange(1, HD, 2)])
    for l in range(LAYERS):
        wq, wk, wv, wo = (g[f"L{l}_attn_{n}"] for n in ("Wq", "Wk", "Wv", "Wo"))
        if l < 2:
            wq, wk, wv, wo = wq.T, wk.T, wv.T, wo.T
        if l == 1:
            wq, wk, wv = wq[shift_order], wk[shift_order], wv[shift_order]
        q = wq.reshape(D, 2, UH, HD)
        k = wk.reshape(D, 2, -1, HD)
        if l == 0:
            q, k = q[..., halves], k[..., halves]
        v = wv.reshape(D, 2, -1, HD)
        w = np.concatenate([y.reshape(D, 2, -1) for y in (q, k, v)], axis=2)
        o[f"Wqkv{l}"] = np.ascontiguousarray(w.reshape(KC, P, 2, -1).transpose(1, 0, 2, 3))
        o[f"Wo{l}"] = np.ascontiguousarray(wo.reshape(KC, P, D).transpose(1, 0, 2))

    assert (which == np.arange(OCT)[:, None] ^ np.arange(OCT)[None, :]).all()
    for name, key in (("Wg0", "w_gate"), ("Wu0", "w_up")):
        w = g[f"L0_ffn_{key}"].transpose(2, 0, 1)
        o[name] = np.ascontiguousarray(np.concatenate([w, w[:, np.arange(OCT) ^ 1]]))
    w = g["L0_ffn_w_down"][which].transpose(0, 3, 1, 2).reshape(HID0, D)
    pad = np.zeros((HC0 * P, D), np.float32)
    pad[:HID0] = w
    o["Wd0"] = np.ascontiguousarray(pad.reshape(HC0, P, D).transpose(1, 0, 2))

    qw = g["L1_ffn_qweight"]
    o["qweight"] = np.concatenate([qw, qw])
    o["qzeros"] = np.ascontiguousarray(g["L1_ffn_qzeros"])
    o["scales"] = np.ascontiguousarray(g["L1_ffn_scales"])
    o["g_idx"] = np.ascontiguousarray(np.repeat(g["L1_ffn_g_idx"][shift_order][None], 4, axis=0))
    o["four"] = np.arange(4, dtype=np.float32).reshape(4, 1)
    o["bias1"] = g["L1_ffn_bias"].reshape(1, D)

    blocks, scales = [], []
    for name in ("w1", "w3"):
        w = g[f"L2_ffn_{name}"]
        blocks.append(w.reshape(HC2, P, KC, P).transpose(3, 0, 2, 1))
        scales.append(g[f"L2_ffn_{name}_scale"])
    w = g["L2_ffn_w2"]
    blocks.append(w.T.reshape(HC2, P, KC, P).transpose(1, 0, 2, 3))
    scales.append(g["L2_ffn_w2_scale"].T)
    o["w123"] = np.ascontiguousarray(np.concatenate(blocks, axis=2))
    o["w123s"] = np.ascontiguousarray(np.repeat(np.concatenate(scales, axis=1)[None], P, axis=0))

    o["U1"] = np.ascontiguousarray(g["L3_ffn_U1"].reshape(KC, P, P).transpose(1, 0, 2))
    v1 = np.zeros((P, 2, HC3 * P), np.float32)
    v1[:, :, :INTER3] = g["L3_ffn_V1"].reshape(P, 2, INTER3)
    o["V1"] = v1.reshape(P, 2, HC3, P)
    u2 = np.zeros((HC3 * P, P), np.float32)
    u2[:INTER3] = g["L3_ffn_U2"]
    o["U2"] = np.ascontiguousarray(u2.reshape(HC3, P, P).transpose(1, 0, 2))
    o["V2"] = g["L3_ffn_V2"]
    bb = np.zeros((2, HC3 * P), np.float32)
    bb[:, :INTER3] = g["L3_ffn_b1"].reshape(2, INTER3)
    o["b1"] = np.ascontiguousarray(bb.reshape(2, HC3, P).transpose(2, 0, 1))
    o["b2"] = np.ascontiguousarray(np.repeat(g["L3_ffn_b2"][None], P, axis=0))
    return o


def kernel(**inputs):
    import concourse.bacc as _bacc
    from concourse import mybir as _mybir
    from concourse.bass_utils import run_bass_kernel_spmd as _run

    nc = _bacc.Bacc("TRN2", target_bir_lowering=False, num_devices=1)
    arrays, aps = {}, {}
    for name, arr in layouts(inputs).items():
        arrays[f"in_{name}"] = arr
        aps[name] = nc.dram_tensor(f"in_{name}", arr.shape, _mybir.dt.from_np(arr.dtype), kind="ExternalInput").ap()
    out = nc.dram_tensor("out_0", (SEQS, SEQ, D), _mybir.dt.float32, kind="ExternalOutput").ap()
    program(nc, aps, out.rearrange("b s d -> (b s) d"))
    r = _run(nc, [arrays], core_ids=[0])
    return r.results[0]["out_0"]
```
